# Optimizing a Trainium2 kernel written in Bass

```python
import numpy as np
import jax
import jax.numpy as jnp

def _softmax(x, axis=-1):
    return jax.nn.softmax(x, axis=axis)

def _gelu(x):
    return jax.nn.gelu(x, approximate=True)

def _silu(x):
    return jax.nn.silu(x)

def _sigmoid(x):
    return jax.nn.sigmoid(x)

def _layernorm(x, axis=-1, eps=1e-05):
    m = jnp.mean(x, axis=axis, keepdims=True)
    v = jnp.var(x, axis=axis, keepdims=True)
    return (x - m) / jnp.sqrt(v + eps)

def _scatter_add(tgt, idx, src, axis=0):
    return tgt.at[idx].add(src)

def _segment_sum(src, seg, n):
    return jax.ops.segment_sum(src, seg, n)
kernel_name = 'mk_xattn_ffn_d2_seqx_r8_530841'

def setup_inputs(seed: int=0):
    np.random.seed(seed)
    _w = jnp.asarray

    def _rec_inputs():
        import jax
        import jax.numpy as jnp
        _rk = jax.random.key(seed)
        x = -0.0003929 + 0.9999 * jax.random.normal(jax.random.fold_in(_rk, 1), (8, 256, 256), jnp.float32)
        _lenS = 256 - jax.random.randint(jax.random.fold_in(_rk, 7), (8,), 0, max(1, 256 // 4) + 1, jnp.int32)
        _lenS2 = 64 - jax.random.randint(jax.random.fold_in(_rk, 8), (8,), 0, max(1, 64 // 4) + 1, jnp.int32)
        _ctx_2048P = jax.random.normal(jax.random.fold_in(_rk, 11), (8, 16, 256), jnp.float32)
        _ctx_2048c = jax.random.dirichlet(jax.random.fold_in(_rk, 511), 0.3 * jnp.ones((16,), jnp.float32), (8, 64))
        _ctx_2048t = jnp.einsum('bsk,bkd->bsd', _ctx_2048c, _ctx_2048P)
        _ctx_2048t = _ctx_2048t * jax.lax.rsqrt(jnp.mean(jnp.square(_ctx_2048t)) + 1e-12) * 0.953939
        ctx_2048 = -0.000514642 + 1.00011 * (_ctx_2048t + 0.3 * jax.random.normal(jax.random.fold_in(_rk, 611), (8, 64, 256), jnp.float32))
        _validS = jnp.arange(256)[None, :] < _lenS[:, None]
        _validS2 = jnp.arange(64)[None, :] < _lenS2[:, None]
        _causal = jnp.tril(jnp.ones((256, 256), dtype=bool))
        mask_BxS2_ik0 = jnp.where(jnp.broadcast_to(_validS2[:, :], (8, 64)), 0, 1).astype(jnp.int32)
        mask_BxS2_bf1 = jnp.ones((8, 64), dtype=bool)
        return (x, ctx_2048, mask_BxS2_ik0, mask_BxS2_bf1)
    x, ctx_2048, mask_BxS2_ik0, mask_BxS2_bf1 = _rec_inputs()

    def _L0_xattn_setup():
        import jax, jax.numpy as jnp
        import numpy as np
        import math
        H = 256
        NH = 16
        HD = H // NH
        EPS_LN = 1e-05
        RES_SCALE_MAX = 0.3

        def _nan_clean(x, lim=10000.0):
            return jnp.nan_to_num(x, nan=0.0, posinf=lim, neginf=-lim)
        key = jax.random.key(seed)
        ks = jax.random.split(key, 12)
        B, S, T = (4, 256, 32)
        std = 1.0 / math.sqrt(H)
        return {'hidden_states': jax.random.normal(ks[0], (B, S, H), jnp.float32), 'audio_tokens': jax.random.normal(ks[1], (B, T, H), jnp.float32), 'attention_mask': jax.random.randint(ks[2], (B, T), 0, 2, jnp.int32), 'Wq': jax.random.normal(ks[3], (H, H), jnp.float32) * std, 'bq': jnp.zeros((H,), jnp.float32), 'Wk': jax.random.normal(ks[4], (H, H), jnp.float32) * std, 'bk': jnp.zeros((H,), jnp.float32), 'Wv': jax.random.normal(ks[5], (H, H), jnp.float32) * std, 'bv': jnp.zeros((H,), jnp.float32), 'Wo': jax.random.normal(ks[6], (H, H), jnp.float32) * std, 'bo': jnp.zeros((H,), jnp.float32), 'ln_gamma': jnp.ones((H,), jnp.float32), 'ln_beta': jnp.zeros((H,), jnp.float32), 'residual_scale': jnp.float32(0.05)}
    _L0_xattn_all = _L0_xattn_setup()
    _L0_xattn_in = {k: v for k, v in _L0_xattn_all.items() if k in ('Wq', 'bq', 'Wk', 'bk', 'Wv', 'bv', 'Wo', 'bo', 'ln_gamma', 'ln_beta', 'residual_scale')}
    del _L0_xattn_all

    def _L0_ffn_setup():
        import jax, jax.numpy as jnp
        import numpy as np
        NUM_EXPERTS = 128
        NUM_KEPT = 48
        TOP_K = 8
        HIDDEN = 256
        INTER = 96
        CAP = 96
        BATCH, SEQ = (2, 128)
        key = jax.random.key(seed)
        k1, k2, k3, k4 = jax.random.split(key, 4)
        hidden_states = jax.random.normal(k1, (BATCH, SEQ, HIDDEN), jnp.float32)
        gate_weight = jax.random.normal(k2, (NUM_EXPERTS, HIDDEN), jnp.float32) * 0.02
        gate_up_proj = jax.random.normal(k3, (NUM_KEPT, 2 * INTER, HIDDEN), jnp.float32) * 0.02
        down_proj = jax.random.normal(k4, (NUM_KEPT, HIDDEN, INTER), jnp.float32) * 0.02
        o2n = -np.ones(NUM_EXPERTS, np.int32)
        o2n[np.arange(NUM_KEPT) * 2] = np.arange(NUM_KEPT, dtype=np.int32)
        old_to_new = jnp.asarray(o2n)
        return {'hidden_states': hidden_states, 'gate_weight': gate_weight, 'gate_up_proj': gate_up_proj, 'down_proj': down_proj, 'old_to_new': old_to_new}
    _L0_ffn_all = _L0_ffn_setup()
    _L0_ffn_in = {k: v for k, v in _L0_ffn_all.items() if k in ('gate_weight', 'gate_up_proj', 'down_proj', 'old_to_new')}
    del _L0_ffn_all

    def _L1_xattn_setup():
        import jax, jax.numpy as jnp
        import numpy as np
        import math
        D_MODEL = 256
        N_Q_HEADS = 16
        N_KV_HEADS = 4
        HEAD_DIM = D_MODEL // N_Q_HEADS
        B = 4
        S = 128

        def _alibi_slopes(num_heads):
            n = 2 ** int(math.floor(math.log2(num_heads)))
            m0 = 2.0 ** (-8.0 / n)
            return m0 ** jnp.arange(1, n + 1, dtype=jnp.float32)
        key = jax.random.key(seed)
        ks = jax.random.split(key, 8)
        xavier = lambda k, fi, fo: jax.random.normal(k, (fi, fo), jnp.float32) * math.sqrt(2.0 / (fi + fo))
        return {'query': jax.random.normal(ks[0], (B, S, D_MODEL), jnp.float32), 'key': jax.random.normal(ks[1], (B, S, D_MODEL), jnp.float32), 'value': jax.random.normal(ks[2], (B, S, D_MODEL), jnp.float32), 'mask': jnp.ones((B, S), dtype=bool), 'Wq': xavier(ks[3], D_MODEL, N_Q_HEADS * HEAD_DIM), 'Wk': xavier(ks[4], D_MODEL, N_KV_HEADS * HEAD_DIM), 'Wv': xavier(ks[5], D_MODEL, N_KV_HEADS * HEAD_DIM), 'Wo': xavier(ks[6], D_MODEL, D_MODEL)}
    _L1_xattn_all = _L1_xattn_setup()
    _L1_xattn_in = {k: v for k, v in _L1_xattn_all.items() if k in ('Wq', 'Wk', 'Wv', 'Wo')}
    del _L1_xattn_all

    def _L1_ffn_setup():
        import jax, jax.numpy as jnp
        import numpy as np
        NUM_EXPERTS = 8
        TOP_K = 2
        MODEL_DIM = 256
        INTER_DIM = 128
        GATE_SCALE = 1.0
        UP_SCALE = 0.0
        key = jax.random.key(seed)
        k1, k2, k3, k4 = jax.random.split(key, 4)
        hidden_states = jax.random.normal(k1, (2, 256, MODEL_DIM), jnp.float32)
        router_gate = jax.random.normal(k2, (NUM_EXPERTS, MODEL_DIM), jnp.float32) * 0.02
        expert_gate_up = jax.random.normal(k3, (NUM_EXPERTS, MODEL_DIM, 2 * INTER_DIM), jnp.float32) * 0.02
        expert_down = jax.random.normal(k4, (NUM_EXPERTS, INTER_DIM, MODEL_DIM), jnp.float32) * 0.02
        return {'hidden_states': hidden_states, 'router_gate': router_gate, 'expert_gate_up': expert_gate_up, 'expert_down': expert_down}
    _L1_ffn_all = _L1_ffn_setup()
    _L1_ffn_in = {k: v for k, v in _L1_ffn_all.items() if k in ('router_gate', 'expert_gate_up', 'expert_down')}
    del _L1_ffn_all
    return {'x': x, 'ctx_2048': ctx_2048, 'mask_BxS2_ik0': mask_BxS2_ik0, 'mask_BxS2_bf1': mask_BxS2_bf1, 'L0_xattn_Wq': _L0_xattn_in['Wq'], 'L0_xattn_bq': _L0_xattn_in['bq'], 'L0_xattn_Wk': _L0_xattn_in['Wk'], 'L0_xattn_bk': _L0_xattn_in['bk'], 'L0_xattn_Wv': _L0_xattn_in['Wv'], 'L0_xattn_bv': _L0_xattn_in['bv'], 'L0_xattn_Wo': _L0_xattn_in['Wo'], 'L0_xattn_bo': _L0_xattn_in['bo'], 'L0_xattn_ln_gamma': _L0_xattn_in['ln_gamma'], 'L0_xattn_ln_beta': _L0_xattn_in['ln_beta'], 'L0_xattn_residual_scale': _L0_xattn_in['residual_scale'], 'L0_ffn_gate_weight': _L0_ffn_in['gate_weight'], 'L0_ffn_gate_up_proj': _L0_ffn_in['gate_up_proj'], 'L0_ffn_down_proj': _L0_ffn_in['down_proj'], 'L0_ffn_old_to_new': _L0_ffn_in['old_to_new'], 'L1_xattn_Wq': _L1_xattn_in['Wq'], 'L1_xattn_Wk': _L1_xattn_in['Wk'], 'L1_xattn_Wv': _L1_xattn_in['Wv'], 'L1_xattn_Wo': _L1_xattn_in['Wo'], 'L1_ffn_router_gate': _L1_ffn_in['router_gate'], 'L1_ffn_expert_gate_up': _L1_ffn_in['expert_gate_up'], 'L1_ffn_expert_down': _L1_ffn_in['expert_down']}

def reference(x, ctx_2048, mask_BxS2_ik0, mask_BxS2_bf1, L0_xattn_Wq, L0_xattn_bq, L0_xattn_Wk, L0_xattn_bk, L0_xattn_Wv, L0_xattn_bv, L0_xattn_Wo, L0_xattn_bo, L0_xattn_ln_gamma, L0_xattn_ln_beta, L0_xattn_residual_scale, L0_ffn_gate_weight, L0_ffn_gate_up_proj, L0_ffn_down_proj, L0_ffn_old_to_new, L1_xattn_Wq, L1_xattn_Wk, L1_xattn_Wv, L1_xattn_Wo, L1_ffn_router_gate, L1_ffn_expert_gate_up, L1_ffn_expert_down):
    import jax
    import jax.numpy as jnp

    def _L0_xattn_ref(hidden_states, audio_tokens, attention_mask, Wq, bq, Wk, bk, Wv, bv, Wo, bo, ln_gamma, ln_beta, residual_scale):
        import jax, jax.numpy as jnp
        import numpy as np
        import math
        H = 256
        NH = 16
        HD = H // NH
        EPS_LN = 1e-05
        RES_SCALE_MAX = 0.3

        def _nan_clean(x, lim=10000.0):
            return jnp.nan_to_num(x, nan=0.0, posinf=lim, neginf=-lim)
        B, S, _ = hidden_states.shape
        T = audio_tokens.shape[1]
        hs = _nan_clean(hidden_states).astype(jnp.float32)
        at = _nan_clean(audio_tokens).astype(jnp.float32)

        def proj(x, W, b, L):
            y = x @ W.T + b
            return y.reshape(B, L, NH, HD).transpose(0, 2, 1, 3)
        q = _nan_clean(proj(hs, Wq, bq, S))
        k = _nan_clean(proj(at, Wk, bk, T))
        v = _nan_clean(proj(at, Wv, bv, T))
        scale = max(math.sqrt(HD), 1e-08)
        scores = jnp.einsum('bhsd,bhtd->bhst', q, k) / scale
        scores = jnp.clip(scores, -50.0, 50.0)
        scores = jnp.nan_to_num(scores, nan=0.0, posinf=50.0, neginf=-50.0)
        attend = (attention_mask.astype(jnp.float32) > 0.5)[:, None, None, :]
        scores = jnp.where(attend, scores, -10000.0)
        scores = jnp.clip(scores, -50.0, 50.0)
        probs = jax.nn.softmax(scores, axis=-1)
        probs = jnp.nan_to_num(probs, nan=0.0, posinf=1.0, neginf=0.0)
        probs = probs / (probs.sum(axis=-1, keepdims=True) + 1e-08)
        ctx = jnp.einsum('bhst,bhtd->bhsd', probs, v)
        ctx = ctx.transpose(0, 2, 1, 3).reshape(B, S, H)
        delta = _nan_clean(ctx @ Wo.T + bo)
        rs = jnp.clip(residual_scale, 0.0, RES_SCALE_MAX)
        delta = rs * delta
        mu = delta.mean(axis=-1, keepdims=True)
        var = jnp.mean((delta - mu) ** 2, axis=-1, keepdims=True)
        delta = (delta - mu) / jnp.sqrt(var + EPS_LN) * ln_gamma + ln_beta
        return delta

    def _L0_ffn_ref(hidden_states, gate_weight, gate_up_proj, down_proj, old_to_new):
        import jax, jax.numpy as jnp
        import numpy as np
        NUM_EXPERTS = 128
        NUM_KEPT = 48
        TOP_K = 8
        HIDDEN = 256
        INTER = 96
        CAP = 96
        BATCH, SEQ = (2, 128)
        B, S, H = hidden_states.shape
        x = hidden_states.reshape(-1, H)
        T = x.shape[0]
        logits = x @ gate_weight.T
        logits = jnp.where(old_to_new[None, :] == -1, -jnp.inf, logits)
        probs = jax.nn.softmax(logits.astype(jnp.float32), axis=-1).astype(logits.dtype)
        top_v, top_i = jax.lax.top_k(probs, TOP_K)
        top_v = top_v / jnp.sum(top_v, axis=-1, keepdims=True)
        sel_new = old_to_new[top_i]
        E = gate_up_proj.shape[0]
        flat_e = sel_new.reshape(-1)
        flat_w = top_v.reshape(-1)
        tok = jnp.repeat(jnp.arange(T), TOP_K)
        oh = (flat_e[:, None] == jnp.arange(E)[None, :]).astype(jnp.int32)
        pos = jnp.sum(jnp.cumsum(oh, axis=0) * oh, axis=-1) - 1
        valid = pos < CAP
        pos_c = jnp.where(valid, pos, CAP)
        xb = jnp.zeros((E, CAP + 1, H), x.dtype).at[flat_e, pos_c].set(x[tok])
        xb = xb[:, :CAP]
        gu = jnp.einsum('ech,eoh->eco', xb, gate_up_proj)
        g, u = jnp.split(gu, 2, axis=-1)
        h = jax.nn.silu(g) * u
        out = jnp.einsum('eci,ehi->ech', h, down_proj)
        y = out[flat_e, jnp.minimum(pos_c, CAP - 1)]
        w = flat_w * valid.astype(flat_w.dtype)
        final = jnp.zeros_like(x).at[tok].add(y * w[:, None])
        return final.reshape(B, S, H)

    def _L1_xattn_ref(query, key, value, mask, Wq, Wk, Wv, Wo):
        import jax, jax.numpy as jnp
        import numpy as np
        import math
        D_MODEL = 256
        N_Q_HEADS = 16
        N_KV_HEADS = 4
        HEAD_DIM = D_MODEL // N_Q_HEADS
        B = 4
        S = 128

        def _alibi_slopes(num_heads):
            n = 2 ** int(math.floor(math.log2(num_heads)))
            m0 = 2.0 ** (-8.0 / n)
            return m0 ** jnp.arange(1, n + 1, dtype=jnp.float32)
        b, q_len, d = query.shape
        kv_len = key.shape[1]
        G = N_KV_HEADS
        Hpg = N_Q_HEADS // G
        dh = HEAD_DIM
        Q = (query @ Wq).reshape(b, q_len, G, Hpg, dh)
        K = (key @ Wk).reshape(b, kv_len, G, dh)
        V = (value @ Wv).reshape(b, kv_len, G, dh)
        Q = Q / math.sqrt(dh)
        scores = jnp.einsum('bqghd,bkgd->bghqk', Q, K)
        rel = jnp.arange(kv_len, dtype=jnp.float32)[None, :] - jnp.arange(q_len, dtype=jnp.float32)[:, None]
        m = _alibi_slopes(N_Q_HEADS).reshape(1, G, Hpg, 1, 1)
        scores = scores + m * rel[None, None, None]
        neg = jnp.finfo(scores.dtype).min
        scores = jnp.where(mask[:, None, None, None, :], scores, neg)
        w = jax.nn.softmax(scores, axis=-1)
        out = jnp.einsum('bghqk,bkgd->bqghd', w, V)
        out = out.reshape(b, q_len, G * Hpg * dh)
        return out @ Wo

    def _L1_ffn_ref(hidden_states, router_gate, expert_gate_up, expert_down):
        import jax, jax.numpy as jnp
        import numpy as np
        NUM_EXPERTS = 8
        TOP_K = 2
        MODEL_DIM = 256
        INTER_DIM = 128
        GATE_SCALE = 1.0
        UP_SCALE = 0.0
        orig_shape = hidden_states.shape
        hs = hidden_states.reshape(-1, orig_shape[-1])
        T = hs.shape[0]
        logits = hs @ router_gate.T
        probs = jax.nn.softmax(logits.astype(jnp.float32), axis=-1)
        topk_scores, topk_idx = jax.lax.top_k(probs, TOP_K)
        topk_scores = topk_scores / jnp.sum(topk_scores, axis=-1, keepdims=True)
        scores_f = topk_scores.T.reshape(-1).astype(hs.dtype)
        ids_f = topk_idx.T.reshape(-1)
        order = jnp.argsort(ids_f)
        sorted_ids = ids_f[order]
        scores_sorted = scores_f[order]
        token_slots = order % T
        x = hs[token_slots]
        inter = jnp.zeros((x.shape[0], 2 * INTER_DIM), x.dtype)
        for e in range(NUM_EXPERTS):
            m = (sorted_ids == e)[:, None]
            inter = inter + jnp.where(m, x, 0) @ expert_gate_up[e]
        gate = inter[..., 0::2]
        up = inter[..., 1::2]
        h = (up + UP_SCALE) * jax.nn.silu(gate * GATE_SCALE)
        out_rows = jnp.zeros((x.shape[0], MODEL_DIM), x.dtype)
        for e in range(NUM_EXPERTS):
            m = (sorted_ids == e)[:, None]
            out_rows = out_rows + jnp.where(m, h, 0) @ expert_down[e]
        out = jnp.zeros_like(hs).at[token_slots].add(out_rows * scores_sorted[:, None])
        return out.reshape(orig_shape)
    x = x + _L0_xattn_ref(_layernorm(x, axis=-1), ctx_2048, mask_BxS2_ik0, L0_xattn_Wq, L0_xattn_bq, L0_xattn_Wk, L0_xattn_bk, L0_xattn_Wv, L0_xattn_bv, L0_xattn_Wo, L0_xattn_bo, L0_xattn_ln_gamma, L0_xattn_ln_beta, L0_xattn_residual_scale)
    x = x + _L0_ffn_ref(_layernorm(x, axis=-1), L0_ffn_gate_weight, L0_ffn_gate_up_proj, L0_ffn_down_proj, L0_ffn_old_to_new)
    x = x + _L1_xattn_ref(_layernorm(x, axis=-1), ctx_2048, ctx_2048, mask_BxS2_bf1, L1_xattn_Wq, L1_xattn_Wk, L1_xattn_Wv, L1_xattn_Wo)
    x = x + _L1_ffn_ref(_layernorm(x, axis=-1), L1_ffn_router_gate, L1_ffn_expert_gate_up, L1_ffn_expert_down)
    return x

_drawn_inputs = setup_inputs


def setup_inputs(seed=0):
    import zlib

    import numpy as np

    out = dict(_drawn_inputs(seed))
    spreads = {'L0_xattn_bq': (0.0, 0.291),
     'L0_xattn_bk': (0.0, 0.8),
     'L0_xattn_bv': (0.0, 0.1),
     'L0_xattn_bo': (0.0, 0.1),
     'L0_xattn_ln_gamma': (1.0, 0.2),
     'L0_xattn_ln_beta': (0.0, 0.1)}
    factors = {'L0_ffn_gate_weight': 8.0,
     'L0_ffn_gate_up_proj': 8.0,
     'L0_ffn_down_proj': 8.0,
     'L1_ffn_router_gate': 8.0,
     'L1_ffn_expert_gate_up': 8.0,
     'L1_ffn_expert_down': 8.0}
    for name, (base, spread) in spreads.items():
        noise = np.random.default_rng([zlib.crc32(name.encode()), seed]).standard_normal(out[name].shape)
        drawn = base * np.exp(spread * noise) if base else spread * noise
        out[name] = jnp.asarray(drawn.astype(out[name].dtype))
    for name, factor in factors.items():
        out[name] = (out[name] * factor).astype(out[name].dtype)
    return out
```

```python
from contextlib import ExitStack

import concourse.bass as bass
import numpy as np
from concourse import mybir

F32, BF16 = mybir.dt.float32, mybir.dt.bfloat16
I32, U32, U8 = mybir.dt.int32, mybir.dt.uint32, mybir.dt.uint8
ALU = mybir.AluOpType
ACT = mybir.ActivationFunctionType
AX = mybir.AxisListType

P = 128
BATCH, SEQ, D = 8, 256, 256
CTX = 64
HEADS, DH = 16, 16
TOKENS = BATCH * SEQ
KC = D // P
ST = SEQ // P
PAIRS = HEADS // 2
VW = DH + 1
GROUPS = 4
OLD, NEW, TOPK, CAP, INTER0 = 128, 48, 8, 96, 96
EPG = 4
QG = NEW // EPG
ROW = D + NEW
PADROWS = TOKENS + P
E1, INTER1 = 8, 128
EPS = 1e-5
MASKED = -1e30
TAKEN = -3e38

C_ID, C_TRI, C_E48 = 0, 128, 256
C_HEAD2, C_HEAD8, C_SLOTE, C_PAD, C_LOC, C_B256, C_E8 = 304, 306, 314, 330, 331, 333, 341
C_N = 349


def constants():
    c = np.zeros((P, C_N), np.float32)
    p = np.arange(P)
    c[:, C_ID:C_ID + P] = np.eye(P)
    c[:, C_TRI:C_TRI + P] = p[:, None] < p[None, :]
    c[:, C_E48:C_E48 + NEW] = np.arange(NEW)
    c[:, C_HEAD2:C_HEAD2 + 2] = (p[:, None] // DH) % 2 == np.arange(2)
    c[:, C_HEAD8:C_HEAD8 + 8] = p[:, None] // DH == np.arange(8)
    c[:, C_SLOTE:C_SLOTE + EPG * EPG] = np.eye(EPG).reshape(-1)
    c[:, C_PAD] = TOKENS + p
    c[:, C_LOC:C_LOC + ST] = p[:, None] + P * np.arange(ST)
    c[:, C_B256:C_B256 + BATCH] = SEQ * np.arange(BATCH)
    c[:, C_E8:C_E8 + E1] = np.arange(E1)
    return c


def thirds(a):
    bf = mybir.dt.np(BF16)
    out = []
    for _ in range(3):
        out.append(a.astype(bf))
        a = a - out[-1].astype(np.float32)
    return out


def position_bias():
    slope = (np.float32(2.0 ** (-8.0 / HEADS)) ** np.arange(1, HEADS + 1, dtype=np.float32)).astype(np.float32)
    key = slope[:, None] * np.arange(CTX, dtype=np.float32)
    query = np.repeat(-slope[:, None], CTX, 1)
    rows = np.stack(thirds(key) + thirds(query)).reshape(6, HEADS * CTX)
    left = np.ones((7, SEQ), rows.dtype)
    left[4:] = np.arange(SEQ)
    return left, rows


def at_least(eng, sem, value):
    if not isinstance(value, int) or value > 0:
        eng.wait_ge(sem, value)


def build(nc, t, out, dbg=None):
    with ExitStack() as ctx:
        def sb(name, shape, dt=F32):
            return ctx.enter_context(nc.sbuf_tensor(name, shape, dt))

        def sem(name):
            return ctx.enter_context(nc.semaphore(name))

        def hold(eng, s, value):
            if isinstance(value, int):
                if value > 0:
                    eng.wait_ge(s, value)
            else:
                eng.wait_ge(s, value)
                eng.sem_inc(held, 1)

        held = sem("held")
        rows_d = nc.dram_tensor("rows_scratch", (PADROWS, ROW), F32, kind="Internal").ap()
        sums_d = [nc.dram_tensor(f"sum{k}_scratch", (PADROWS, D), F32, kind="Internal").ap() for k in range(2)]
        share_d = nc.dram_tensor("share_scratch", (BATCH, E1, SEQ), F32, kind="Internal").ap()
        out_v = out.rearrange("(b j p) d -> b p j d", j=ST, p=P)
        x_v = t["x"].rearrange("(b j p) d -> b p j d", j=ST, p=P)
        rows_v = rows_d[0:TOKENS, :].rearrange("(b j p) d -> b p j d", j=ST, p=P)
        sums_v = [s[0:TOKENS, :].rearrange("(b j p) d -> b p j d", j=ST, p=P) for s in sums_d]

        x_all = sb("x_all", [P, BATCH * ST, D])
        cst = sb("cst", [P, C_N])
        ident = cst[:, C_ID:C_ID + P]
        half = sb("half", [P, ST])
        cT = sb("cT", [P, KC, BATCH * CTX])
        NV, NK, NW = BATCH * PAIRS * 2 * VW, KC * BATCH * CTX, KC * D
        early = sb("early", [P, NV + NK + 2 * NW])
        v_blk = [early[:, 0:NV].rearrange("p (b r a v) -> p b r a v", b=BATCH, r=PAIRS, a=2),
                 sb("v_blk1", [P, BATCH, PAIRS, 2, VW])[:]]
        kT = [early[:, NV:NV + NK].rearrange("p (k c) -> p k c", k=KC), sb("kT1", [P, KC, BATCH * CTX])[:]]
        wk0, wv0 = (early[:, NV + NK + n * NW:NV + NK + n * NW + NW].rearrange("p (k d) -> p k d", k=KC)
                    for n in range(2))
        wq0, wo0 = (sb(n, [P, KC, D]) for n in ("wq0", "wo0"))
        wq1, wo1, wk1 = (sb(n, [P, KC, D]) for n in ("wq1", "wo1", "wk1"))
        wk1n, wv1 = (sb(n, [P, KC, GROUPS * DH]) for n in ("wk1n", "wv1"))
        gate0 = sb("gate0", [P, KC, OLD])
        bq0, bk0 = sb("bq0", [P, KC]), sb("bk0", [P, KC])
        bv0, bo0, gamma, beta = (sb(n, [P, D]) for n in ("bv0", "bo0", "gamma", "beta"))
        cdup = sb("cdup", [P, KC, BATCH, 2, CTX])
        mask_i = sb("mask_i", [P, BATCH], I32)
        hi = sb("hi", [P, BATCH])
        lo = sb("lo", [P, 1])
        rs = sb("rs", [P, 1])
        rs2 = sb("rs2", [P, 1])
        o2n_c, o2n_r = sb("o2n_c", [P, 1], I32), sb("o2n_r", [P, OLD], I32)
        o2n_f = sb("o2n_f", [P, 1])
        unkept = sb("unkept", [P, OLD])
        map_f, map_b = sb("map_f", [P, NEW]), sb("map_b", [P, NEW], BF16)
        tri, ones_b, ident_b = (sb(n, [P, P], BF16) for n in ("tri", "ones_b", "ident_b"))
        place = sb("place", [P, QG, CAP, EPG], BF16)
        loc1 = sb("loc1", [P, ST, 2], BF16)
        stat6 = sb("stat6", [P, ST, 6])
        mv_a, mv_d, mv_h = (sb(n, [P, ST, 2]) for n in ("mv_a", "mv_d", "mv_h"))
        rstd_a, rstd_d, rstd_h = (sb(n, [P, ST]) for n in ("rstd_a", "rstd_d", "rstd_h"))
        ve_a, ve_d, ve_h = (sb(n, [P, ST]) for n in ("ve_a", "ve_d", "ve_h"))
        hs = sb("hs", [P, ST, D])
        hsT = sb("hsT", [P, KC, SEQ])
        qT = sb("qT", [P, KC, SEQ])
        k_blk = sb("k_blk", [P, KC, 2, CTX])
        xbeta = sb("xbeta", [P, ST, D])
        prob = sb("prob", [P, 4, KC, SEQ])
        rden = sb("rden", [P, ST, PAIRS, 2])
        att = sb("att", [P, ST, D])
        attT = sb("attT", [P, KC, SEQ])
        delta = sb("delta", [P, ST, D])
        dgam = sb("dgam", [P, ST, D])
        h_rows = sb("h_rows", [P, ST, D])
        hT = sb("hT", [P, KC, SEQ])
        logit = sb("logit", [P, ST, OLD])
        top = sb("top", [P, ST, TOPK])
        ntop = sb("ntop", [P, ST])
        etop = sb("etop", [P, ST, TOPK])
        den = sb("den", [P, ST])
        rdn = sb("rdn", [P, ST])
        left = sb("left", [P, ST, OLD])
        sel = sb("sel", [P, ST, OLD], BF16)
        selsum = sb("selsum", [P, OLD], BF16)
        selboth = sb("selboth", [P, OLD], BF16)
        expl = sb("expl", [P, ST, OLD])
        wsel = sb("wsel", [P, ST, OLD])
        countT = sb("countT", [P, ST, P], BF16)
        wselT = sb("wselT", [P, ST, P])
        w_rows = sb("w_rows", [P, ST, NEW])
        off = sb("off", [P, ST, NEW])
        pos = sb("pos", [P, ST, NEW], BF16)
        hit = sb("hit", [P, ST, QG, CAP, EPG], BF16)
        slots = sb("slots", [CAP, NEW, 2])
        slot_b = sb("slot_b", [CAP, NEW])
        empty = sb("empty", [CAP, NEW])
        slot_f = sb("slot_f", [CAP, NEW])
        slot_i = sb("slot_i", [CAP, NEW], U32)
        zrow = sb("zrow", [P, ROW])
        take = [sb(f"take{h}", [CAP, EPG], U32) for h in range(2)]
        give = [sb(f"give{h}", [CAP, EPG], U32) for h in range(2)]
        xb = [sb(f"xb{h}", [CAP, EPG, ROW]) for h in range(2)]
        NG, ND = KC * EPG * 2 * INTER0, EPG * D
        late = sb("late", [P, max(2 * NG + 2 * ND, BATCH * ST * D + E1 * SEQ)])
        gu0 = [late[:, h * NG:h * NG + NG].rearrange("p (k e o) -> p k e o", k=KC, e=EPG) for h in range(2)]
        down0 = [late[0:INTER0, 2 * NG + h * ND:2 * NG + h * ND + ND].rearrange("p (e d) -> p e d", e=EPG)
                 for h in range(2)]
        y = [sb(f"y{h}", [CAP, EPG, D]) for h in range(2)]
        wpick = sb("wpick", [CAP, EPG, EPG])
        wslot = [sb(f"wslot{h}", [CAP, EPG]) for h in range(2)]
        xbT = sb("xbT", [P, KC, EPG * CAP])
        silu0 = sb("silu0", [INTER0, EPG, CAP])
        act0 = sb("act0", [INTER0, EPG, CAP])
        x_add = late[:, 0:BATCH * ST * D].rearrange("p (n d) -> p n d", d=D)
        share = late[:, BATCH * ST * D:BATCH * ST * D + E1 * SEQ].rearrange("p (e s) -> p e s", e=E1)
        gu1 = hit[:].rearrange("p j q c e -> p (j q c e)").bitcast(F32)[:, 0:E1 * KC * 2 * INTER1]\
            .rearrange("p (e k s i) -> p e k s i", e=E1, k=KC, s=2)
        down1 = place[:].rearrange("p q c e -> p (q c e)").bitcast(F32)[:, 0:E1 * D].rearrange("p (e d) -> p e d", e=E1)
        gate1 = sb("gate1", [P, KC, E1])
        bias_k = early[:, 0:BATCH * HEADS * CTX // 2].bitcast(BF16)[0:7].rearrange("p (b c) -> p b c", b=BATCH)
        bias_q = sb("bias_q", [7, SEQ], BF16)
        mask_u = sb("mask_u", [1, BATCH * CTX], U8)
        mask_b = sb("mask_b", [1, BATCH, 1, CTX], BF16)
        k1_blk = sb("k1_blk", [P, KC, 8, CTX])
        great = sb("great", [P, 4, 8])
        soft = prob[:].rearrange("p j m s -> p j (m s)")
        softT = cdup[:].rearrange("p k b a c -> p (k b a c)").rearrange("p (u c) -> p u c", u=4)
        hT1 = sb("hT1", [P, KC, SEQ])
        logit1 = sb("logit1", [P, ST, E1])
        top1, index1 = sb("top1", [P, ST, 8]), sb("index1", [P, ST, 8], U32)
        gap, egap, wsum = (sb(n, [P, ST]) for n in ("gap", "egap", "wsum"))
        wpair = sb("wpair", [P, 2, ST])
        chosen = sb("chosen", [P, 2, ST, E1])
        chosen_w = sb("chosen_w", [P, 2, ST, E1])
        share_c = sb("share_c", [P, ST, E1])
        shareT = sb("shareT", [E1, SEQ])
        silu1 = [sb(f"silu1_{h}", [P, SEQ]) for h in range(2)]
        act1 = [sb(f"act1_{h}", [P, SEQ]) for h in range(2)]
        act1w = [sb(f"act1w_{h}", [P, SEQ]) for h in range(2)]
        o_rows = delta

        banks = [ctx.enter_context(nc.psum_tensor(f"bank{k}", [P, 512], F32)) for k in range(8)]

        S = {}
        for n in ("ctx_in", "cst_in", "kv_w_in", "q_w_in", "bias_in", "route_in", "l1_w_in", "x_in", "zero_out",
                  "half_set", "wk1_set", "cdup_set", "vblk_zero", "vblk_ones", "hi_set", "bound_set", "rs_set",
                  "map_set", "tri_set", "place_set", "loc_set",
                  "kT_mm", "kT_set", "v_mm", "v_set",
                  "stat_a", "mv_a_set", "ve_a_set", "rstd_a_set", "hs_set", "hs_T", "hsT_set", "q_mm", "q_set",
                  "k_set", "xbeta_set",
                  "s_mm", "exp_set", "clip_set", "pv_mm", "rden_set", "att_set", "att_T", "attT_set", "o_mm",
                  "delta_set", "stat_d", "mv_d_set", "ve_d_set", "pow_d_set", "rstd_d_set", "dgam_set", "x1_set",
                  "stat_h", "mv_h_set", "ve_h_set", "rstd_h_set", "h_set", "x1_out", "h_out", "w_out",
                  "h_T", "hT_set", "l_mm", "logit_set", "top_set", "ntop_set", "left_set", "sel_set", "expl_set",
                  "etop_set", "den_set", "wsel_set", "count_mm", "wsel_T", "countT_set", "wselT_set", "pos_mm",
                  "w_set", "off_set", "pos_set", "hit_set", "slot_mm", "slot_acc", "slotb_acc", "selsum_set", "route_done",
                  "w0_ld0", "w0_ld1", "take_set", "give_set", "gather0", "gather1", "scatter0", "scatter1",
                  "xb_T", "xbT_set", "wpick_set", "wslot_set", "gu0_mm", "silu0_set", "act0_set", "y_mm", "yv_set", "ya_set",
                  "gate1_in", "bias_q_in", "bias1_in", "mask_u_in", "mask_b_set", "e1_w_in",
                  "sum_in0", "sum_in1", "x2_set", "k1_set",
                  "s1_mm", "great_set", "sub_set", "soft_set", "soft_T", "softT_set", "x3_set",
                  "h1_T", "hT1_set", "l1_mm", "logit1_set", "top1_set", "index1_set", "gap_set", "egap_set", "wsum_set",
                  "w0_set", "w1_set", "chosen_set", "chosen_w_set", "share_set", "share_T", "shareT_set",
                  "share_out", "share_in", "gu1_mm", "silu1_set", "act1_set", "act1w_set", "down1_mm", "o_set", "o_out"):
            S[n] = sem(n)
        block = ctx.enter_context(nc.Block())

        @block.sync
        def _(sp):
            sp.dma_start(cT[:], t["ctxT"]).then_inc(S["ctx_in"], 16)
            sp.dma_start(wk0[:], t["wk0"]).then_inc(S["kv_w_in"], 16)
            sp.dma_start(wv0[:], t["wv0"]).then_inc(S["kv_w_in"], 16)
            sp.dma_start(cst[:], t["cst"]).then_inc(S["cst_in"], 16)
            for n, v in ((wq0, "wq0"), (wo0, "wo0"), (gate0, "gate0")):
                sp.dma_start(n[:], t[v]).then_inc(S["q_w_in"], 16)
            with sp.Fori(0, BATCH) as b:
                sp.dma_start(x_all[:, bass.ds(ST * b, ST), :], x_v[b]).then_inc(S["x_in"], 16)
                sp.wait_ge(S["x_in"], 16 * b + 16)
                sp.sem_inc(held, 1)
            for n, v in ((wq1, "wq1"), (wk1n, "wk1"), (wv1, "wv1"), (wo1, "wo1")):
                sp.dma_start(n[:], t[v]).then_inc(S["l1_w_in"], 16)
            sp.wait_ge(S["place_set"], 2)
            sp.dma_start(rows_d[TOKENS:PADROWS, :], zrow[:]).then_inc(S["zero_out"], 16)
            for k in range(2):
                sp.dma_start(sums_d[k][TOKENS:PADROWS, :], zrow[:, 0:D]).then_inc(S["zero_out"], 16)
            for k in range(TOKENS // P):
                sp.dma_start(sums_d[1][P * k:P * k + P, :], zrow[:, 0:D]).then_inc(S["zero_out"], 16)

            def store_x1(b):
                at_least(sp, S["x1_set"], 2 * b + 2)
                sp.dma_start(sums_v[0][b], x_all[:, bass.ds(ST * b, ST), :]).then_inc(S["x1_out"], 16)
                at_least(sp, S["h_set"], 2 * b + 2)
                sp.dma_start(rows_v[b][:, :, 0:D], h_rows[:]).then_inc(S["h_out"], 16)

            def store_w(b):
                at_least(sp, S["w_set"], 2 * b + 2)
                sp.dma_start(rows_v[b][:, :, D:ROW], w_rows[:]).then_inc(S["w_out"], 16)


            def load_w0(i, h):
                q = 2 * i + h
                at_least(sp, S["gu0_mm"], 2 * (q - 1))
                sp.dma_start(gu0[h][:], t["gu0"][q]).then_inc(S[f"w0_ld{h}"], 16)
                at_least(sp, S["y_mm"], 2 * (q - 1))
                sp.dma_start(down0[h][:], t["down0"][q]).then_inc(S[f"w0_ld{h}"], 16)

            load_w0(0, 0)
            load_w0(0, 1)
            store_x1(0)
            with sp.Fori(0, BATCH - 1) as i:
                store_w(i)
                store_x1(i + 1)
            store_w(BATCH - 1)

            sp.wait_ge(S["route_done"], 1)
            sp.wait_ge(S["slot_mm"], BATCH)
            sp.wait_ge(S["pv_mm"], 2 * BATCH)
            sp.dma_start(gu1, t["gu1"]).then_inc(S["e1_w_in"], 16)
            sp.dma_start(down1, t["down1"]).then_inc(S["e1_w_in"], 16)
            for b in range(BATCH):
                sp.dma_start(bias_k[1:7, b, :], t["bias_k"]).then_inc(S["bias1_in"], 16)
            sp.wait_ge(S["mask_b_set"], 1)
            for b in range(BATCH):
                sp.dma_start(bias_k[0:1, b].rearrange("p (h c) -> p h c", c=CTX),
                             mask_b[:, b].broadcast_to([1, HEADS, CTX])).then_inc(S["bias1_in"], 16)
            with sp.Fori(1, QG // 2) as i:
                for h in range(2):
                    load_w0(i, h)

            sp.wait_ge(S["scatter0"], 16 * NEW // 2)
            sp.wait_ge(S["scatter1"], 16 * NEW // 2)
            sp.wait_ge(S["y_mm"], 2 * QG)

            def load_x(b):
                sp.dma_start(x_all[:, bass.ds(ST * b, ST), :], sums_v[0][b]).then_inc(S["sum_in0"], 16)
                sp.dma_start(x_add[:, bass.ds(ST * b, ST), :], sums_v[1][b]).then_inc(S["sum_in1"], 16)
                hold(sp, S["sum_in0"], 16 * b + 16)
                hold(sp, S["sum_in1"], 16 * b + 16)

            def share_bc(b):
                at_least(sp, S["shareT_set"], b + 1)
                sp.dma_start(share_d[b], shareT[:]).then_inc(S["share_out"], 16)
                hold(sp, S["share_out"], 16 * b + 16)
                hold(sp, S["act1w_set"], E1 * b)
                sp.dma_start(share, share_d[b].partition_broadcast(P)).then_inc(S["share_in"], 16)

            def store(b):
                at_least(sp, S["o_set"], b + 1)
                sp.dma_start(out_v[b], o_rows[:]).then_inc(S["o_out"], 16)

            with sp.Fori(0, BATCH) as b:
                load_x(b)
            share_bc(0)
            with sp.Fori(0, BATCH - 1) as b:
                store(b)
                share_bc(b + 1)
            store(BATCH - 1)
            sp.wait_ge(S["o_out"], 16 * BATCH)
            sp.wait_ge(S["share_out"], 16 * BATCH)
            if dbg is not None:
                sp.dma_start(dbg["slot"], slot_f[:]).then_inc(S["cst_in"], 16)
                sp.dma_start(dbg["rows"], rows_d).then_inc(S["cst_in"], 16)
                for k in range(2):
                    sp.dma_start(dbg["sum%d" % k], sums_d[k]).then_inc(S["cst_in"], 16)
                sp.wait_ge(S["cst_in"], 80)

        @block.gpsimd
        def _(pool):
            pool.memset(half[:], -0.5).then_inc(S["half_set"], 1)
            pool.memset(zrow[:], 0.0).then_inc(S["place_set"], 1)
            pool.memset(lo[:], float(np.exp(-50.0))).then_inc(S["half_set"], 1)
            pool.wait_ge(S["ctx_in"], 16)
            cv = cT[:].rearrange("p k (b c) -> p (k b) c", c=CTX)
            dv = cdup[:].rearrange("p k b a c -> p (k b) a c")
            for a in range(2):
                pool.tensor_copy(dv[:, :, a, :], cv).then_inc(S["cdup_set"], 1)
            for v in v_blk:
                pool.memset(v[:], 0.0).then_inc(S["vblk_zero"], 1)
            pool.iota(place[:], [[0, QG], [1, CAP], [0, EPG]], base=0, channel_multiplier=0,
                      allow_small_or_imprecise_dtypes=True).then_inc(S["place_set"], 1)
            pool.memset(slots[:], 0.0).then_inc(S["place_set"], 1)
            pool.memset(slot_b[:], 0.0).then_inc(S["place_set"], 1)
            pool.memset(selsum[:], 0.0).then_inc(S["place_set"], 1)
            pool.memset(ones_b[:], 1.0).then_inc(S["place_set"], 1)
            pool.wait_ge(S["l1_w_in"], 64)
            wn = wk1n[:].rearrange("p k (g d) -> p (k g) d", d=DH)
            we = wk1[:].rearrange("p k (g h d) -> p (k g) h d", g=GROUPS, d=DH)
            for h in range(HEADS // GROUPS):
                pool.tensor_copy(we[:, :, h, :], wn).then_inc(S["wk1_set"], 1)

            def rstd(b, mv_set, mv, ve, ve_set, out_, out_set):
                hold(pool, mv_set, 2 * b + 2)
                pool.tensor_scalar(ve[:], mv[:, :, 1], EPS, None, ALU.add).then_inc(ve_set, 1)
                at_least(pool, ve_set, b + 1)
                pool.tensor_tensor(out_[:], ve[:], half[:], ALU.pow).then_inc(out_set, 1)

            def a_rstd(b):
                rstd(b, S["mv_a_set"], mv_a, ve_a, S["ve_a_set"], rstd_a, S["rstd_a_set"])

            def a_keys(b):
                hold(pool, S["s_mm"], 8 * b)
                src = kT[0].rearrange("p m (b c) -> p m b c", c=CTX)
                for a in range(2):
                    head = cst[:, C_HEAD2 + a:C_HEAD2 + a + 1, None].broadcast_to([P, KC, CTX])
                    pool.tensor_tensor(k_blk[:, :, a, :], src[:, :, b, :], head, ALU.mult).then_inc(S["k_set"], 1)

            def b_beta(b):
                hold(pool, S["x1_set"], 2 * b)
                for j in range(ST):
                    pool.tensor_tensor(xbeta[:, j, :], x_all[:, ST * b + j, :], beta[:], ALU.add)\
                        .then_inc(S["xbeta_set"], 1)

            def b_rstd(b):
                hold(pool, S["mv_d_set"], 2 * b + 2)
                pool.tensor_scalar(ve_d[:], mv_d[:, :, 1], rs2[:, 0:1], EPS, ALU.mult, ALU.add)\
                    .then_inc(S["ve_d_set"], 1)
                at_least(pool, S["ve_d_set"], b + 1)
                pool.tensor_tensor(ve_d[:], ve_d[:], half[:], ALU.pow).then_inc(S["pow_d_set"], 1)
                hold(pool, S["pow_d_set"], b + 1)
                pool.tensor_scalar(rstd_d[:], ve_d[:], rs[:, 0:1], None, ALU.mult).then_inc(S["rstd_d_set"], 1)

            def b_rstd2(b):
                rstd(b, S["mv_h_set"], mv_h, ve_h, S["ve_h_set"], rstd_h, S["rstd_h_set"])

            def body(b, a_=True, b_=True):
                if a_:
                    a_rstd(b + 1)
                if b_:
                    b_beta(b)
                if a_:
                    a_keys(b + 1)
                if b_:
                    b_rstd(b)
                    b_rstd2(b)

            pool.wait_ge(S["kT_set"], 2)
            pool.wait_ge(S["rs_set"], 2)
            pool.wait_ge(S["half_set"], 2)
            body(-1, b_=False)
            body(0)
            with pool.Fori(1, BATCH - 1) as b:
                body(b)
            body(BATCH - 1, a_=False)

            def group(tab, q):
                return tab[:, EPG * q:EPG * q + EPG] if isinstance(q, int) else tab[:, bass.ds(EPG * q, EPG)]

            def fetch(i, h):
                q = 2 * i + h
                hold(pool, S["xb_T"], q - 1)
                hold(pool, S["wpick_set"], q - 1)
                pool.tensor_copy(take[h][:], group(slot_i, q)).then_inc(S["take_set"], 1)
                hold(pool, S["take_set"], q + 1)
                for e in range(EPG):
                    pool.indirect_dma_start(xb[h][:, e, :], None, rows_d,
                                            bass.IndirectOffsetOnAxis(ap=take[h][:, e:e + 1], axis=0))\
                        .then_inc(S[f"gather{h}"], 16)

            def add(i, h):
                q = 2 * i + h
                for c in range(2):
                    hold(pool, S[f"scatter{c}"], 16 * (EPG // 2) * q)
                pool.tensor_copy(give[h][:], group(slot_i, q)).then_inc(S["give_set"], 1)
                hold(pool, S["give_set"], q + 1)
                for n, e in enumerate((0, 2, 1, 3)):
                    c = n % 2
                    hold(pool, S["yv_set" if e < 2 else "ya_set"], 2 * q + e % 2 + 1)
                    hold(pool, S[f"scatter{c}"], 16 * ((EPG // 2) * q + n // 2))
                    pool.indirect_dma_start(sums_d[c], bass.IndirectOffsetOnAxis(ap=give[h][:, e:e + 1], axis=0),
                                            y[h][:, e, :], None, compute_op=ALU.add).then_inc(S[f"scatter{c}"], 16)

            pool.wait_ge(S["route_done"], 1)
            pool.wait_ge(S["x1_out"], 16 * BATCH)
            pool.wait_ge(S["h_out"], 16 * BATCH)
            pool.wait_ge(S["w_out"], 16 * BATCH)
            pool.wait_ge(S["zero_out"], 16 * (3 + TOKENS // P))
            for i, h in ((-1, 0), (-1, 1), (0, 0), (0, 1)):
                fetch(i + 1, h)
                if i >= 0:
                    add(i, h)
            with pool.Fori(1, QG // 2 - 1) as i:
                for h in range(2):
                    fetch(i + 1, h)
                    add(i, h)
            for h in range(2):
                add(QG // 2 - 1, h)

            def a1_x(b):
                hold(pool, S["sum_in0"], 16 * b + 16)
                hold(pool, S["sum_in1"], 16 * b + 16)
                x = x_all[:, bass.ds(ST * b, ST), :]
                pool.tensor_tensor(x, x, x_add[:, bass.ds(ST * b, ST), :], ALU.add).then_inc(S["x2_set"], 1)

            def a1_keys(b):
                hold(pool, S["s1_mm"], 4 * b)
                src = kT[1].rearrange("p m (b c) -> p m b c", c=CTX)
                for m in range(KC):
                    pool.tensor_tensor(k1_blk[:, m], src[:, m, b, None, :].broadcast_to([P, 8, CTX]),
                                       cst[:, C_HEAD8:C_HEAD8 + 8, None].broadcast_to([P, 8, CTX]), ALU.mult)\
                        .then_inc(S["k1_set"], 1)

            def a1_rstd(b):
                rstd(BATCH + b, S["mv_a_set"], mv_a, ve_a, S["ve_a_set"], rstd_a, S["rstd_a_set"])

            def b1_rstd(b):
                rstd(BATCH + b, S["mv_h_set"], mv_h, ve_h, S["ve_h_set"], rstd_h, S["rstd_h_set"])

            def d1_share(b, e):
                if e == 0:
                    hold(pool, S["share_in"], 16 * b + 16)
                hold(pool, S["act1_set"], E1 * b + e + 1)
                hold(pool, S["down1_mm"], E1 * b + e - 1)
                pool.tensor_tensor(act1w[e % 2][:], act1[e % 2][:], share[:, e, :], ALU.mult).then_inc(S["act1w_set"], 1)

            def layer1(b, a_=True, b_=True, d_=True):
                if a_:
                    a1_rstd(b + 1)
                if d_:
                    d1_share(b - 1, 0)
                    d1_share(b - 1, 1)
                if a_:
                    a1_keys(b + 1)
                if d_:
                    d1_share(b - 1, 2)
                    d1_share(b - 1, 3)
                if b_:
                    b1_rstd(b)
                if d_:
                    for e in range(4, E1):
                        d1_share(b - 1, e)

            pool.wait_ge(S["kT_set"], 4)
            a1_x(0)
            a1_x(1)
            layer1(-1, b_=False, d_=False)
            a1_x(2)
            layer1(0, d_=False)
            a1_x(3)
            layer1(1)
            with pool.Fori(2, BATCH - 2) as b:
                a1_x(b + 2)
                layer1(b)
            layer1(BATCH - 2)
            layer1(BATCH - 1, a_=False)
            layer1(BATCH, a_=False, b_=False)

        @block.scalar
        def _(act):
            for n, v in ((bq0, "bq0"), (bk0, "bk0"), (mask_i, "mask0")):
                act.dma_start(n[:], t[v]).then_inc(S["bias_in"], 16)
            for n, v in ((bv0, "bv0"), (bo0, "bo0"), (gamma, "gamma"), (beta, "beta"), (rs, "rs")):
                act.dma_start(n[:], t[v].partition_broadcast(P)).then_inc(S["bias_in"], 16)
            act.dma_start(o2n_c[:], t["o2n"].rearrange("(p o) -> p o", o=1)).then_inc(S["route_in"], 16)
            act.dma_start(o2n_r[:], t["o2n"].partition_broadcast(P)).then_inc(S["route_in"], 16)
            act.dma_start(mask_u[:], t["mask1"]).then_inc(S["mask_u_in"], 16)
            act.dma_start(bias_q[:], t["bias_q"]).then_inc(S["bias_q_in"], 16)
            act.dma_start(gate1[:], t["gate1"]).then_inc(S["gate1_in"], 16)
            act.wait_ge(S["hi_set"], 1)
            act.activation(hi[:], hi[:], ACT.Exp).then_inc(S["bound_set"], 1)

            def c_hT(b):
                at_least(act, S["h_T"], b + 1)
                at_least(act, S["l_mm"], b)
                act.activation(hT[:].rearrange("p k s -> p (k s)"), banks[6][:, :], ACT.Copy).then_inc(S["hT_set"], 1)

            def b_exp(b, j):
                at_least(act, S["s_mm"], 8 * b + 2 * j + 2)
                at_least(act, S["pv_mm"], 2 * b)
                act.activation(prob[:, j].rearrange("p m s -> p (m s)"), banks[1 + j % 2][:, :], ACT.Exp,
                               scale=DH ** -0.5).then_inc(S["exp_set"], 1)

            def a_hsT(b):
                at_least(act, S["hs_T"], b + 1)
                at_least(act, S["q_mm"], b)
                act.activation(hsT[:].rearrange("p k s -> p (k s)"), banks[0][:, :], ACT.Copy)\
                    .then_inc(S["hsT_set"], 1)

            def a_q(b):
                at_least(act, S["q_mm"], b + 1)
                at_least(act, S["s_mm"], 8 * b)
                for m in range(KC):
                    act.activation(qT[:, m, :], banks[0][:, SEQ * m:SEQ * m + SEQ], ACT.Identity,
                                   bias=bq0[:, m:m + 1]).then_inc(S["q_set"], 1)

            def c_exp(b):
                at_least(act, S["ntop_set"], b + 1)
                at_least(act, S["wsel_set"], 2 * b)
                for j in range(ST):
                    act.activation(expl[:, j, :], logit[:, j, :], ACT.Exp, bias=ntop[:, j:j + 1])\
                        .then_inc(S["expl_set"], 1)
                    act.activation(etop[:, j, :], top[:, j, :], ACT.Exp, bias=ntop[:, j:j + 1],
                                   accum_out=den[:, j:j + 1]).then_inc(S["etop_set"], 1)

            def b_attT(b):
                at_least(act, S["att_T"], b + 1)
                at_least(act, S["o_mm"], b)
                act.activation(attT[:].rearrange("p k s -> p (k s)"), banks[5][:, :], ACT.Copy)\
                    .then_inc(S["attT_set"], 1)

            def c_wT(b):
                at_least(act, S["countT_set"], b + 1)
                at_least(act, S["pos_mm"], b)
                act.activation(wselT[:].rearrange("p j s -> p (j s)"), banks[6][:, 256:512], ACT.Copy)\
                    .then_inc(S["wselT_set"], 1)

            def c_w(b):
                at_least(act, S["pos_set"], b + 1)
                at_least(act, S["den_set"], b + 1)
                at_least(act, S["w_out"], 16 * b)
                for j in range(ST):
                    act.activation(w_rows[:, j, :], banks[7][:, 96 + NEW * j:96 + NEW * j + NEW], ACT.Copy,
                                   scale=rdn[:, j:j + 1]).then_inc(S["w_set"], 1)

            def body(b, a_=True, b_=True, c_=True):
                if c_:
                    c_hT(b - 1)
                if b_:
                    b_exp(b, 0)
                    b_exp(b, 1)
                if a_:
                    a_hsT(b + 1)
                if b_:
                    b_exp(b, 2)
                    b_exp(b, 3)
                if c_:
                    c_exp(b - 1)
                if a_:
                    a_q(b + 1)
                if b_:
                    b_attT(b)
                if c_:
                    c_wT(b - 1)
                    c_w(b - 1)

            act.wait_ge(S["bias_in"], 16 * 8)
            body(-1, b_=False, c_=False)
            body(0, c_=False)
            with act.Fori(1, BATCH - 1) as b:
                body(b)
            body(BATCH - 1, a_=False)
            body(BATCH, a_=False, b_=False)

            def x0_T(i, h):
                q = 2 * i + h
                at_least(act, S["xb_T"], q + 1)
                at_least(act, S["gu0_mm"], 2 * q)
                act.activation(xbT[:, 0, :], banks[0][:, 0:EPG * CAP], ACT.Copy).then_inc(S["xbT_set"], 1)

            def silu(i, h):
                q = 2 * i + h
                for u in range(2):
                    at_least(act, S["gu0_mm"], 2 * q + u + 1)
                    at_least(act, S["act0_set"], 2 * q + u - 1)
                    src = banks[2 + u][0:INTER0, 0:2 * 2 * CAP].rearrange("i (e s c) -> i e s c", e=2, s=2)
                    act.activation(silu0[:, 2 * u:2 * u + 2, :], src[:, :, 0, :], ACT.Silu).then_inc(S["silu0_set"], 1)

            def y0(i, h):
                q = 2 * i + h
                at_least(act, S["wslot_set"], q + 1)
                at_least(act, S["y_mm"], 2 * q + 2)
                for c in range(2):
                    at_least(act, S[f"scatter{c}"], 16 * (EPG // 2) * (q - 1))
                for e in range(2, EPG):
                    act.activation(y[h][:, e, :], banks[5 + 2 * h][0:CAP, D * (e - 2):D * (e - 2) + D], ACT.Copy,
                                   scale=wslot[h][:, e:e + 1]).then_inc(S["ya_set"], 1)

            def experts(i, h, i1, h1, first=False, last=False):
                if not last:
                    x0_T(i1, h1)
                if not first:
                    y0(i, h)
                if not last:
                    silu(i1, h1)

            experts(-1, 1, 0, 0, first=True)
            experts(0, 0, 0, 1)
            experts(0, 1, 1, 0)
            with act.Fori(1, QG // 2 - 1) as i:
                experts(i, 0, i, 1)
                experts(i, 1, i + 1, 0)
            experts(QG // 2 - 1, 0, QG // 2 - 1, 1)
            experts(QG // 2 - 1, 1, QG // 2, 0, last=True)

            def a1_hsT(b):
                at_least(act, S["hs_T"], BATCH + b + 1)
                at_least(act, S["q_mm"], BATCH + b)
                act.activation(hsT[:].rearrange("p k s -> p (k s)"), banks[0][:, :], ACT.Copy)\
                    .then_inc(S["hsT_set"], 1)

            def a1_q(b):
                at_least(act, S["q_mm"], BATCH + b + 1)
                at_least(act, S["s1_mm"], 4 * b)
                act.activation(qT[:].rearrange("p k s -> p (k s)"), banks[0][:, :], ACT.Copy,
                               scale=DH ** -0.5).then_inc(S["q_set"], 1)

            def b1_exp(b, u):
                at_least(act, S["sub_set"], 4 * b + u + 1)
                act.activation(soft[:, u, :], soft[:, u, :], ACT.Exp).then_inc(S["soft_set"], 1)

            def b1_softT(b, u):
                at_least(act, S["soft_T"], 4 * b + u + 1)
                at_least(act, S["pv_mm"], ST * (BATCH + b))
                act.activation(softT[:, u, :], banks[3][:, :], ACT.Copy).then_inc(S["softT_set"], 1)

            def b1_attT(b):
                at_least(act, S["att_T"], BATCH + b + 1)
                at_least(act, S["o_mm"], BATCH + b)
                act.activation(attT[:].rearrange("p k s -> p (k s)"), banks[0][:, :], ACT.Copy)\
                    .then_inc(S["attT_set"], 1)

            def c1_hT(b):
                at_least(act, S["h1_T"], b + 1)
                at_least(act, S["gu1_mm"], E1 * b)
                act.activation(hT1[:].rearrange("p k s -> p (k s)"), banks[5][:, :], ACT.Copy).then_inc(S["hT1_set"], 1)

            def c1_exp(b):
                at_least(act, S["gap_set"], b + 1)
                act.activation(egap[:], gap[:], ACT.Exp).then_inc(S["egap_set"], 1)

            def c1_shareT(b):
                at_least(act, S["share_T"], b + 1)
                hold(act, S["share_out"], 16 * b)
                act.activation(shareT[:], banks[6][0:E1, 0:SEQ], ACT.Copy).then_inc(S["shareT_set"], 1)

            def d1_silu(b, e):
                at_least(act, S["gu1_mm"], E1 * b + e + 1)
                at_least(act, S["act1_set"], E1 * b + e - 1)
                act.activation(silu1[e % 2][:], banks[5 + e % 2][:, 0:SEQ], ACT.Silu).then_inc(S["silu1_set"], 1)

            def layer1(b, a_=True, b_=True, d_=True):
                if d_:
                    c1_exp(b - 1)
                if b_:
                    b1_exp(b, 0)
                    b1_exp(b, 1)
                if a_:
                    a1_hsT(b + 1)
                if d_:
                    c1_shareT(b - 1)
                if b_:
                    b1_softT(b, 0)
                    b1_exp(b, 2)
                    b1_softT(b, 1)
                    b1_exp(b, 3)
                if a_:
                    a1_q(b + 1)
                if b_:
                    b1_softT(b, 2)
                    b1_softT(b, 3)
                if d_:
                    for e in range(0, 4):
                        d1_silu(b - 1, e)
                if b_:
                    b1_attT(b)
                if d_:
                    for e in range(4, E1):
                        d1_silu(b - 1, e)
                if b_:
                    c1_hT(b)

            layer1(-1, b_=False, d_=False)
            layer1(0, d_=False)
            layer1(1)
            with act.Fori(2, BATCH - 1) as b:
                layer1(b)
            layer1(BATCH - 1, a_=False)
            layer1(BATCH, a_=False, b_=False)

        @block.tensor
        def _(pe):
            pe.wait_ge(S["ctx_in"], 16)
            pe.wait_ge(S["kv_w_in"], 32)
            for m in range(KC):
                for k in range(KC):
                    mm = pe.matmul(banks[m][:, :], wk0[:, k, P * m:P * m + P], cT[:, k, :], start=k == 0, stop=k == KC - 1)
                mm.then_inc(S["kT_mm"], 1)
            pe.wait_ge(S["cdup_set"], 2)
            for b in range(BATCH):
                for k in range(KC):
                    mm = pe.matmul(banks[2 + b // 2][:, D * (b % 2):D * (b % 2) + D],
                                   cdup[:, k, b].rearrange("p a c -> p (a c)"), wv0[:, k, :],
                                   start=k == 0, stop=k == KC - 1)
                if b % 2:
                    mm.then_inc(S["v_mm"], 1)
            pe.wait_ge(S["wk1_set"], 4)
            pe.wait_ge(S["kT_set"], 2)
            for m in range(KC):
                for k in range(KC):
                    mm = pe.matmul(banks[m][:, :], wk1[:, k, P * m:P * m + P], cT[:, k, :], start=k == 0, stop=k == KC - 1)
                mm.then_inc(S["kT_mm"], 1)
            for b in range(BATCH):
                for k in range(KC):
                    mm = pe.matmul(banks[6][:, CTX * b:CTX * b + CTX], cdup[:, k, b].rearrange("p a c -> p (a c)"),
                                   wv1[:, k, :], start=k == 0, stop=k == KC - 1)
            mm.then_inc(S["v_mm"], 1)

            def a_T(b):
                at_least(pe, S["hs_set"], b + 1)
                at_least(pe, S["q_set"], 2 * b)
                for j in range(ST):
                    for k in range(KC):
                        mm = pe.transpose(banks[0][:, SEQ * k + P * j:SEQ * k + P * j + P], hs[:, j, P * k:P * k + P], ident)
                mm.then_inc(S["hs_T"], 1)

            def a_q(b):
                at_least(pe, S["hsT_set"], b + 1)
                for m in range(KC):
                    for k in range(KC):
                        mm = pe.matmul(banks[0][:, SEQ * m:SEQ * m + SEQ], wq0[:, k, P * m:P * m + P], hsT[:, k, :],
                                       start=k == 0, stop=k == KC - 1)
                mm.then_inc(S["q_mm"], 1)

            def b_s(b, j):
                at_least(pe, S["exp_set"], 4 * b + j - 1)
                if j == 0:
                    at_least(pe, S["q_set"], 2 * b + 2)
                    at_least(pe, S["k_set"], 2 * b + 2)
                for m in range(KC):
                    rows = slice(32 * j, 32 * j + 32)
                    pe.matmul(banks[1 + j % 2][:, SEQ * m:SEQ * m + SEQ],
                              k_blk[rows, m].rearrange("p a c -> p (a c)"), qT[rows, m, :],
                              start=True, stop=True).then_inc(S["s_mm"], 1)

            def b_pv(b):
                at_least(pe, S["clip_set"], 4 * b + 4)
                at_least(pe, S["att_set"], 2 * b)
                for j in range(ST):
                    for r in range(PAIRS):
                        mm = pe.matmul(banks[3 + j][:, 2 * VW * r:2 * VW * r + 2 * VW],
                                       prob[:, r % 4, r // 4, P * j:P * j + P],
                                       v_blk[0][:, b, r].rearrange("p a d -> p (a d)"), start=True, stop=True)
                    mm.then_inc(S["pv_mm"], 1)

            def b_T(b):
                at_least(pe, S["att_set"], 2 * b + 2)
                at_least(pe, S["delta_set"], b)
                for j in range(ST):
                    for k in range(KC):
                        mm = pe.transpose(banks[5][:, SEQ * k + P * j:SEQ * k + P * j + P], att[:, j, P * k:P * k + P], ident)
                mm.then_inc(S["att_T"], 1)

            def b_o(b):
                at_least(pe, S["attT_set"], b + 1)
                for j in range(ST):
                    for k in range(KC):
                        mm = pe.matmul(banks[5][:, D * j:D * j + D], attT[:, k, P * j:P * j + P], wo0[:, k, :],
                                       start=k == 0, stop=k == KC - 1)
                mm.then_inc(S["o_mm"], 1)

            def c_T(b):
                at_least(pe, S["h_set"], 2 * b + 2)
                at_least(pe, S["wselT_set"], b)
                at_least(pe, S["countT_set"], b)
                for j in range(ST):
                    for k in range(KC):
                        mm = pe.transpose(banks[6][:, SEQ * k + P * j:SEQ * k + P * j + P], h_rows[:, j, P * k:P * k + P], ident)
                mm.then_inc(S["h_T"], 1)

            def c_l(b):
                at_least(pe, S["hT_set"], b + 1)
                for j in range(ST):
                    for k in range(KC):
                        mm = pe.matmul(banks[6][:, OLD * j:OLD * j + OLD], hT[:, k, P * j:P * j + P], gate0[:, k, :],
                                       start=k == 0, stop=k == KC - 1)
                mm.then_inc(S["l_mm"], 1)

            def c_count(b):
                at_least(pe, S["sel_set"], b + 1)
                at_least(pe, S["selsum_set"], 2 * b)
                at_least(pe, S["logit_set"], b + 1)
                for j in range(ST):
                    o = banks[6][:, P * j:P * j + P]
                    pe.matmul(o, selsum[:] , ones_b[:], start=True, stop=False)
                    if j == 1:
                        pe.matmul(o, sel[:, 0, :], ones_b[:], start=False, stop=False)
                    mm = pe.matmul(o, sel[:, j, :], tri[:], start=False, stop=True)
                mm.then_inc(S["count_mm"], 1)

            def c_wT(b):
                at_least(pe, S["wsel_set"], 2 * b + 2)
                for j in range(ST):
                    mm = pe.transpose(banks[6][:, 256 + P * j:256 + P * j + P], wsel[:, j, :], ident)
                mm.then_inc(S["wsel_T"], 1)

            def c_pos(b):
                at_least(pe, S["countT_set"], b + 1)
                at_least(pe, S["wselT_set"], b + 1)
                at_least(pe, S["w_set"], 2 * b)
                at_least(pe, S["slotb_acc"], b - 1)
                for j in range(ST):
                    pe.matmul(banks[7][:, NEW * j:NEW * j + NEW], countT[:, j, :], map_b[:], start=True, stop=True)
                    mm = pe.matmul(banks[7][:, 96 + NEW * j:96 + NEW * j + NEW], wselT[:, j, :], map_f[:],
                                   start=True, stop=True)
                mm.then_inc(S["pos_mm"], 1)

            def d_slots(b):
                at_least(pe, S["hit_set"], 2 * b + 2)
                at_least(pe, S["w_set"], 2 * b + 2)
                at_least(pe, S["slotb_acc"], b)
                at_least(pe, S["slot_acc"], b)
                for j in range(ST):
                    for n in range(NEW):
                        mm = pe.matmul(banks[7][0:CAP, 256 + 2 * n:256 + 2 * n + 2], hit[:, j, n // EPG, :, n % EPG],
                                       loc1[:, j, :], start=j == 0 and n == 0, stop=j == ST - 1, skip_group_check=True)
                mm.then_inc(S["slot_mm"], 1)

            def body(b, a_=True, b_=True, c_=True, d_=True):
                if d_:
                    d_slots(b - 2)
                if c_:
                    c_T(b - 1)
                if b_:
                    b_s(b, 0)
                    b_s(b, 1)
                if a_:
                    a_T(b + 1)
                if c_:
                    c_l(b - 1)
                if b_:
                    b_s(b, 2)
                    b_s(b, 3)
                if a_:
                    a_q(b + 1)
                if b_:
                    b_pv(b)
                if c_:
                    c_count(b - 1)
                    c_wT(b - 1)
                if b_:
                    b_T(b)
                if c_:
                    c_pos(b - 1)
                if b_:
                    b_o(b)

            pe.wait_ge(S["cst_in"], 16)
            pe.wait_ge(S["q_w_in"], 48)
            pe.wait_ge(S["kT_set"], 4)
            pe.wait_ge(S["v_set"], 13)
            pe.wait_ge(S["tri_set"], 1)
            pe.wait_ge(S["place_set"], 6)
            pe.wait_ge(S["map_set"], 4)
            pe.wait_ge(S["loc_set"], 2)
            pe.wait_ge(S["vblk_ones"], 4)
            body(-1, b_=False, c_=False, d_=False)
            body(0, c_=False, d_=False)
            body(1, d_=False)
            with pe.Fori(2, BATCH - 1) as b:
                body(b)
            body(BATCH - 1, a_=False)
            body(BATCH, a_=False, b_=False)
            body(BATCH + 1, a_=False, b_=False, c_=False)

            def x0_T(i, h):
                q = 2 * i + h
                at_least(pe, S[f"gather{h}"], 16 * EPG * (i + 1))
                at_least(pe, S["xbT_set"], 2 * q)
                for k in range(KC):
                    for e in range(EPG):
                        mm = pe.transpose(banks[k][:, CAP * e:CAP * e + CAP], xb[h][:, e, P * k:P * k + P],
                                          ident[0:CAP, 0:CAP])
                mm.then_inc(S["xb_T"], 1)

            def gu(i, h):
                q = 2 * i + h
                at_least(pe, S["xbT_set"], 2 * q + 2)
                at_least(pe, S["act0_set"], 2 * q)
                at_least(pe, S[f"w0_ld{h}"], 32 * (i + 1))
                for e in range(EPG):
                    for s in range(2):
                        o = CAP * (2 * (e % 2) + s)
                        for k in range(KC):
                            mm = pe.matmul(banks[2 + e // 2][0:INTER0, o:o + CAP],
                                           gu0[h][:, k, e, INTER0 * s:INTER0 * s + INTER0], xbT[:, k, CAP * e:CAP * e + CAP],
                                           start=k == 0, stop=k == KC - 1)
                    if e % 2:
                        mm.then_inc(S["gu0_mm"], 1)

            def down(i, h):
                q = 2 * i + h
                for e in range(EPG):
                    if e % 2 == 0:
                        at_least(pe, S["act0_set"], 2 * q + e // 2 + 1)
                        at_least(pe, S["ya_set" if e else "yv_set"], 2 * (q - 1))
                    mm = pe.matmul(banks[4 + 2 * h + e // 2][0:CAP, D * (e % 2):D * (e % 2) + D], act0[:, e, :],
                                   down0[h][:, e, :], start=True, stop=True)
                    if e % 2:
                        mm.then_inc(S["y_mm"], 1)

            def experts(i, h, i1, h1, first=False, last=False):
                if not last:
                    x0_T(i1, h1)
                if not first:
                    down(i, h)
                if not last:
                    gu(i1, h1)

            pe.wait_ge(S["route_done"], 1)
            pe.wait_ge(S["w_set"], 2 * BATCH)
            experts(-1, 1, 0, 0, first=True)
            experts(0, 0, 0, 1)
            experts(0, 1, 1, 0)
            with pe.Fori(1, QG // 2 - 1) as i:
                experts(i, 0, i, 1)
                experts(i, 1, i + 1, 0)
            experts(QG // 2 - 1, 0, QG // 2 - 1, 1)
            experts(QG // 2 - 1, 1, QG // 2, 0, last=True)

            def a1_T(b):
                at_least(pe, S["hs_set"], BATCH + b + 1)
                at_least(pe, S["q_set"], 2 * BATCH + b)
                for j in range(ST):
                    for k in range(KC):
                        mm = pe.transpose(banks[0][:, SEQ * k + P * j:SEQ * k + P * j + P], hs[:, j, P * k:P * k + P], ident)
                mm.then_inc(S["hs_T"], 1)

            def a1_q(b):
                at_least(pe, S["hsT_set"], BATCH + b + 1)
                for m in range(KC):
                    for k in range(KC):
                        mm = pe.matmul(banks[0][:, SEQ * m:SEQ * m + SEQ], wq1[:, k, P * m:P * m + P], hsT[:, k, :],
                                       start=k == 0, stop=k == KC - 1)
                mm.then_inc(S["q_mm"], 1)

            def b1_s(b, u):
                j, m = u // KC, u % KC
                at_least(pe, S["sub_set"], 4 * b + u - 1)
                if u == 0:
                    at_least(pe, S["q_set"], 2 * BATCH + b + 1)
                    at_least(pe, S["k1_set"], KC * b + KC)
                o = banks[1 + u % 2][:, :]
                pe.matmul(o, qT[:, m, P * j:P * j + P], k1_blk[:, m].rearrange("p h c -> p (h c)"), start=True,
                          stop=False)
                pe.matmul(o, bias_q[:, P * j:P * j + P], bias_k[:, b, 512 * m:512 * m + 512], start=False, stop=True)\
                    .then_inc(S["s1_mm"], 1)

            def b1_T(b, u):
                at_least(pe, S["soft_set"], 4 * b + u + 1)
                at_least(pe, S["softT_set"], 4 * b + u)
                for r in range(4):
                    mm = pe.transpose(banks[3][:, P * r:P * r + P], soft[:, u, P * r:P * r + P], ident)
                mm.then_inc(S["soft_T"], 1)

            def b1_pv(b, j):
                at_least(pe, S["softT_set"], 4 * b + 2 * j + 2)
                at_least(pe, S["att_set"], ST * (BATCH + b) + j)
                for r in range(PAIRS):
                    mm = pe.matmul(banks[4][:, 2 * VW * r:2 * VW * r + 2 * VW],
                                   softT[:, 2 * j + r // 4, P * (r % 4):P * (r % 4) + P],
                                   v_blk[1][:, b, r].rearrange("p a d -> p (a d)"), start=True, stop=True)
                mm.then_inc(S["pv_mm"], 1)

            def b1_T2(b):
                at_least(pe, S["att_set"], ST * (BATCH + b) + ST)
                if not (isinstance(b, int) and b == BATCH - 1):
                    at_least(pe, S["q_set"], 2 * BATCH + b + 2)
                for j in range(ST):
                    for k in range(KC):
                        mm = pe.transpose(banks[0][:, SEQ * k + P * j:SEQ * k + P * j + P], att[:, j, P * k:P * k + P], ident)
                mm.then_inc(S["att_T"], 1)

            def b1_o(b):
                at_least(pe, S["attT_set"], BATCH + b + 1)
                for j in range(ST):
                    for k in range(KC):
                        mm = pe.matmul(banks[0][:, D * j:D * j + D], attT[:, k, P * j:P * j + P], wo1[:, k, :],
                                       start=k == 0, stop=k == KC - 1)
                mm.then_inc(S["o_mm"], 1)

            def c1_T(b):
                at_least(pe, S["h_set"], 2 * (BATCH + b) + 2)
                at_least(pe, S["act1_set"], E1 * b)
                for j in range(ST):
                    for k in range(KC):
                        mm = pe.transpose(banks[5][:, SEQ * k + P * j:SEQ * k + P * j + P], h_rows[:, j, P * k:P * k + P], ident)
                mm.then_inc(S["h1_T"], 1)

            def c1_l(b):
                at_least(pe, S["hT1_set"], b + 1)
                for j in range(ST):
                    for k in range(KC):
                        mm = pe.matmul(banks[6][:, E1 * j:E1 * j + E1], hT1[:, k, P * j:P * j + P], gate1[:, k, :],
                                       start=k == 0, stop=k == KC - 1)
                mm.then_inc(S["l1_mm"], 1)

            def c1_shareT(b):
                at_least(pe, S["share_set"], b + 1)
                for j in range(ST):
                    mm = pe.transpose(banks[6][0:E1, P * j:P * j + P], share_c[:, j, :], ident)
                mm.then_inc(S["share_T"], 1)

            def d1_gu(b, e):
                at_least(pe, S["act1_set"], E1 * b + e - 1)
                if e == 1:
                    at_least(pe, S["shareT_set"], b + 1)
                o = banks[5 + e % 2]
                for n in range(2):
                    for k in range(KC):
                        mm = pe.matmul(o[:, SEQ * n:SEQ * n + SEQ], gu1[:, e, k, n, :], hT1[:, k, :],
                                       start=k == 0, stop=k == KC - 1)
                mm.then_inc(S["gu1_mm"], 1)

            def d1_down(b, e):
                at_least(pe, S["act1w_set"], E1 * b + e + 1)
                if e == 0:
                    at_least(pe, S["o_set"], b)
                for j in range(ST):
                    mm = pe.matmul(banks[7][:, D * j:D * j + D], act1w[e % 2][:, P * j:P * j + P], down1[:, e, :],
                                   start=e == 0 and j == 0, stop=e == E1 - 1, skip_group_check=True)
                mm.then_inc(S["down1_mm"], 1)

            def layer1(b, a_=True, b_=True, d_=True):
                steps = [
                    (b_, lambda: b1_s(b, 0)), (b_, lambda: b1_s(b, 1)), (a_, lambda: a1_T(b + 1)),
                    (d_, lambda: c1_shareT(b - 1)), (b_, lambda: b1_T(b, 0)), (b_, lambda: b1_s(b, 2)),
                    (b_, lambda: b1_T(b, 1)), (b_, lambda: b1_s(b, 3)), (a_, lambda: a1_q(b + 1)),
                    (d_, lambda: d1_gu(b - 1, 0)), (b_, lambda: b1_pv(b, 0)), (b_, lambda: b1_T(b, 2)),
                    (d_, lambda: d1_gu(b - 1, 1)), (b_, lambda: b1_T(b, 3)), (d_, lambda: d1_down(b - 1, 0)),
                    (d_, lambda: d1_gu(b - 1, 2)), (b_, lambda: b1_pv(b, 1)), (d_, lambda: d1_down(b - 1, 1)),
                    (d_, lambda: d1_gu(b - 1, 3)), (b_, lambda: b1_T2(b)), (d_, lambda: d1_down(b - 1, 2)),
                    (d_, lambda: d1_gu(b - 1, 4)), (b_, lambda: b1_o(b)), (d_, lambda: d1_down(b - 1, 3)),
                    (d_, lambda: d1_gu(b - 1, 5)), (d_, lambda: d1_down(b - 1, 4)), (d_, lambda: d1_gu(b - 1, 6)),
                    (d_, lambda: d1_down(b - 1, 5)), (d_, lambda: d1_gu(b - 1, 7)), (d_, lambda: d1_down(b - 1, 6)),
                    (d_, lambda: d1_down(b - 1, 7)), (b_, lambda: c1_T(b)), (b_, lambda: c1_l(b)),
                ]
                for do, step in steps:
                    if do:
                        step()

            pe.wait_ge(S["l1_w_in"], 64)
            pe.wait_ge(S["gate1_in"], 16)
            pe.wait_ge(S["bias_q_in"], 16)
            pe.wait_ge(S["e1_w_in"], 32)
            pe.wait_ge(S["bias1_in"], 2 * 16 * BATCH)
            pe.wait_ge(S["yv_set"], 2 * QG)
            pe.wait_ge(S["ya_set"], 2 * QG)
            layer1(-1, b_=False, d_=False)
            layer1(0, d_=False)
            layer1(1)
            with pe.Fori(2, BATCH - 1) as b:
                layer1(b)
            layer1(BATCH - 1, a_=False)
            layer1(BATCH, a_=False, b_=False)

        @block.vector
        def _(dve):
            dve.wait_ge(S["bias_in"], 16 * 8)
            dve.tensor_scalar(hi[:], mask_i[:], 0.5, 100.0, ALU.is_gt, ALU.mult).then_inc(S["rs_set"], 1)
            dve.tensor_scalar(rs[:], rs[:], 0.0, 0.3, ALU.max, ALU.min).then_inc(S["rs_set"], 1)
            dve.wait_ge(S["rs_set"], 2)
            dve.tensor_scalar(hi[:], hi[:], -50.0, None, ALU.add).then_inc(S["hi_set"], 1)
            dve.tensor_tensor(rs2[:], rs[:], rs[:], ALU.mult).then_inc(S["rs_set"], 1)
            dve.wait_ge(S["mask_u_in"], 16)
            dve.tensor_scalar(mask_b[:].rearrange("p b o c -> p (b o c)"), mask_u[:], 1.0, -MASKED, ALU.subtract,
                              ALU.mult).then_inc(S["mask_b_set"], 1)
            dve.wait_ge(S["route_in"], 32)
            dve.wait_ge(S["cst_in"], 16)
            dve.tensor_copy(o2n_f[:], o2n_c[:]).then_inc(S["map_set"], 1)
            dve.tensor_scalar(unkept[:], o2n_r[:], -1.0, MASKED, ALU.is_equal, ALU.mult).then_inc(S["map_set"], 1)
            dve.tensor_copy(tri[:], cst[:, C_TRI:C_TRI + P]).then_inc(S["tri_set"], 1)
            dve.memset(loc1[:, :, 1], 1.0).then_inc(S["loc_set"], 1)
            dve.tensor_copy(loc1[:, :, 0], cst[:, C_LOC:C_LOC + ST]).then_inc(S["loc_set"], 1)
            dve.wait_ge(S["map_set"], 1)
            for m in (map_f, map_b):
                dve.tensor_scalar(m[:], cst[:, C_E48:C_E48 + NEW], o2n_f[:, 0:1], None, ALU.is_equal)\
                    .then_inc(S["map_set"], 1)
            for m in range(KC):
                dve.wait_ge(S["kT_mm"], m + 1)
                dve.tensor_scalar(kT[0][:, m, :], banks[m][:, :], bk0[:, m:m + 1], None, ALU.add).then_inc(S["kT_set"], 1)
            dve.wait_ge(S["vblk_zero"], 2)
            for v in v_blk:
                for a in range(2):
                    dve.memset(v[CTX * a:CTX * a + CTX, :, :, a, DH:VW], 1.0).then_inc(S["vblk_ones"], 1)
            for c in range(4):
                dve.wait_ge(S["v_mm"], c + 1)
                for a in range(2):
                    h = slice(CTX * a, CTX * a + CTX)
                    src = banks[2 + c][h, :].rearrange("p (b r a d) -> p b r a d", b=2, a=2, d=DH)
                    bias = bv0[h, :].rearrange("p (r a d) -> p r a d", a=2, d=DH)
                    for e in range(2):
                        ins = dve.tensor_tensor(v_blk[0][h, 2 * c + e, :, a, 0:DH], src[:, e, :, a, :],
                                                bias[:, :, a, :], ALU.add)
                    ins.then_inc(S["v_set"], 1)
            for m in range(KC):
                dve.wait_ge(S["kT_mm"], KC + m + 1)
                dve.tensor_copy(kT[1][:, m, :], banks[m][:, :]).then_inc(S["kT_set"], 1)
            dve.wait_ge(S["v_mm"], 5)
            for a in range(2):
                h = slice(CTX * a, CTX * a + CTX)
                src = banks[6][h, :].rearrange("p (b g d) -> p b g d", b=BATCH, d=DH)
                dst = v_blk[1][h, :, :, a, 0:DH].rearrange("p b (g r) d -> p b g r d", r=2)
                for r in range(2):
                    dve.tensor_copy(dst[:, :, :, r, :], src).then_inc(S["v_set"], 1)
            dve.tensor_copy(ident_b[:], ident).then_inc(S["v_set"], 1)
            dve.wait_ge(S["bound_set"], 1)
            dve.wait_ge(S["place_set"], 6)

            def a_stat(b):
                hold(dve, S["x_in"], 16 * b + 16)
                for j in range(ST):
                    dve.bn_stats(stat6[:, j, :], x_all[:, ST * b + j, :]).then_inc(S["stat_a"], 1)
                hold(dve, S["stat_a"], 2 * b + 2)
                hold(dve, S["rstd_a_set"], b)
                for j in range(ST):
                    dve.bn_aggr(mv_a[:, j, :], stat6[:, j, :]).then_inc(S["mv_a_set"], 1)

            def a_norm(b):
                at_least(dve, S["rstd_a_set"], b + 1)
                at_least(dve, S["hs_T"], b)
                for j in range(ST):
                    ins = dve.tensor_scalar(hs[:, j, :], x_all[:, ST * b + j, :], mv_a[:, j, 0:1], rstd_a[:, j:j + 1],
                                            ALU.subtract, ALU.mult)
                ins.then_inc(S["hs_set"], 1)

            def b_clip(b, j):
                at_least(dve, S["exp_set"], 4 * b + j + 1)
                v = prob[:, j].rearrange("p m s -> p (m s)")
                dve.tensor_scalar(v, v, hi[:, b:b + 1] if isinstance(b, int) else hi[:, bass.ds(b, 1)], lo[:, 0:1],
                                  ALU.min, ALU.max).then_inc(S["clip_set"], 1)

            def b_att(b, j):
                at_least(dve, S["pv_mm"], 2 * b + j + 1)
                at_least(dve, S["att_T"], b)
                src = banks[3 + j][:, 0:HEADS * VW].rearrange("p (h v) -> p h v", v=VW)
                r = rden[:, j].rearrange("p r a -> p (r a)")
                dve.reciprocal(r, src[:, :, DH]).then_inc(S["rden_set"], 1)
                at_least(dve, S["rden_set"], 2 * b + j + 1)
                dve.tensor_tensor(att[:, j, :].rearrange("p (h d) -> p h d", d=DH), src[:, :, 0:DH],
                                  r[:, :, None].broadcast_to([P, HEADS, DH]), ALU.mult).then_inc(S["att_set"], 1)

            def b_delta(b):
                at_least(dve, S["o_mm"], b + 1)
                dve.tensor_tensor(delta[:], banks[5][:, :].rearrange("p (j d) -> p j d", d=D),
                                  bo0[:, None, :].broadcast_to([P, ST, D]), ALU.add).then_inc(S["delta_set"], 1)
                at_least(dve, S["delta_set"], b + 1)
                for j in range(ST):
                    dve.bn_stats(stat6[:, j, :], delta[:, j, :]).then_inc(S["stat_d"], 1)
                hold(dve, S["stat_d"], 2 * b + 2)
                for j in range(ST):
                    dve.bn_aggr(mv_d[:, j, :], stat6[:, j, :]).then_inc(S["mv_d_set"], 1)
                at_least(dve, S["mv_d_set"], 2 * b + 2)
                for j in range(ST):
                    dve.scalar_tensor_tensor(dgam[:, j, :], delta[:, j, :], mv_d[:, j, 0:1], gamma[:], ALU.subtract,
                                             ALU.mult).then_inc(S["dgam_set"], 1)

            def b_x1(b):
                at_least(dve, S["rstd_d_set"], b + 1)
                at_least(dve, S["xbeta_set"], 2 * b + 2)
                at_least(dve, S["dgam_set"], 2 * b + 2)
                for j in range(ST):
                    dve.scalar_tensor_tensor(x_all[:, ST * b + j, :], dgam[:, j, :], rstd_d[:, j:j + 1], xbeta[:, j, :],
                                             ALU.mult, ALU.add).then_inc(S["x1_set"], 1)
                hold(dve, S["x1_set"], 2 * b + 2)
                for j in range(ST):
                    dve.bn_stats(stat6[:, j, :], x_all[:, ST * b + j, :]).then_inc(S["stat_h"], 1)
                hold(dve, S["stat_h"], 2 * b + 2)
                for j in range(ST):
                    dve.bn_aggr(mv_h[:, j, :], stat6[:, j, :]).then_inc(S["mv_h_set"], 1)

            def b_h(b):
                at_least(dve, S["rstd_h_set"], b + 1)
                at_least(dve, S["h_T"], b)
                at_least(dve, S["h_out"], 16 * b)
                for j in range(ST):
                    dve.tensor_scalar(h_rows[:, j, :], x_all[:, ST * b + j, :], mv_h[:, j, 0:1], rstd_h[:, j:j + 1],
                                      ALU.subtract, ALU.mult).then_inc(S["h_set"], 1)

            def c_top(b):
                at_least(dve, S["l_mm"], b + 1)
                at_least(dve, S["etop_set"], 2 * b)
                dve.tensor_tensor(logit[:], banks[6][:, 0:ST * OLD].rearrange("p (j o) -> p j o", o=OLD),
                                  unkept[:, None, :].broadcast_to([P, ST, OLD]), ALU.add).then_inc(S["logit_set"], 1)
                hold(dve, S["logit_set"], b + 1)
                for j in range(ST):
                    dve.max(top[:, j, :], logit[:, j, :]).then_inc(S["top_set"], 1)
                at_least(dve, S["top_set"], 2 * b + 2)
                dve.tensor_scalar(ntop[:], top[:, :, 0], -1.0, None, ALU.mult).then_inc(S["ntop_set"], 1)
                for j in range(ST):
                    dve.match_replace(left[:, j, :], top[:, j, :], logit[:, j, :], TAKEN).then_inc(S["left_set"], 1)
                at_least(dve, S["count_mm"], b)
                if not isinstance(b, int) or b > 0:
                    dve.tensor_tensor(selboth[:], sel[:, 0, :], sel[:, 1, :], ALU.add).then_inc(S["selsum_set"], 1)
                    at_least(dve, S["selsum_set"], 2 * b - 1)
                    dve.tensor_tensor(selsum[:], selsum[:], selboth[:], ALU.add).then_inc(S["selsum_set"], 1)
                at_least(dve, S["left_set"], 2 * b + 2)
                dve.tensor_tensor(sel[:], left[:], logit[:], ALU.not_equal).then_inc(S["sel_set"], 1)

            def c_weight(b):
                at_least(dve, S["expl_set"], 2 * b + 2)
                at_least(dve, S["sel_set"], b + 1)
                at_least(dve, S["wsel_T"], b)
                for j in range(ST):
                    dve.tensor_tensor(wsel[:, j, :], expl[:, j, :], sel[:, j, :], ALU.mult).then_inc(S["wsel_set"], 1)
                at_least(dve, S["etop_set"], 2 * b + 2)
                at_least(dve, S["w_set"], 2 * b)
                dve.reciprocal(rdn[:], den[:]).then_inc(S["den_set"], 1)

            def c_count(b):
                at_least(dve, S["wsel_T"], b + 1)
                at_least(dve, S["pos_mm"], b)
                dve.tensor_scalar(countT[:].rearrange("p j s -> p (j s)"), banks[6][:, 0:ST * P], float(P), None,
                                  ALU.min).then_inc(S["countT_set"], 1)

            def c_pos(b):
                at_least(dve, S["pos_mm"], b + 1)
                dve.tensor_scalar(off[:].rearrange("p j e -> p (j e)"), banks[7][:, 96:192], 0.0, float(P), ALU.is_le,
                                  ALU.mult).then_inc(S["off_set"], 1)
                at_least(dve, S["off_set"], b + 1)
                dve.scalar_tensor_tensor(pos[:].rearrange("p j e -> p (j e)"), banks[7][:, 0:96], float(P),
                                         off[:].rearrange("p j e -> p (j e)"), ALU.min, ALU.add).then_inc(S["pos_set"], 1)

            def c_hit(b):
                at_least(dve, S["pos_set"], b + 1)
                at_least(dve, S["slot_mm"], b)
                for j in range(ST):
                    choice = pos[:, j, :].rearrange("t (q e) -> t q e", e=EPG)
                    dve.tensor_tensor(hit[:, j], place[:], choice[:, :, None, :].broadcast_to([P, QG, CAP, EPG]),
                                      ALU.is_equal).then_inc(S["hit_set"], 1)

            def d_slots(b):
                at_least(dve, S["slot_mm"], b + 1)
                src = banks[7][0:CAP, 256:256 + 2 * NEW].rearrange("p (n v) -> p n v", v=2)
                at_least(dve, S["slot_acc"], b)
                at_least(dve, S["slotb_acc"], b)
                dve.tensor_tensor(slots[:], src, slots[:], ALU.add).then_inc(S["slot_acc"], 1)
                col = cst[0:CAP, C_B256 + b:C_B256 + b + 1] if isinstance(b, int) else cst[0:CAP, bass.ds(C_B256 + b, 1)]
                dve.scalar_tensor_tensor(slot_b[:], src[:, :, 1], col, slot_b[:], ALU.mult, ALU.add)\
                    .then_inc(S["slotb_acc"], 1)

            def body(b, a_=True, b_=True, c_=True, d_=True):
                if a_:
                    a_stat(b + 1)
                if b_:
                    b_clip(b, 0)
                if a_:
                    a_norm(b + 1)
                if d_:
                    d_slots(b - 2)
                if b_:
                    b_clip(b, 1)
                if c_:
                    c_top(b - 1)
                if b_:
                    b_clip(b, 2)
                    b_clip(b, 3)
                if c_:
                    c_weight(b - 1)
                    c_count(b - 1)
                if b_:
                    b_att(b, 0)
                    b_att(b, 1)
                if c_:
                    c_pos(b - 1)
                if b_:
                    b_delta(b)
                if c_:
                    c_hit(b - 1)
                if b_:
                    b_x1(b)
                    b_h(b)

            body(-1, b_=False, c_=False, d_=False)
            body(0, c_=False, d_=False)
            body(1, d_=False)
            with dve.Fori(2, BATCH - 1) as b:
                body(b)
            body(BATCH - 1, a_=False)
            body(BATCH, a_=False, b_=False)
            body(BATCH + 1, a_=False, b_=False, c_=False)
            dve.wait_ge(S["slotb_acc"], BATCH)
            dve.wait_ge(S["slot_acc"], BATCH)
            dve.tensor_scalar(empty[:], slots[:, :, 1], -1.0, 1.0, ALU.mult, ALU.add).then_inc(S["slot_acc"], 1)
            dve.tensor_tensor(slot_f[:], slots[:, :, 0], slot_b[:], ALU.add).then_inc(S["slot_acc"], 1)
            dve.wait_ge(S["slot_acc"], BATCH + 2)
            dve.scalar_tensor_tensor(slot_f[:], empty[:], cst[0:CAP, C_PAD:C_PAD + 1], slot_f[:], ALU.mult, ALU.add)\
                .then_inc(S["slot_acc"], 1)
            dve.wait_ge(S["slot_acc"], BATCH + 3)
            dve.tensor_copy(slot_i[:], slot_f[:]).then_inc(S["route_done"], 1)

            def x0_T(i, h):
                q = 2 * i + h
                at_least(dve, S["xb_T"], q + 1)
                at_least(dve, S["gu0_mm"], 2 * q)
                dve.tensor_copy(xbT[:, 1, :], banks[1][:, 0:EPG * CAP]).then_inc(S["xbT_set"], 1)
                wgt = xb[h][:, :, D + EPG * q:D + EPG * q + EPG] if isinstance(q, int) else \
                    xb[h][:, :, bass.ds(D + EPG * q, EPG)]
                own = cst[0:CAP, C_SLOTE:C_SLOTE + EPG * EPG].rearrange("p (e f) -> p e f", f=EPG)
                at_least(dve, S["wslot_set"], q)
                dve.tensor_tensor(wpick[:], wgt, own, ALU.mult).then_inc(S["wpick_set"], 1)
                at_least(dve, S["wpick_set"], q + 1)
                at_least(dve, S["ya_set"], 2 * (q - 1))
                at_least(dve, S["yv_set"], 2 * (q - 1))
                dve.tensor_reduce(wslot[h][:], wpick[:], AX.X, ALU.add).then_inc(S["wslot_set"], 1)

            def act0_mul(i, h):
                q = 2 * i + h
                for u in range(2):
                    at_least(dve, S["silu0_set"], 2 * q + u + 1)
                    at_least(dve, S["y_mm"], 2 * (q - 1) + u + 1)
                    src = banks[2 + u][0:INTER0, 0:2 * 2 * CAP].rearrange("i (e s c) -> i e s c", e=2, s=2)
                    dve.tensor_tensor(act0[:, 2 * u:2 * u + 2, :], silu0[:, 2 * u:2 * u + 2, :], src[:, :, 1, :],
                                      ALU.mult).then_inc(S["act0_set"], 1)

            def y0(i, h):
                q = 2 * i + h
                at_least(dve, S["y_mm"], 2 * q + 1)
                at_least(dve, S["wslot_set"], q + 1)
                for c in range(2):
                    at_least(dve, S[f"scatter{c}"], 16 * (EPG // 2) * (q - 1))
                for e in range(2):
                    dve.tensor_scalar(y[h][:, e, :], banks[4 + 2 * h][0:CAP, D * e:D * e + D], wslot[h][:, e:e + 1],
                                      None, ALU.mult).then_inc(S["yv_set"], 1)

            def experts(i, h, i1, h1, first=False, last=False):
                if not last:
                    x0_T(i1, h1)
                if not first:
                    y0(i, h)
                if not last:
                    act0_mul(i1, h1)

            experts(-1, 1, 0, 0, first=True)
            experts(0, 0, 0, 1)
            experts(0, 1, 1, 0)
            with dve.Fori(1, QG // 2 - 1) as i:
                experts(i, 0, i, 1)
                experts(i, 1, i + 1, 0)
            experts(QG // 2 - 1, 0, QG // 2 - 1, 1)
            experts(QG // 2 - 1, 1, QG // 2, 0, last=True)

            def a1_stat(b):
                hold(dve, S["x2_set"], b + 1)
                for j in range(ST):
                    dve.bn_stats(stat6[:, j, :], x_all[:, ST * b + j, :]).then_inc(S["stat_a"], 1)
                hold(dve, S["stat_a"], 2 * (BATCH + b) + 2)
                hold(dve, S["rstd_a_set"], BATCH + b)
                for j in range(ST):
                    dve.bn_aggr(mv_a[:, j, :], stat6[:, j, :]).then_inc(S["mv_a_set"], 1)

            def b1_max(b, u):
                at_least(dve, S["s1_mm"], 4 * b + u + 1)
                src = banks[1 + u % 2][:, :].rearrange("p (h c) -> p h c", c=CTX)
                dve.tensor_reduce(great[:, u, :], src, AX.X, ALU.max).then_inc(S["great_set"], 1)
                at_least(dve, S["great_set"], 4 * b + u + 1)
                at_least(dve, S["soft_T"], 4 * (b - 1) + u + 1)
                dve.tensor_tensor(soft[:, u, :].rearrange("p (h c) -> p h c", c=CTX), src,
                                  great[:, u, :, None].broadcast_to([P, 8, CTX]), ALU.subtract).then_inc(S["sub_set"], 1)

            def b1_att(b, j):
                at_least(dve, S["pv_mm"], ST * (BATCH + b) + j + 1)
                at_least(dve, S["att_T"], BATCH + b)
                src = banks[4][:, 0:HEADS * VW].rearrange("p (h v) -> p h v", v=VW)
                r = rden[:, j].rearrange("p r a -> p (r a)")
                dve.reciprocal(r, src[:, :, DH]).then_inc(S["rden_set"], 1)
                at_least(dve, S["rden_set"], ST * (BATCH + b) + j + 1)
                dve.tensor_tensor(att[:, j, :].rearrange("p (h d) -> p h d", d=DH), src[:, :, 0:DH],
                                  r[:, :, None].broadcast_to([P, HEADS, DH]), ALU.mult).then_inc(S["att_set"], 1)

            def b1_x3(b):
                at_least(dve, S["o_mm"], BATCH + b + 1)
                x = x_all[:, bass.ds(ST * b, ST), :]
                dve.tensor_tensor(x, x, banks[0][:, :].rearrange("p (j d) -> p j d", d=D), ALU.add)\
                    .then_inc(S["x3_set"], 1)
                hold(dve, S["x3_set"], b + 1)
                for j in range(ST):
                    dve.bn_stats(stat6[:, j, :], x_all[:, ST * b + j, :]).then_inc(S["stat_h"], 1)
                hold(dve, S["stat_h"], 2 * (BATCH + b) + 2)
                for j in range(ST):
                    dve.bn_aggr(mv_h[:, j, :], stat6[:, j, :]).then_inc(S["mv_h_set"], 1)

            def b1_h(b):
                at_least(dve, S["rstd_h_set"], BATCH + b + 1)
                at_least(dve, S["h1_T"], b)
                for j in range(ST):
                    dve.tensor_scalar(h_rows[:, j, :], x_all[:, ST * b + j, :], mv_h[:, j, 0:1], rstd_h[:, j:j + 1],
                                      ALU.subtract, ALU.mult).then_inc(S["h_set"], 1)

            def c1_top(b):
                at_least(dve, S["l1_mm"], b + 1)
                dve.tensor_copy(logit1[:].rearrange("p j e -> p (j e)"), banks[6][:, 0:ST * E1])\
                    .then_inc(S["logit1_set"], 1)
                hold(dve, S["logit1_set"], b + 1)
                for j in range(ST):
                    dve.max(top1[:, j, :], logit1[:, j, :]).then_inc(S["top1_set"], 1)
                hold(dve, S["top1_set"], 2 * b + 2)
                for j in range(ST):
                    dve.max_index(index1[:, j, :], top1[:, j, :], logit1[:, j, :]).then_inc(S["index1_set"], 1)
                dve.tensor_tensor(gap[:], top1[:, :, 1], top1[:, :, 0], ALU.subtract).then_inc(S["gap_set"], 1)
                at_least(dve, S["index1_set"], 2 * b + 2)
                for n in range(2):
                    dve.tensor_tensor(chosen[:, n], index1[:, :, n:n + 1].broadcast_to([P, ST, E1]),
                                      cst[:, None, C_E8:C_E8 + E1].broadcast_to([P, ST, E1]), ALU.is_equal)\
                        .then_inc(S["chosen_set"], 1)

            def c1_share(b):
                at_least(dve, S["egap_set"], b + 1)
                dve.tensor_scalar(wsum[:], egap[:], 1.0, None, ALU.add).then_inc(S["wsum_set"], 1)
                at_least(dve, S["wsum_set"], b + 1)
                dve.reciprocal(wpair[:, 0, :], wsum[:]).then_inc(S["w0_set"], 1)
                at_least(dve, S["w0_set"], b + 1)
                dve.tensor_tensor(wpair[:, 1, :], wpair[:, 0, :], egap[:], ALU.mult).then_inc(S["w1_set"], 1)
                at_least(dve, S["w1_set"], b + 1)
                at_least(dve, S["chosen_set"], 2 * b + 2)
                for n in range(2):
                    dve.tensor_tensor(chosen_w[:, n], chosen[:, n], wpair[:, n, :, None].broadcast_to([P, ST, E1]),
                                      ALU.mult).then_inc(S["chosen_w_set"], 1)
                at_least(dve, S["chosen_w_set"], 2 * b + 2)
                at_least(dve, S["share_T"], b)
                dve.tensor_tensor(share_c[:], chosen_w[:, 0], chosen_w[:, 1], ALU.add).then_inc(S["share_set"], 1)

            def a1_norm(b):
                at_least(dve, S["rstd_a_set"], BATCH + b + 1)
                at_least(dve, S["hs_T"], BATCH + b)
                for j in range(ST):
                    ins = dve.tensor_scalar(hs[:, j, :], x_all[:, ST * b + j, :], mv_a[:, j, 0:1], rstd_a[:, j:j + 1],
                                            ALU.subtract, ALU.mult)
                ins.then_inc(S["hs_set"], 1)

            def d1_mul(b, e):
                at_least(dve, S["silu1_set"], E1 * b + e + 1)
                at_least(dve, S["act1w_set"], E1 * b + e - 1)
                dve.tensor_tensor(act1[e % 2][:], silu1[e % 2][:], banks[5 + e % 2][:, SEQ:2 * SEQ], ALU.mult)\
                    .then_inc(S["act1_set"], 1)

            def d1_out(b):
                at_least(dve, S["down1_mm"], E1 * b + E1)
                at_least(dve, S["o_out"], 16 * b)
                dve.tensor_tensor(o_rows[:], banks[7][:, :].rearrange("p (j d) -> p j d", d=D),
                                  x_all[:, bass.ds(ST * b, ST), :], ALU.add).then_inc(S["o_set"], 1)

            def layer1(b, a_=True, b_=True, d_=True):
                if d_:
                    c1_top(b - 1)
                if b_:
                    b1_max(b, 0)
                if a_:
                    a1_stat(b + 1)
                if b_:
                    b1_max(b, 1)
                if d_:
                    c1_share(b - 1)
                if a_:
                    a1_norm(b + 1)
                if b_:
                    b1_max(b, 2)
                    b1_max(b, 3)
                if d_:
                    d1_mul(b - 1, 0)
                if b_:
                    b1_att(b, 0)
                if d_:
                    d1_mul(b - 1, 1)
                    d1_mul(b - 1, 2)
                if b_:
                    b1_att(b, 1)
                if d_:
                    d1_mul(b - 1, 3)
                    d1_mul(b - 1, 4)
                if b_:
                    b1_x3(b)
                if d_:
                    d1_mul(b - 1, 5)
                if b_:
                    b1_h(b)
                if d_:
                    d1_mul(b - 1, 6)
                    d1_mul(b - 1, 7)
                    d1_out(b - 1)

            layer1(-1, b_=False, d_=False)
            layer1(0, d_=False)
            layer1(1)
            with dve.Fori(2, BATCH - 1) as b:
                layer1(b)
            layer1(BATCH - 1, a_=False)
            layer1(BATCH, a_=False, b_=False)


def laid_out(i):
    def chunks(w):
        return np.ascontiguousarray(w.reshape(-1, P, w.shape[-1]).transpose(1, 0, 2))

    def dup(m):
        return np.ascontiguousarray(np.concatenate([m.T, m.T], 0))
    left, rows = position_bias()
    return {
        "x": i["x"].reshape(TOKENS, D),
        "ctxT": chunks(i["ctx_2048"].reshape(BATCH * CTX, D).T),
        "cst": constants(), "bias_q": left, "bias_k": rows,
        "wk0": chunks(i["L0_xattn_Wk"].T), "wv0": chunks(i["L0_xattn_Wv"].T),
        "wq0": chunks(i["L0_xattn_Wq"].T), "wo0": chunks(i["L0_xattn_Wo"].T),
        "gate0": chunks(i["L0_ffn_gate_weight"].T),
        "wq1": chunks(i["L1_xattn_Wq"]), "wk1": chunks(i["L1_xattn_Wk"]),
        "wv1": chunks(i["L1_xattn_Wv"]), "wo1": chunks(i["L1_xattn_Wo"]),
        "bq0": i["L0_xattn_bq"].reshape(KC, P).T, "bk0": i["L0_xattn_bk"].reshape(KC, P).T,
        "bv0": i["L0_xattn_bv"], "bo0": i["L0_xattn_bo"],
        "gamma": i["L0_xattn_ln_gamma"], "beta": i["L0_xattn_ln_beta"],
        "rs": i["L0_xattn_residual_scale"].reshape(1),
        "o2n": i["L0_ffn_old_to_new"],
        "mask0": dup(i["mask_BxS2_ik0"]), "mask1": i["mask_BxS2_bf1"].view(np.uint8).reshape(1, BATCH * CTX),
        "gu0": np.ascontiguousarray(i["L0_ffn_gate_up_proj"].reshape(QG, EPG, 2 * INTER0, KC, P).transpose(0, 4, 3, 1, 2)),
        "down0": np.ascontiguousarray(i["L0_ffn_down_proj"].reshape(QG, EPG, D, INTER0).transpose(0, 3, 1, 2)),
        "gate1": chunks(i["L1_ffn_router_gate"].T),
        "gu1": np.ascontiguousarray(i["L1_ffn_expert_gate_up"].reshape(E1, KC, P, INTER1, 2).transpose(2, 0, 1, 4, 3)),
        "down1": np.ascontiguousarray(i["L1_ffn_expert_down"].transpose(1, 0, 2)),
    }


def kernel(**inputs):
    from concourse import bacc
    from concourse.bass_utils import run_bass_kernel_spmd

    nc = bacc.Bacc("TRN2", target_bir_lowering=False, num_devices=1)
    arrays = {f"in_{n}": np.ascontiguousarray(a) for n, a in laid_out(inputs).items()}
    t = {n[3:]: nc.dram_tensor(n, a.shape, mybir.dt.from_np(a.dtype), kind="ExternalInput").ap()
         for n, a in arrays.items()}
    out = nc.dram_tensor("out", (TOKENS, D), F32, kind="ExternalOutput").ap()
    build(nc, t, out)
    r = run_bass_kernel_spmd(nc, [arrays], core_ids=[0])
    return r.results[0]["out"].reshape(BATCH, SEQ, D)
```

```python
from contextlib import ExitStack

import concourse.bass as bass
import numpy as np
from concourse import mybir

F32, BF16 = mybir.dt.float32, mybir.dt.bfloat16
I32, U32, U8 = mybir.dt.int32, mybir.dt.uint32, mybir.dt.uint8
ALU = mybir.AluOpType
ACT = mybir.ActivationFunctionType
AX = mybir.AxisListType

P = 128
BATCH, SEQ, D = 8, 256, 256
CTX = 64
HEADS, DH = 16, 16
TOKENS = BATCH * SEQ
KC = D // P
ST = SEQ // P
PAIRS = HEADS // 2
VW = DH + 1
GROUPS = 4
OLD, NEW, TOPK, CAP, INTER0 = 128, 48, 8, 96, 96
EPG = 4
QG = NEW // EPG
ROW = D + NEW
PADROWS = TOKENS + P
E1, INTER1 = 8, 128
EPS = 1e-5
MASKED = -1e30
TAKEN = -3e38
PV_BANK = (3, 7)
SOFT_BANK = (3, 0, 1, 2)

C_ID, C_TRI, C_E48 = 0, 128, 256
C_HEAD2, C_HEAD8, C_SLOTE, C_PAD, C_LOC, C_B256, C_E8 = 304, 306, 314, 330, 331, 333, 341
C_N = 349


def constants():
    c = np.zeros((P, C_N), np.float32)
    p = np.arange(P)
    c[:, C_ID:C_ID + P] = np.eye(P)
    c[:, C_TRI:C_TRI + P] = p[:, None] < p[None, :]
    c[:, C_E48:C_E48 + NEW] = np.arange(NEW)
    c[:, C_HEAD2:C_HEAD2 + 2] = (p[:, None] // DH) % 2 == np.arange(2)
    c[:, C_HEAD8:C_HEAD8 + 8] = p[:, None] // DH == np.arange(8)
    c[:, C_SLOTE:C_SLOTE + EPG * EPG] = np.eye(EPG).reshape(-1)
    c[:, C_PAD] = TOKENS + p
    c[:, C_LOC:C_LOC + ST] = p[:, None] + P * np.arange(ST)
    c[:, C_B256:C_B256 + BATCH] = SEQ * np.arange(BATCH)
    c[:, C_E8:C_E8 + E1] = np.arange(E1)
    return c


def thirds(a):
    bf = mybir.dt.np(BF16)
    out = []
    for _ in range(3):
        out.append(a.astype(bf))
        a = a - out[-1].astype(np.float32)
    return out


def position_bias():
    slope = (np.float32(2.0 ** (-8.0 / HEADS)) ** np.arange(1, HEADS + 1, dtype=np.float32)).astype(np.float32)
    key = slope[:, None] * np.arange(CTX, dtype=np.float32)
    query = np.repeat(-slope[:, None], CTX, 1)
    rows = np.stack(thirds(key) + thirds(query)).reshape(6, HEADS * CTX)
    left = np.ones((7, SEQ), rows.dtype)
    left[4:] = np.arange(SEQ)
    return left, rows


def at_least(eng, sem, value):
    if not isinstance(value, int) or value > 0:
        eng.wait_ge(sem, value)


def build(nc, t, out, dbg=None):
    with ExitStack() as ctx:
        def sb(name, shape, dt=F32):
            return ctx.enter_context(nc.sbuf_tensor(name, shape, dt))

        def sem(name):
            return ctx.enter_context(nc.semaphore(name))

        def hold(eng, s, value):
            if isinstance(value, int):
                if value > 0:
                    eng.wait_ge(s, value)
            else:
                eng.wait_ge(s, value)
                eng.sem_inc(held, 1)

        held = sem("held")
        rows_d = nc.dram_tensor("rows_scratch", (PADROWS, ROW), F32, kind="Internal").ap()
        sums_d = [nc.dram_tensor(f"sum{k}_scratch", (PADROWS, D), F32, kind="Internal").ap() for k in range(2)]
        share_d = nc.dram_tensor("share_scratch", (BATCH, E1, SEQ), F32, kind="Internal").ap()
        out_v = out.rearrange("(b j p) d -> b p j d", j=ST, p=P)
        x_v = t["x"].rearrange("(b j p) d -> b p j d", j=ST, p=P)
        rows_v = rows_d[0:TOKENS, :].rearrange("(b j p) d -> b p j d", j=ST, p=P)
        sums_v = [s[0:TOKENS, :].rearrange("(b j p) d -> b p j d", j=ST, p=P) for s in sums_d]

        x_all = sb("x_all", [P, BATCH * ST, D])
        cst = sb("cst", [P, C_N])
        ident = cst[:, C_ID:C_ID + P]
        half = sb("half", [P, ST])
        cT = sb("cT", [P, KC, BATCH * CTX])
        NV, NK, NW = BATCH * PAIRS * 2 * VW, KC * BATCH * CTX, KC * D
        early = sb("early", [P, NV + NK + 2 * NW])
        v_blk = [early[:, 0:NV].rearrange("p (b r a v) -> p b r a v", b=BATCH, r=PAIRS, a=2),
                 sb("v_blk1", [P, BATCH, PAIRS, 2, VW])[:]]
        kT = [early[:, NV:NV + NK].rearrange("p (k c) -> p k c", k=KC), sb("kT1", [P, KC, BATCH * CTX])[:]]
        wk0, wv0 = (early[:, NV + NK + n * NW:NV + NK + n * NW + NW].rearrange("p (k d) -> p k d", k=KC)
                    for n in range(2))
        wq0, wo0 = (sb(n, [P, KC, D]) for n in ("wq0", "wo0"))
        wq1, wo1, wk1 = (sb(n, [P, KC, D]) for n in ("wq1", "wo1", "wk1"))
        wk1n, wv1 = (sb(n, [P, KC, GROUPS * DH]) for n in ("wk1n", "wv1"))
        gate0 = sb("gate0", [P, KC, OLD])
        bq0, bk0 = sb("bq0", [P, KC]), sb("bk0", [P, KC])
        bv0, bo0, gamma, beta = (sb(n, [P, D]) for n in ("bv0", "bo0", "gamma", "beta"))
        cdup = sb("cdup", [P, KC, BATCH, 2, CTX])
        mask_i = sb("mask_i", [P, BATCH], I32)
        hi = sb("hi", [P, BATCH])
        lo = sb("lo", [P, 1])
        rs = sb("rs", [P, 1])
        rs2 = sb("rs2", [P, 1])
        o2n_c, o2n_r = sb("o2n_c", [P, 1], I32), sb("o2n_r", [P, OLD], I32)
        o2n_f = sb("o2n_f", [P, 1])
        unkept = sb("unkept", [P, OLD])
        map_f, map_b = sb("map_f", [P, NEW]), sb("map_b", [P, NEW], BF16)
        tri, ones_b, ident_b = (sb(n, [P, P], BF16) for n in ("tri", "ones_b", "ident_b"))
        place = sb("place", [P, QG, CAP, EPG], BF16)
        loc1 = sb("loc1", [P, ST, 2], BF16)
        stat6, stat6_d, stat6_h = (sb(n, [P, ST, 6]) for n in ("stat6", "stat6_d", "stat6_h"))
        mv_a, mv_d, mv_h = (sb(n, [P, ST, 2]) for n in ("mv_a", "mv_d", "mv_h"))
        rstd_a, rstd_d, rstd_h = (sb(n, [P, ST]) for n in ("rstd_a", "rstd_d", "rstd_h"))
        ve_a, ve_d, ve_h = (sb(n, [P, ST]) for n in ("ve_a", "ve_d", "ve_h"))
        hs = sb("hs", [P, ST, D])
        hsT = sb("hsT", [P, KC, SEQ])
        qT = sb("qT", [P, KC, SEQ])
        k_blk = sb("k_blk", [P, KC, 2, CTX])
        xbeta = sb("xbeta", [P, ST, D])
        prob = sb("prob", [P, 4, KC, SEQ])
        rden = sb("rden", [P, ST, PAIRS, 2])
        att = sb("att", [P, ST, D])
        attT = sb("attT", [P, KC, SEQ])
        delta = sb("delta", [P, ST, D])
        dgam = sb("dgam", [P, ST, D])
        h_rows = sb("h_rows", [P, ST, D])
        hT = sb("hT", [P, KC, SEQ])
        logit = sb("logit", [P, ST, OLD])
        top = sb("top", [P, ST, TOPK])
        ntop = sb("ntop", [P, ST])
        etop = sb("etop", [P, ST, TOPK])
        den = sb("den", [P, ST])
        rdn = sb("rdn", [P, ST])
        left = sb("left", [P, ST, OLD])
        sel = sb("sel", [P, ST, OLD], BF16)
        selsum = sb("selsum", [P, OLD], BF16)
        selboth = sb("selboth", [P, OLD], BF16)
        expl = sb("expl", [P, ST, OLD])
        wsel = sb("wsel", [P, ST, OLD])
        countT = sb("countT", [P, ST, P], BF16)
        wselT = sb("wselT", [P, ST, P])
        w_rows = sb("w_rows", [P, ST, NEW])
        off = sb("off", [P, ST, NEW])
        pos = sb("pos", [P, ST, NEW], BF16)
        hit = sb("hit", [P, ST, QG, CAP, EPG], BF16)
        slots = sb("slots", [CAP, NEW, 2])
        slot_b = sb("slot_b", [CAP, NEW])
        empty = sb("empty", [CAP, NEW])
        slot_f = sb("slot_f", [CAP, NEW])
        slot_i = sb("slot_i", [CAP, NEW], U32)
        zrow = sb("zrow", [P, ROW])
        take = [sb(f"take{h}", [CAP, EPG], U32) for h in range(2)]
        give = [sb(f"give{h}", [CAP, EPG], U32) for h in range(2)]
        xb = [sb(f"xb{h}", [CAP, EPG, ROW]) for h in range(2)]
        NG, ND = KC * EPG * 2 * INTER0, EPG * D
        late = sb("late", [P, max(2 * NG + 2 * ND, BATCH * ST * D + E1 * SEQ)])
        gu0 = [late[:, h * NG:h * NG + NG].rearrange("p (k e o) -> p k e o", k=KC, e=EPG) for h in range(2)]
        down0 = [late[0:INTER0, 2 * NG + h * ND:2 * NG + h * ND + ND].rearrange("p (e d) -> p e d", e=EPG)
                 for h in range(2)]
        y = [sb(f"y{h}", [CAP, EPG, D]) for h in range(2)]
        wpick = sb("wpick", [CAP, EPG, EPG])
        wslot = [sb(f"wslot{h}", [CAP, EPG]) for h in range(2)]
        xbT = sb("xbT", [P, KC, EPG * CAP])
        silu0 = sb("silu0", [INTER0, EPG, CAP])
        act0 = sb("act0", [INTER0, EPG, CAP])
        x_add = late[:, 0:BATCH * ST * D].rearrange("p (n d) -> p n d", d=D)
        share = late[:, BATCH * ST * D:BATCH * ST * D + E1 * SEQ].rearrange("p (e s) -> p e s", e=E1)
        gu1 = hit[:].rearrange("p j q c e -> p (j q c e)").bitcast(F32)[:, 0:E1 * KC * 2 * INTER1]\
            .rearrange("p (e k s i) -> p e k s i", e=E1, k=KC, s=2)
        down1 = place[:].rearrange("p q c e -> p (q c e)").bitcast(F32)[:, 0:E1 * D].rearrange("p (e d) -> p e d", e=E1)
        gate1 = sb("gate1", [P, KC, E1])
        bias_k = early[:, 0:BATCH * HEADS * CTX // 2].bitcast(BF16)[0:7].rearrange("p (b c) -> p b c", b=BATCH)
        bias_q = sb("bias_q", [7, SEQ], BF16)
        mask_u = sb("mask_u", [1, BATCH * CTX], U8)
        mask_b = sb("mask_b", [1, BATCH, 1, CTX], BF16)
        k1_blk = sb("k1_blk", [P, KC, 8, CTX])
        great = sb("great", [P, 4, 8])
        soft = prob[:].rearrange("p j m s -> p j (m s)")
        softT = cdup[:].rearrange("p k b a c -> p (k b a c)").rearrange("p (u c) -> p u c", u=4)
        hT1 = sb("hT1", [P, KC, SEQ])
        hTr = hT
        logit1 = sb("logit1", [P, ST, E1])
        top1, index1 = sb("top1", [P, ST, 8]), sb("index1", [P, ST, 8], U32)
        gap, egap, wsum = (sb(n, [P, ST]) for n in ("gap", "egap", "wsum"))
        wpair = sb("wpair", [P, 2, ST])
        chosen = sb("chosen", [P, 2, ST, E1])
        chosen_w = sb("chosen_w", [P, 2, ST, E1])
        share_c = sb("share_c", [P, ST, E1])
        shareT = sb("shareT", [E1, SEQ])
        silu1 = [sb(f"silu1_{h}", [P, SEQ]) for h in range(2)]
        act1 = [sb(f"act1_{h}", [P, SEQ]) for h in range(2)]
        act1w = [sb(f"act1w_{h}", [P, SEQ]) for h in range(2)]
        o_rows = delta

        banks = [ctx.enter_context(nc.psum_tensor(f"bank{k}", [P, 512], F32)) for k in range(8)]

        S = {}
        for n in ("ctx_in", "cst_in", "kv_w_in", "q_w_in", "bias_in", "route_in", "l1_w_in", "x_in", "zero_out",
                  "half_set", "wk1_set", "cdup_set", "vblk_zero", "vblk_ones", "hi_set", "bound_set", "rs_set",
                  "map_set", "tri_set", "place_set", "loc_set",
                  "kT_mm", "kT_set", "v_mm", "v_set",
                  "stat_a", "mv_a_set", "ve_a_set", "rstd_a_set", "hs_set", "hs_T", "hsT_set", "q_mm", "q_set",
                  "k_set", "xbeta_set",
                  "s_mm", "exp_set", "clip_set", "pv_mm", "rden_set", "att_set", "att_T", "attT_set", "o_mm",
                  "delta_set", "stat_d", "mv_d_set", "ve_d_set", "pow_d_set", "rstd_d_set", "dgam_set", "x1_set",
                  "stat_h", "mv_h_set", "ve_h_set", "rstd_h_set", "h_set", "x1_out", "h_out", "w_out",
                  "h_T", "hT_set", "l_mm", "logit_set", "top_set", "ntop_set", "left_set", "sel_set", "expl_set",
                  "etop_set", "den_set", "wsel_set", "count_mm", "wsel_T", "countT_set", "wselT_set", "pos_mm",
                  "w_set", "off_set", "pos_set", "hit_set", "slot_mm", "slot_acc", "slotb_acc", "selsum_set", "route_done",
                  "w0_ld0", "w0_ld1", "take_set", "give_set", "gather0", "gather1", "scatter0", "scatter1",
                  "xb_T", "xbT_set", "wpick_set", "wslot_set", "gu0_mm", "silu0_set", "act0_set", "y_mm", "yv_set", "ya_set",
                  "gate1_in", "bias_q_in", "bias1_in", "mask_u_in", "mask_b_set", "e1_w_in",
                  "sum_in0", "sum_in1", "x2_set", "k1_set",
                  "s1_mm", "great_set", "sub_set", "soft_set", "soft_T", "softT_set", "x3_set",
                  "h1_T", "hT1_set", "hTr_set", "l1_mm", "logit1_set", "top1_set", "index1_set", "gap_set", "egap_set", "wsum_set",
                  "w0_set", "w1_set", "chosen_set", "chosen_w_set", "share_set", "share_T", "shareT_set",
                  "share_out", "share_in", "gu1_mm", "silu1_set", "act1_set", "act1w_set", "down1_mm", "o_set", "o_out"):
            S[n] = sem(n)
        block = ctx.enter_context(nc.Block())

        @block.sync
        def _(sp):
            sp.dma_start(cT[:], t["ctxT"]).then_inc(S["ctx_in"], 16)
            sp.dma_start(wk0[:], t["wk0"]).then_inc(S["kv_w_in"], 16)
            sp.dma_start(wv0[:], t["wv0"]).then_inc(S["kv_w_in"], 16)
            sp.dma_start(cst[:], t["cst"]).then_inc(S["cst_in"], 16)
            for n, v in ((wq0, "wq0"), (wo0, "wo0"), (gate0, "gate0")):
                sp.dma_start(n[:], t[v]).then_inc(S["q_w_in"], 16)
            with sp.Fori(0, BATCH) as b:
                sp.dma_start(x_all[:, bass.ds(ST * b, ST), :], x_v[b]).then_inc(S["x_in"], 16)
                sp.wait_ge(S["x_in"], 16 * b + 16)
                sp.sem_inc(held, 1)
            for n, v in ((wq1, "wq1"), (wk1n, "wk1"), (wv1, "wv1"), (wo1, "wo1")):
                sp.dma_start(n[:], t[v]).then_inc(S["l1_w_in"], 16)
            sp.wait_ge(S["place_set"], 2)
            sp.dma_start(rows_d[TOKENS:PADROWS, :], zrow[:]).then_inc(S["zero_out"], 16)
            for k in range(2):
                sp.dma_start(sums_d[k][TOKENS:PADROWS, :], zrow[:, 0:D]).then_inc(S["zero_out"], 16)
            for k in range(TOKENS // P):
                sp.dma_start(sums_d[1][P * k:P * k + P, :], zrow[:, 0:D]).then_inc(S["zero_out"], 16)

            def store_x1(b):
                at_least(sp, S["x1_set"], 2 * b + 2)
                sp.dma_start(sums_v[0][b], x_all[:, bass.ds(ST * b, ST), :]).then_inc(S["x1_out"], 16)
                at_least(sp, S["h_set"], 2 * b + 2)
                sp.dma_start(rows_v[b][:, :, 0:D], h_rows[:]).then_inc(S["h_out"], 16)

            def store_w(b):
                at_least(sp, S["w_set"], 2 * b + 2)
                sp.dma_start(rows_v[b][:, :, D:ROW], w_rows[:]).then_inc(S["w_out"], 16)


            def load_w0(i, h):
                q = 2 * i + h
                at_least(sp, S["gu0_mm"], 2 * (q - 1))
                sp.dma_start(gu0[h][:], t["gu0"][q]).then_inc(S[f"w0_ld{h}"], 16)
                at_least(sp, S["y_mm"], 2 * (q - 1))
                sp.dma_start(down0[h][:], t["down0"][q]).then_inc(S[f"w0_ld{h}"], 16)

            load_w0(0, 0)
            load_w0(0, 1)
            store_x1(0)
            with sp.Fori(0, BATCH - 1) as i:
                store_x1(i + 1)
                store_w(i)
            store_w(BATCH - 1)

            sp.wait_ge(S["route_done"], 1)
            sp.wait_ge(S["slot_mm"], ST * BATCH)
            sp.wait_ge(S["pv_mm"], 2 * BATCH)
            sp.dma_start(gu1, t["gu1"]).then_inc(S["e1_w_in"], 16)
            sp.dma_start(down1, t["down1"]).then_inc(S["e1_w_in"], 16)
            for b in range(BATCH):
                sp.dma_start(bias_k[1:7, b, :], t["bias_k"]).then_inc(S["bias1_in"], 16)
            sp.wait_ge(S["mask_b_set"], 1)
            for b in range(BATCH):
                sp.dma_start(bias_k[0:1, b].rearrange("p (h c) -> p h c", c=CTX),
                             mask_b[:, b].broadcast_to([1, HEADS, CTX])).then_inc(S["bias1_in"], 16)
            with sp.Fori(1, QG // 2) as i:
                for h in range(2):
                    load_w0(i, h)

            sp.wait_ge(S["scatter0"], 16 * NEW // 2)
            sp.wait_ge(S["scatter1"], 16 * NEW // 2)
            sp.wait_ge(S["y_mm"], 2 * QG)

            def load_x(b):
                sp.dma_start(x_all[:, bass.ds(ST * b, ST), :], sums_v[0][b]).then_inc(S["sum_in0"], 16)
                sp.dma_start(x_add[:, bass.ds(ST * b, ST), :], sums_v[1][b]).then_inc(S["sum_in1"], 16)
                hold(sp, S["sum_in0"], 16 * b + 16)
                hold(sp, S["sum_in1"], 16 * b + 16)

            def share_send(b):
                at_least(sp, S["shareT_set"], b + 1)
                sp.dma_start(share_d[b], shareT[:]).then_inc(S["share_out"], 16)

            def share_take(b):
                hold(sp, S["share_out"], 16 * b + 16)
                hold(sp, S["act1w_set"], E1 * b)
                sp.dma_start(share, share_d[b].partition_broadcast(P)).then_inc(S["share_in"], 16)

            def store(b):
                at_least(sp, S["o_set"], b + 1)
                sp.dma_start(out_v[b], o_rows[:]).then_inc(S["o_out"], 16)

            with sp.Fori(0, BATCH) as b:
                load_x(b)
            for b in range(2):
                share_send(b)
                share_take(b)
            with sp.Fori(2, BATCH) as b:
                store(b - 2)
                share_send(b)
                share_take(b)
            for b in range(BATCH - 2, BATCH):
                store(b)
            sp.wait_ge(S["o_out"], 16 * BATCH)
            sp.wait_ge(S["share_out"], 16 * BATCH)
            if dbg is not None:
                sp.dma_start(dbg["slot"], slot_f[:]).then_inc(S["cst_in"], 16)
                sp.dma_start(dbg["rows"], rows_d).then_inc(S["cst_in"], 16)
                for k in range(2):
                    sp.dma_start(dbg["sum%d" % k], sums_d[k]).then_inc(S["cst_in"], 16)
                sp.wait_ge(S["cst_in"], 80)

        @block.gpsimd
        def _(pool):
            pool.memset(half[:], -0.5).then_inc(S["half_set"], 1)
            pool.memset(zrow[:], 0.0).then_inc(S["place_set"], 1)
            pool.memset(lo[:], float(np.exp(-50.0))).then_inc(S["half_set"], 1)
            pool.wait_ge(S["ctx_in"], 16)
            cv = cT[:].rearrange("p k (b c) -> p (k b) c", c=CTX)
            dv = cdup[:].rearrange("p k b a c -> p (k b) a c")
            for a in range(2):
                pool.tensor_copy(dv[:, :, a, :], cv).then_inc(S["cdup_set"], 1)
            for v in v_blk:
                pool.memset(v[:], 0.0).then_inc(S["vblk_zero"], 1)
            pool.iota(place[:], [[0, QG], [1, CAP], [0, EPG]], base=0, channel_multiplier=0,
                      allow_small_or_imprecise_dtypes=True).then_inc(S["place_set"], 1)
            pool.memset(slots[:], 0.0).then_inc(S["place_set"], 1)
            pool.memset(slot_b[:], 0.0).then_inc(S["place_set"], 1)
            pool.memset(selsum[:], 0.0).then_inc(S["place_set"], 1)
            pool.memset(ones_b[:], 1.0).then_inc(S["place_set"], 1)
            pool.wait_ge(S["l1_w_in"], 64)
            wn = wk1n[:].rearrange("p k (g d) -> p (k g) d", d=DH)
            we = wk1[:].rearrange("p k (g h d) -> p (k g) h d", g=GROUPS, d=DH)
            for h in range(HEADS // GROUPS):
                pool.tensor_copy(we[:, :, h, :], wn).then_inc(S["wk1_set"], 1)

            def rstd(b, mv_set, mv, ve, ve_set, out_, out_set):
                hold(pool, mv_set, 2 * b + 2)
                pool.tensor_scalar(ve[:], mv[:, :, 1], EPS, None, ALU.add).then_inc(ve_set, 1)
                at_least(pool, ve_set, b + 1)
                pool.tensor_tensor(out_[:], ve[:], half[:], ALU.pow).then_inc(out_set, 1)

            def a_rstd(b):
                rstd(b, S["mv_a_set"], mv_a, ve_a, S["ve_a_set"], rstd_a, S["rstd_a_set"])

            def a_keys(b):
                hold(pool, S["s_mm"], 8 * b)
                src = kT[0].rearrange("p m (b c) -> p m b c", c=CTX)
                for a in range(2):
                    head = cst[:, C_HEAD2 + a:C_HEAD2 + a + 1, None].broadcast_to([P, KC, CTX])
                    pool.tensor_tensor(k_blk[:, :, a, :], src[:, :, b, :], head, ALU.mult).then_inc(S["k_set"], 1)

            def b_beta(b):
                hold(pool, S["x1_set"], 2 * b)
                for j in range(ST):
                    pool.tensor_tensor(xbeta[:, j, :], x_all[:, ST * b + j, :], beta[:], ALU.add)\
                        .then_inc(S["xbeta_set"], 1)

            def b_rstd(b):
                hold(pool, S["mv_d_set"], 2 * b + 2)
                pool.tensor_scalar(ve_d[:], mv_d[:, :, 1], rs2[:, 0:1], EPS, ALU.mult, ALU.add)\
                    .then_inc(S["ve_d_set"], 1)
                at_least(pool, S["ve_d_set"], b + 1)
                pool.tensor_tensor(ve_d[:], ve_d[:], half[:], ALU.pow).then_inc(S["pow_d_set"], 1)
                hold(pool, S["pow_d_set"], b + 1)
                pool.tensor_scalar(rstd_d[:], ve_d[:], rs[:, 0:1], None, ALU.mult).then_inc(S["rstd_d_set"], 1)

            def b_rstd2(b):
                rstd(b, S["mv_h_set"], mv_h, ve_h, S["ve_h_set"], rstd_h, S["rstd_h_set"])

            def body(b, stages=range(5)):
                if 2 in stages:
                    b_rstd2(b - 2)
                if 0 in stages:
                    a_rstd(b)
                    a_keys(b)
                if 1 in stages:
                    b_beta(b - 1)
                    b_rstd(b - 1)

            pool.wait_ge(S["kT_set"], 2)
            pool.wait_ge(S["rs_set"], 2)
            pool.wait_ge(S["half_set"], 2)
            for b in range(0, 5):
                body(b, range(b + 1))
            with pool.Fori(5, BATCH) as b:
                body(b)
            for b in range(BATCH, BATCH + 4):
                body(b, range(b - BATCH + 1, 5))

            def group(tab, q):
                return tab[:, EPG * q:EPG * q + EPG] if isinstance(q, int) else tab[:, bass.ds(EPG * q, EPG)]

            def fetch(i, h):
                q = 2 * i + h
                hold(pool, S["xb_T"], q - 1)
                hold(pool, S["wpick_set"], q - 1)
                pool.tensor_copy(take[h][:], group(slot_i, q)).then_inc(S["take_set"], 1)
                hold(pool, S["take_set"], q + 1)
                for e in range(EPG):
                    pool.indirect_dma_start(xb[h][:, e, :], None, rows_d,
                                            bass.IndirectOffsetOnAxis(ap=take[h][:, e:e + 1], axis=0))\
                        .then_inc(S[f"gather{h}"], 16)

            def add(i, h):
                q = 2 * i + h
                for c in range(2):
                    hold(pool, S[f"scatter{c}"], 16 * (EPG // 2) * q)
                pool.tensor_copy(give[h][:], group(slot_i, q)).then_inc(S["give_set"], 1)
                hold(pool, S["give_set"], q + 1)
                for n, e in enumerate((0, 2, 1, 3)):
                    c = n % 2
                    hold(pool, S["yv_set" if e < 2 else "ya_set"], 2 * q + e % 2 + 1)
                    hold(pool, S[f"scatter{c}"], 16 * ((EPG // 2) * q + n // 2))
                    pool.indirect_dma_start(sums_d[c], bass.IndirectOffsetOnAxis(ap=give[h][:, e:e + 1], axis=0),
                                            y[h][:, e, :], None, compute_op=ALU.add).then_inc(S[f"scatter{c}"], 16)

            pool.wait_ge(S["route_done"], 1)
            pool.wait_ge(S["x1_out"], 16 * BATCH)
            pool.wait_ge(S["h_out"], 16 * BATCH)
            pool.wait_ge(S["w_out"], 16 * BATCH)
            pool.wait_ge(S["zero_out"], 16 * (3 + TOKENS // P))
            for i, h in ((-1, 0), (-1, 1), (0, 0), (0, 1)):
                fetch(i + 1, h)
                if i >= 0:
                    add(i, h)
            with pool.Fori(1, QG // 2 - 1) as i:
                for h in range(2):
                    fetch(i + 1, h)
                    add(i, h)
            for h in range(2):
                add(QG // 2 - 1, h)

            def a1_x(b):
                hold(pool, S["sum_in0"], 16 * b + 16)
                hold(pool, S["sum_in1"], 16 * b + 16)
                x = x_all[:, bass.ds(ST * b, ST), :]
                pool.tensor_tensor(x, x, x_add[:, bass.ds(ST * b, ST), :], ALU.add).then_inc(S["x2_set"], 1)

            def a1_keys(b):
                hold(pool, S["s1_mm"], 4 * b)
                src = kT[1].rearrange("p m (b c) -> p m b c", c=CTX)
                for m in range(KC):
                    pool.tensor_tensor(k1_blk[:, m], src[:, m, b, None, :].broadcast_to([P, 8, CTX]),
                                       cst[:, C_HEAD8:C_HEAD8 + 8, None].broadcast_to([P, 8, CTX]), ALU.mult)\
                        .then_inc(S["k1_set"], 1)

            def a1_rstd(b):
                rstd(BATCH + b, S["mv_a_set"], mv_a, ve_a, S["ve_a_set"], rstd_a, S["rstd_a_set"])

            def b1_rstd(b):
                rstd(BATCH + b, S["mv_h_set"], mv_h, ve_h, S["ve_h_set"], rstd_h, S["rstd_h_set"])

            def d1_share(b, e):
                if e == 0:
                    hold(pool, S["share_in"], 16 * b + 16)
                hold(pool, S["act1_set"], E1 * b + e + 1)
                hold(pool, S["down1_mm"], E1 * b + e - 1)
                pool.tensor_tensor(act1w[e % 2][:], act1[e % 2][:], share[:, e, :], ALU.mult).then_inc(S["act1w_set"], 1)

            def layer1(b, stages=range(5)):
                if 0 in stages:
                    a1_keys(b)
                    a1_x(b)
                if 3 in stages:
                    for e in range(5):
                        d1_share(b - 3, e)
                if 0 in stages:
                    a1_rstd(b)
                if 3 in stages:
                    d1_share(b - 3, 5)
                if 1 in stages:
                    b1_rstd(b - 1)
                if 3 in stages:
                    d1_share(b - 3, 6)
                    d1_share(b - 3, 7)

            pool.wait_ge(S["kT_set"], 4)
            for b in range(0, 5):
                layer1(b, range(b + 1))
            with pool.Fori(5, BATCH) as b:
                layer1(b)
            for b in range(BATCH, BATCH + 4):
                layer1(b, range(b - BATCH + 1, 5))

        @block.scalar
        def _(act):
            for n, v in ((bq0, "bq0"), (bk0, "bk0"), (mask_i, "mask0")):
                act.dma_start(n[:], t[v]).then_inc(S["bias_in"], 16)
            for n, v in ((bv0, "bv0"), (bo0, "bo0"), (gamma, "gamma"), (beta, "beta"), (rs, "rs")):
                act.dma_start(n[:], t[v].partition_broadcast(P)).then_inc(S["bias_in"], 16)
            act.dma_start(o2n_c[:], t["o2n"].rearrange("(p o) -> p o", o=1)).then_inc(S["route_in"], 16)
            act.dma_start(o2n_r[:], t["o2n"].partition_broadcast(P)).then_inc(S["route_in"], 16)
            act.dma_start(mask_u[:], t["mask1"]).then_inc(S["mask_u_in"], 16)
            act.dma_start(bias_q[:], t["bias_q"]).then_inc(S["bias_q_in"], 16)
            act.dma_start(gate1[:], t["gate1"]).then_inc(S["gate1_in"], 16)
            act.wait_ge(S["hi_set"], 1)
            act.activation(hi[:], hi[:], ACT.Exp).then_inc(S["bound_set"], 1)

            def c_hT(b):
                at_least(act, S["h_T"], b + 1)
                at_least(act, S["l_mm"], b)
                act.activation(hT[:].rearrange("p k s -> p (k s)"), banks[6][:, :], ACT.Copy).then_inc(S["hT_set"], 1)

            def b_exp(b, j):
                at_least(act, S["s_mm"], 8 * b + 2 * j + 2)
                at_least(act, S["pv_mm"], 2 * b)
                act.activation(prob[:, j].rearrange("p m s -> p (m s)"), banks[1 + j % 2][:, :], ACT.Exp,
                               scale=DH ** -0.5).then_inc(S["exp_set"], 1)

            def a_hsT(b):
                at_least(act, S["hs_T"], b + 1)
                at_least(act, S["q_mm"], b)
                act.activation(hsT[:].rearrange("p k s -> p (k s)"), banks[0][:, :], ACT.Copy)\
                    .then_inc(S["hsT_set"], 1)

            def a_q(b):
                at_least(act, S["q_mm"], b + 1)
                at_least(act, S["s_mm"], 8 * b)
                for m in range(KC):
                    act.activation(qT[:, m, :], banks[0][:, SEQ * m:SEQ * m + SEQ], ACT.Identity,
                                   bias=bq0[:, m:m + 1]).then_inc(S["q_set"], 1)

            def c_exp(b):
                at_least(act, S["ntop_set"], b + 1)
                at_least(act, S["wsel_set"], 2 * b)
                for j in range(ST):
                    act.activation(expl[:, j, :], logit[:, j, :], ACT.Exp, bias=ntop[:, j:j + 1])\
                        .then_inc(S["expl_set"], 1)
                    act.activation(etop[:, j, :], top[:, j, :], ACT.Exp, bias=ntop[:, j:j + 1],
                                   accum_out=den[:, j:j + 1]).then_inc(S["etop_set"], 1)

            def b_attT(b):
                at_least(act, S["att_T"], b + 1)
                at_least(act, S["o_mm"], b)
                act.activation(attT[:].rearrange("p k s -> p (k s)"), banks[5][:, :], ACT.Copy)\
                    .then_inc(S["attT_set"], 1)

            def c_wT(b):
                at_least(act, S["countT_set"], b + 1)
                at_least(act, S["pos_mm"], b)
                act.activation(wselT[:].rearrange("p j s -> p (j s)"), banks[6][:, 256:512], ACT.Copy)\
                    .then_inc(S["wselT_set"], 1)

            def c_w(b):
                at_least(act, S["pos_set"], b + 1)
                at_least(act, S["den_set"], b + 1)
                at_least(act, S["w_out"], 16 * b)
                for j in range(ST):
                    act.activation(w_rows[:, j, :], banks[7][:, 96 + NEW * j:96 + NEW * j + NEW], ACT.Copy,
                                   scale=rdn[:, j:j + 1]).then_inc(S["w_set"], 1)

            def body(b, stages=range(5)):
                if 3 in stages:
                    c_w(b - 3)
                if 1 in stages:
                    b_exp(b - 1, 0)
                    b_exp(b - 1, 1)
                if 2 in stages:
                    c_hT(b - 2)
                if 1 in stages:
                    b_exp(b - 1, 2)
                    b_exp(b - 1, 3)
                if 2 in stages:
                    c_exp(b - 2)
                if 1 in stages:
                    b_attT(b - 1)
                if 0 in stages:
                    a_hsT(b)
                if 2 in stages:
                    c_wT(b - 2)
                if 0 in stages:
                    a_q(b)

            act.wait_ge(S["bias_in"], 16 * 8)
            for b in range(0, 5):
                body(b, range(b + 1))
            with act.Fori(5, BATCH) as b:
                body(b)
            for b in range(BATCH, BATCH + 4):
                body(b, range(b - BATCH + 1, 5))

            def x0_T(i, h):
                q = 2 * i + h
                at_least(act, S["xb_T"], q + 1)
                at_least(act, S["gu0_mm"], 2 * q)
                act.activation(xbT[:, 0, :], banks[0][:, 0:EPG * CAP], ACT.Copy).then_inc(S["xbT_set"], 1)

            def silu(i, h):
                q = 2 * i + h
                for u in range(2):
                    at_least(act, S["gu0_mm"], 2 * q + u + 1)
                    at_least(act, S["act0_set"], 2 * q + u - 1)
                    src = banks[2 + u][0:INTER0, 0:2 * 2 * CAP].rearrange("i (e s c) -> i e s c", e=2, s=2)
                    act.activation(silu0[:, 2 * u:2 * u + 2, :], src[:, :, 0, :], ACT.Silu).then_inc(S["silu0_set"], 1)

            def y0(i, h):
                q = 2 * i + h
                at_least(act, S["wslot_set"], q + 1)
                at_least(act, S["y_mm"], 2 * q + 2)
                for c in range(2):
                    at_least(act, S[f"scatter{c}"], 16 * (EPG // 2) * (q - 1))
                for e in range(2, EPG):
                    act.activation(y[h][:, e, :], banks[5 + 2 * h][0:CAP, D * (e - 2):D * (e - 2) + D], ACT.Copy,
                                   scale=wslot[h][:, e:e + 1]).then_inc(S["ya_set"], 1)

            def experts(i, h, i1, h1, first=False, last=False):
                if not last:
                    x0_T(i1, h1)
                if not first:
                    y0(i, h)
                if not last:
                    silu(i1, h1)

            experts(-1, 1, 0, 0, first=True)
            experts(0, 0, 0, 1)
            experts(0, 1, 1, 0)
            with act.Fori(1, QG // 2 - 1) as i:
                experts(i, 0, i, 1)
                experts(i, 1, i + 1, 0)
            experts(QG // 2 - 1, 0, QG // 2 - 1, 1)
            experts(QG // 2 - 1, 1, QG // 2, 0, last=True)

            def a1_hsT(b):
                at_least(act, S["hs_T"], BATCH + b + 1)
                at_least(act, S["q_mm"], BATCH + b)
                act.activation(hsT[:].rearrange("p k s -> p (k s)"), banks[0][:, :], ACT.Copy)\
                    .then_inc(S["hsT_set"], 1)

            def a1_q(b):
                at_least(act, S["q_mm"], BATCH + b + 1)
                at_least(act, S["s1_mm"], 4 * b)
                act.activation(qT[:].rearrange("p k s -> p (k s)"), banks[0][:, :], ACT.Copy,
                               scale=DH ** -0.5).then_inc(S["q_set"], 1)

            def b1_exp(b, u):
                at_least(act, S["sub_set"], 4 * b + u + 1)
                act.activation(soft[:, u, :], soft[:, u, :], ACT.Exp).then_inc(S["soft_set"], 1)

            def b1_softT(b, u):
                at_least(act, S["soft_T"], 4 * b + u + 1)
                at_least(act, S["pv_mm"], ST * (BATCH + b))
                act.activation(softT[:, u, :], banks[SOFT_BANK[u]][:, :], ACT.Copy).then_inc(S["softT_set"], 1)

            def b1_attT(b):
                at_least(act, S["att_T"], BATCH + b + 1)
                at_least(act, S["o_mm"], BATCH + b)
                act.activation(attT[:].rearrange("p k s -> p (k s)"), banks[0][:, :], ACT.Copy)\
                    .then_inc(S["attT_set"], 1)

            def c1_hT(b):
                at_least(act, S["h1_T"], b + 1)
                at_least(act, S["l1_mm"], b)
                at_least(act, S["hT1_set"], b)
                act.activation(hTr[:].rearrange("p k s -> p (k s)"), banks[3][:, :], ACT.Copy).then_inc(S["hTr_set"], 1)

            def d1_hT(b):
                at_least(act, S["hTr_set"], b + 1)
                at_least(act, S["gu1_mm"], E1 * b)
                act.activation(hT1[:], hTr[:], ACT.Copy).then_inc(S["hT1_set"], 1)

            def c1_exp(b):
                at_least(act, S["gap_set"], b + 1)
                act.activation(egap[:], gap[:], ACT.Exp).then_inc(S["egap_set"], 1)

            def c1_shareT(b):
                at_least(act, S["share_T"], b + 1)
                hold(act, S["share_out"], 16 * b)
                act.activation(shareT[:], banks[4][0:E1, 0:SEQ], ACT.Copy).then_inc(S["shareT_set"], 1)

            def d1_silu(b, e):
                at_least(act, S["gu1_mm"], E1 * b + e + 1)
                at_least(act, S["act1_set"], E1 * b + e - 1)
                act.activation(silu1[e % 2][:], banks[5 + e % 2][:, 0:SEQ], ACT.Silu).then_inc(S["silu1_set"], 1)

            def layer1(b, stages=range(5)):
                if 1 in stages:
                    b1_exp(b - 1, 0)
                    b1_exp(b - 1, 1)
                if 2 in stages:
                    c1_exp(b - 2)
                if 1 in stages:
                    b1_exp(b - 1, 2)
                    b1_exp(b - 1, 3)
                if 2 in stages:
                    c1_shareT(b - 2)
                if 1 in stages:
                    b1_softT(b - 1, 0)
                    b1_softT(b - 1, 1)
                if 3 in stages:
                    d1_silu(b - 3, 0)
                    d1_silu(b - 3, 1)
                if 1 in stages:
                    b1_softT(b - 1, 2)
                    b1_softT(b - 1, 3)
                if 3 in stages:
                    for e in range(2, 5):
                        d1_silu(b - 3, e)
                if 1 in stages:
                    b1_attT(b - 1)
                if 3 in stages:
                    d1_silu(b - 3, 5)
                    d1_silu(b - 3, 6)
                if 0 in stages:
                    a1_hsT(b)
                if 3 in stages:
                    d1_silu(b - 3, 7)
                if 2 in stages:
                    d1_hT(b - 2)
                if 1 in stages:
                    c1_hT(b - 1)
                if 0 in stages:
                    a1_q(b)

            for b in range(0, 5):
                layer1(b, range(b + 1))
            with act.Fori(5, BATCH) as b:
                layer1(b)
            for b in range(BATCH, BATCH + 4):
                layer1(b, range(b - BATCH + 1, 5))

        @block.tensor
        def _(pe):
            pe.wait_ge(S["ctx_in"], 16)
            pe.wait_ge(S["kv_w_in"], 32)
            for m in range(KC):
                for k in range(KC):
                    mm = pe.matmul(banks[m][:, :], wk0[:, k, P * m:P * m + P], cT[:, k, :], start=k == 0, stop=k == KC - 1)
                mm.then_inc(S["kT_mm"], 1)
            pe.wait_ge(S["cdup_set"], 2)
            for b in range(BATCH):
                for k in range(KC):
                    mm = pe.matmul(banks[2 + b // 2][:, D * (b % 2):D * (b % 2) + D],
                                   cdup[:, k, b].rearrange("p a c -> p (a c)"), wv0[:, k, :],
                                   start=k == 0, stop=k == KC - 1)
                if b % 2:
                    mm.then_inc(S["v_mm"], 1)
            pe.wait_ge(S["wk1_set"], 4)
            pe.wait_ge(S["kT_set"], 2)
            for m in range(KC):
                for k in range(KC):
                    mm = pe.matmul(banks[m][:, :], wk1[:, k, P * m:P * m + P], cT[:, k, :], start=k == 0, stop=k == KC - 1)
                mm.then_inc(S["kT_mm"], 1)
            for b in range(BATCH):
                for k in range(KC):
                    mm = pe.matmul(banks[6][:, CTX * b:CTX * b + CTX], cdup[:, k, b].rearrange("p a c -> p (a c)"),
                                   wv1[:, k, :], start=k == 0, stop=k == KC - 1)
            mm.then_inc(S["v_mm"], 1)

            def a_T(b):
                at_least(pe, S["hs_set"], b + 1)
                at_least(pe, S["q_set"], 2 * b)
                for j in range(ST):
                    for k in range(KC):
                        mm = pe.transpose(banks[0][:, SEQ * k + P * j:SEQ * k + P * j + P], hs[:, j, P * k:P * k + P], ident)
                mm.then_inc(S["hs_T"], 1)

            def a_q(b, m):
                at_least(pe, S["hsT_set"], b + 1)
                for k in range(KC):
                    mm = pe.matmul(banks[0][:, SEQ * m:SEQ * m + SEQ], wq0[:, k, P * m:P * m + P], hsT[:, k, :],
                                   start=k == 0, stop=k == KC - 1)
                if m == KC - 1:
                    mm.then_inc(S["q_mm"], 1)

            def b_s(b, j):
                at_least(pe, S["exp_set"], 4 * b + j - 1)
                if j == 0:
                    at_least(pe, S["q_set"], 2 * b + 2)
                    at_least(pe, S["k_set"], 2 * b + 2)
                for m in range(KC):
                    rows = slice(32 * j, 32 * j + 32)
                    pe.matmul(banks[1 + j % 2][:, SEQ * m:SEQ * m + SEQ],
                              k_blk[rows, m].rearrange("p a c -> p (a c)"), qT[rows, m, :],
                              start=True, stop=True).then_inc(S["s_mm"], 1)

            def b_pv(b, j):
                at_least(pe, S["clip_set"], 4 * b + 4)
                if j == 0:
                    at_least(pe, S["att_set"], 2 * b - 1)
                else:
                    at_least(pe, S["w_set"], 2 * (b - 1))
                for r in range(PAIRS):
                    mm = pe.matmul(banks[PV_BANK[j]][:, 2 * VW * r:2 * VW * r + 2 * VW], prob[:, r % 4, r // 4, P * j:P * j + P],
                                   v_blk[0][:, b, r].rearrange("p a d -> p (a d)"), start=True, stop=True)
                mm.then_inc(S["pv_mm"], 1)

            def b_T(b):
                at_least(pe, S["att_set"], 2 * b + 2)
                at_least(pe, S["delta_set"], b)
                for j in range(ST):
                    for k in range(KC):
                        mm = pe.transpose(banks[5][:, SEQ * k + P * j:SEQ * k + P * j + P], att[:, j, P * k:P * k + P], ident)
                mm.then_inc(S["att_T"], 1)

            def b_o(b):
                at_least(pe, S["attT_set"], b + 1)
                for j in range(ST):
                    for k in range(KC):
                        mm = pe.matmul(banks[5][:, D * j:D * j + D], attT[:, k, P * j:P * j + P], wo0[:, k, :],
                                       start=k == 0, stop=k == KC - 1)
                mm.then_inc(S["o_mm"], 1)

            def c_T(b):
                at_least(pe, S["h_set"], 2 * b + 2)
                at_least(pe, S["wselT_set"], b)
                at_least(pe, S["countT_set"], b)
                for j in range(ST):
                    for k in range(KC):
                        mm = pe.transpose(banks[6][:, SEQ * k + P * j:SEQ * k + P * j + P], h_rows[:, j, P * k:P * k + P], ident)
                mm.then_inc(S["h_T"], 1)

            def c_l(b):
                at_least(pe, S["hT_set"], b + 1)
                for j in range(ST):
                    for k in range(KC):
                        mm = pe.matmul(banks[6][:, OLD * j:OLD * j + OLD], hT[:, k, P * j:P * j + P], gate0[:, k, :],
                                       start=k == 0, stop=k == KC - 1)
                mm.then_inc(S["l_mm"], 1)

            def c_count(b):
                at_least(pe, S["sel_set"], b + 1)
                at_least(pe, S["selsum_set"], 2 * b)
                at_least(pe, S["logit_set"], b + 1)
                for j in range(ST):
                    o = banks[6][:, P * j:P * j + P]
                    pe.matmul(o, selsum[:] , ones_b[:], start=True, stop=False)
                    if j == 1:
                        pe.matmul(o, sel[:, 0, :], ones_b[:], start=False, stop=False)
                    mm = pe.matmul(o, sel[:, j, :], tri[:], start=False, stop=True)
                mm.then_inc(S["count_mm"], 1)

            def c_wT(b):
                at_least(pe, S["wsel_set"], 2 * b + 2)
                for j in range(ST):
                    mm = pe.transpose(banks[6][:, 256 + P * j:256 + P * j + P], wsel[:, j, :], ident)
                mm.then_inc(S["wsel_T"], 1)

            def c_pos(b):
                at_least(pe, S["countT_set"], b + 1)
                at_least(pe, S["wselT_set"], b + 1)
                at_least(pe, S["w_set"], 2 * b)
                if not (isinstance(b, int) and b == BATCH - 1):
                    at_least(pe, S["att_set"], 2 * (b + 1) + 2)
                for j in range(ST):
                    pe.matmul(banks[7][:, NEW * j:NEW * j + NEW], countT[:, j, :], map_b[:], start=True, stop=True)
                    mm = pe.matmul(banks[7][:, 96 + NEW * j:96 + NEW * j + NEW], wselT[:, j, :], map_f[:],
                                   start=True, stop=True)
                mm.then_inc(S["pos_mm"], 1)

            def d_slots(b, j, part):
                if part == 0:
                    at_least(pe, S["hit_set"], 2 * b + j + 1)
                    at_least(pe, S["slotb_acc"], b)
                    at_least(pe, S["slot_acc"], b)
                for n in range(NEW // 4 * part, NEW // 4 * (part + 1)):
                    mm = pe.matmul(banks[4][0:CAP, 2 * n:2 * n + 2], hit[:, j, n // EPG, :, n % EPG], loc1[:, j, :],
                                   start=j == 0 and n == 0, stop=j == ST - 1, skip_group_check=True)
                if part == 3:
                    mm.then_inc(S["slot_mm"], 1)

            def body(b, stages=range(5)):
                if 4 in stages:
                    d_slots(b - 4, 1, 0)
                    d_slots(b - 4, 1, 1)
                if 1 in stages:
                    b_s(b - 1, 0)
                    b_s(b - 1, 1)
                if 4 in stages:
                    d_slots(b - 4, 1, 2)
                    d_slots(b - 4, 1, 3)
                if 2 in stages:
                    c_T(b - 2)
                if 1 in stages:
                    b_s(b - 1, 2)
                if 2 in stages:
                    c_l(b - 2)
                if 1 in stages:
                    b_s(b - 1, 3)
                if 3 in stages:
                    d_slots(b - 3, 0, 0)
                if 1 in stages:
                    b_pv(b - 1, 0)
                if 1 in stages:
                    b_pv(b - 1, 1)
                if 2 in stages:
                    c_count(b - 2)
                if 3 in stages:
                    d_slots(b - 3, 0, 1)
                if 1 in stages:
                    b_T(b - 1)
                if 0 in stages:
                    a_T(b)
                if 2 in stages:
                    c_wT(b - 2)
                if 1 in stages:
                    b_o(b - 1)
                if 0 in stages:
                    a_q(b, 0)
                if 3 in stages:
                    d_slots(b - 3, 0, 2)
                if 0 in stages:
                    a_q(b, 1)
                if 2 in stages:
                    c_pos(b - 2)
                if 3 in stages:
                    d_slots(b - 3, 0, 3)

            pe.wait_ge(S["cst_in"], 16)
            pe.wait_ge(S["q_w_in"], 48)
            pe.wait_ge(S["kT_set"], 4)
            pe.wait_ge(S["v_set"], 13)
            pe.wait_ge(S["tri_set"], 1)
            pe.wait_ge(S["place_set"], 6)
            pe.wait_ge(S["map_set"], 4)
            pe.wait_ge(S["loc_set"], 2)
            pe.wait_ge(S["vblk_ones"], 4)
            for b in range(0, 5):
                body(b, range(b + 1))
            with pe.Fori(5, BATCH) as b:
                body(b)
            for b in range(BATCH, BATCH + 4):
                body(b, range(b - BATCH + 1, 5))

            def x0_T(i, h):
                q = 2 * i + h
                at_least(pe, S[f"gather{h}"], 16 * EPG * (i + 1))
                at_least(pe, S["xbT_set"], 2 * q)
                for k in range(KC):
                    for e in range(EPG):
                        mm = pe.transpose(banks[k][:, CAP * e:CAP * e + CAP], xb[h][:, e, P * k:P * k + P],
                                          ident[0:CAP, 0:CAP])
                mm.then_inc(S["xb_T"], 1)

            def gu(i, h):
                q = 2 * i + h
                at_least(pe, S["xbT_set"], 2 * q + 2)
                at_least(pe, S["act0_set"], 2 * q)
                at_least(pe, S[f"w0_ld{h}"], 32 * (i + 1))
                for e in range(EPG):
                    for s in range(2):
                        o = CAP * (2 * (e % 2) + s)
                        for k in range(KC):
                            mm = pe.matmul(banks[2 + e // 2][0:INTER0, o:o + CAP],
                                           gu0[h][:, k, e, INTER0 * s:INTER0 * s + INTER0], xbT[:, k, CAP * e:CAP * e + CAP],
                                           start=k == 0, stop=k == KC - 1)
                    if e % 2:
                        mm.then_inc(S["gu0_mm"], 1)

            def down(i, h):
                q = 2 * i + h
                for e in range(EPG):
                    if e % 2 == 0:
                        at_least(pe, S["act0_set"], 2 * q + e // 2 + 1)
                        at_least(pe, S["ya_set" if e else "yv_set"], 2 * (q - 1))
                    mm = pe.matmul(banks[4 + 2 * h + e // 2][0:CAP, D * (e % 2):D * (e % 2) + D], act0[:, e, :],
                                   down0[h][:, e, :], start=True, stop=True)
                    if e % 2:
                        mm.then_inc(S["y_mm"], 1)

            def experts(i, h, i1, h1, first=False, last=False):
                if not last:
                    x0_T(i1, h1)
                if not first:
                    down(i, h)
                if not last:
                    gu(i1, h1)

            pe.wait_ge(S["route_done"], 1)
            pe.wait_ge(S["w_set"], 2 * BATCH)
            experts(-1, 1, 0, 0, first=True)
            experts(0, 0, 0, 1)
            experts(0, 1, 1, 0)
            with pe.Fori(1, QG // 2 - 1) as i:
                experts(i, 0, i, 1)
                experts(i, 1, i + 1, 0)
            experts(QG // 2 - 1, 0, QG // 2 - 1, 1)
            experts(QG // 2 - 1, 1, QG // 2, 0, last=True)

            def a1_T(b):
                at_least(pe, S["hs_set"], BATCH + b + 1)
                at_least(pe, S["x3_set"], b)
                for j in range(ST):
                    for k in range(KC):
                        mm = pe.transpose(banks[0][:, SEQ * k + P * j:SEQ * k + P * j + P], hs[:, j, P * k:P * k + P], ident)
                mm.then_inc(S["hs_T"], 1)

            def a1_q(b):
                at_least(pe, S["hsT_set"], BATCH + b + 1)
                for m in range(KC):
                    for k in range(KC):
                        mm = pe.matmul(banks[0][:, SEQ * m:SEQ * m + SEQ], wq1[:, k, P * m:P * m + P], hsT[:, k, :],
                                       start=k == 0, stop=k == KC - 1)
                mm.then_inc(S["q_mm"], 1)

            def b1_s(b, u):
                j, m = u // KC, u % KC
                if u < 2:
                    at_least(pe, S["softT_set"], 4 * (b - 1) + u + 3)
                else:
                    at_least(pe, S["sub_set"], 4 * b + u - 1)
                if u == 0:
                    at_least(pe, S["q_set"], 2 * BATCH + b + 1)
                    at_least(pe, S["k1_set"], KC * b + KC)
                o = banks[1 + u % 2][:, :]
                pe.matmul(o, qT[:, m, P * j:P * j + P], k1_blk[:, m].rearrange("p h c -> p (h c)"), start=True,
                          stop=False)
                pe.matmul(o, bias_q[:, P * j:P * j + P], bias_k[:, b, 512 * m:512 * m + 512], start=False, stop=True)\
                    .then_inc(S["s1_mm"], 1)

            def b1_T(b, u):
                at_least(pe, S["soft_set"], 4 * b + u + 1)
                if u == 0:
                    at_least(pe, S["logit1_set"], b)
                for r in range(4):
                    mm = pe.transpose(banks[SOFT_BANK[u]][:, P * r:P * r + P], soft[:, u, P * r:P * r + P], ident)
                mm.then_inc(S["soft_T"], 1)

            def b1_pv(b, j):
                at_least(pe, S["softT_set"], 4 * b + 2 * j + 2)
                at_least(pe, S["att_set"], ST * (BATCH + b) + j)
                at_least(pe, S["shareT_set"], b)
                for r in range(PAIRS):
                    mm = pe.matmul(banks[4][:, 2 * VW * r:2 * VW * r + 2 * VW],
                                   softT[:, 2 * j + r // 4, P * (r % 4):P * (r % 4) + P],
                                   v_blk[1][:, b, r].rearrange("p a d -> p (a d)"), start=True, stop=True)
                mm.then_inc(S["pv_mm"], 1)

            def b1_T2(b):
                at_least(pe, S["att_set"], ST * (BATCH + b) + ST)
                for j in range(ST):
                    for k in range(KC):
                        mm = pe.transpose(banks[0][:, SEQ * k + P * j:SEQ * k + P * j + P], att[:, j, P * k:P * k + P], ident)
                mm.then_inc(S["att_T"], 1)

            def b1_o(b):
                at_least(pe, S["attT_set"], BATCH + b + 1)
                for j in range(ST):
                    for k in range(KC):
                        mm = pe.matmul(banks[0][:, D * j:D * j + D], attT[:, k, P * j:P * j + P], wo1[:, k, :],
                                       start=k == 0, stop=k == KC - 1)
                mm.then_inc(S["o_mm"], 1)

            def c1_T(b):
                at_least(pe, S["h_set"], 2 * (BATCH + b) + 2)
                at_least(pe, S["softT_set"], 4 * b + 1)
                for j in range(ST):
                    for k in range(KC):
                        mm = pe.transpose(banks[3][:, SEQ * k + P * j:SEQ * k + P * j + P], h_rows[:, j, P * k:P * k + P], ident)
                mm.then_inc(S["h1_T"], 1)

            def c1_l(b):
                at_least(pe, S["hTr_set"], b + 1)
                for j in range(ST):
                    for k in range(KC):
                        mm = pe.matmul(banks[3][:, E1 * j:E1 * j + E1], hTr[:, k, P * j:P * j + P], gate1[:, k, :],
                                       start=k == 0, stop=k == KC - 1)
                mm.then_inc(S["l1_mm"], 1)

            def c1_shareT(b):
                at_least(pe, S["share_set"], b + 1)
                at_least(pe, S["att_set"], ST * (BATCH + b) + ST)
                for j in range(ST):
                    mm = pe.transpose(banks[4][0:E1, P * j:P * j + P], share_c[:, j, :], ident)
                mm.then_inc(S["share_T"], 1)

            def d1_gu(b, e):
                at_least(pe, S["act1_set"], E1 * b + e - 1)
                if e == 0:
                    at_least(pe, S["hT1_set"], b + 1)
                o = banks[5 + e % 2]
                for n in range(2):
                    for k in range(KC):
                        mm = pe.matmul(o[:, SEQ * n:SEQ * n + SEQ], gu1[:, e, k, n, :], hT1[:, k, :],
                                       start=k == 0, stop=k == KC - 1)
                mm.then_inc(S["gu1_mm"], 1)

            def d1_down(b, e):
                at_least(pe, S["act1w_set"], E1 * b + e + 1)
                if e == 0:
                    at_least(pe, S["o_set"], b)
                for j in range(ST):
                    mm = pe.matmul(banks[7][:, D * j:D * j + D], act1w[e % 2][:, P * j:P * j + P], down1[:, e, :],
                                   start=e == 0 and j == 0, stop=e == E1 - 1, skip_group_check=True)
                mm.then_inc(S["down1_mm"], 1)

            def layer1(b, stages=range(5)):
                if 1 in stages:
                    b1_s(b - 1, 0)
                    b1_s(b - 1, 1)
                if 3 in stages:
                    d1_gu(b - 3, 0)
                if 1 in stages:
                    b1_s(b - 1, 2)
                if 1 in stages:
                    b1_s(b - 1, 3)
                if 3 in stages:
                    d1_gu(b - 3, 1)
                if 2 in stages:
                    c1_shareT(b - 2)
                if 1 in stages:
                    for u in range(4):
                        b1_T(b - 1, u)
                    b1_pv(b - 1, 0)
                if 3 in stages:
                    d1_down(b - 3, 0)
                    d1_gu(b - 3, 2)
                if 3 in stages:
                    d1_down(b - 3, 1)
                    d1_gu(b - 3, 3)
                if 1 in stages:
                    b1_pv(b - 1, 1)
                if 3 in stages:
                    d1_down(b - 3, 2)
                    d1_gu(b - 3, 4)
                if 1 in stages:
                    b1_T2(b - 1)
                if 3 in stages:
                    d1_down(b - 3, 3)
                    d1_gu(b - 3, 5)
                if 1 in stages:
                    b1_o(b - 1)
                if 3 in stages:
                    d1_down(b - 3, 4)
                    d1_gu(b - 3, 6)
                if 0 in stages:
                    a1_T(b)
                if 3 in stages:
                    d1_down(b - 3, 5)
                    d1_gu(b - 3, 7)
                if 1 in stages:
                    c1_T(b - 1)
                if 0 in stages:
                    a1_q(b)
                if 3 in stages:
                    d1_down(b - 3, 6)
                if 1 in stages:
                    c1_l(b - 1)
                if 3 in stages:
                    d1_down(b - 3, 7)

            pe.wait_ge(S["l1_w_in"], 64)
            pe.wait_ge(S["gate1_in"], 16)
            pe.wait_ge(S["bias_q_in"], 16)
            pe.wait_ge(S["e1_w_in"], 32)
            pe.wait_ge(S["bias1_in"], 2 * 16 * BATCH)
            pe.wait_ge(S["yv_set"], 2 * QG)
            pe.wait_ge(S["ya_set"], 2 * QG)
            for b in range(0, 5):
                layer1(b, range(b + 1))
            with pe.Fori(5, BATCH) as b:
                layer1(b)
            for b in range(BATCH, BATCH + 4):
                layer1(b, range(b - BATCH + 1, 5))

        @block.vector
        def _(dve):
            dve.wait_ge(S["bias_in"], 16 * 8)
            dve.tensor_scalar(hi[:], mask_i[:], 0.5, 100.0, ALU.is_gt, ALU.mult).then_inc(S["rs_set"], 1)
            dve.tensor_scalar(rs[:], rs[:], 0.0, 0.3, ALU.max, ALU.min).then_inc(S["rs_set"], 1)
            dve.wait_ge(S["rs_set"], 2)
            dve.tensor_scalar(hi[:], hi[:], -50.0, None, ALU.add).then_inc(S["hi_set"], 1)
            dve.tensor_tensor(rs2[:], rs[:], rs[:], ALU.mult).then_inc(S["rs_set"], 1)
            dve.wait_ge(S["mask_u_in"], 16)
            dve.tensor_scalar(mask_b[:].rearrange("p b o c -> p (b o c)"), mask_u[:], 1.0, -MASKED, ALU.subtract,
                              ALU.mult).then_inc(S["mask_b_set"], 1)
            dve.wait_ge(S["route_in"], 32)
            dve.wait_ge(S["cst_in"], 16)
            dve.tensor_copy(o2n_f[:], o2n_c[:]).then_inc(S["map_set"], 1)
            dve.tensor_scalar(unkept[:], o2n_r[:], -1.0, MASKED, ALU.is_equal, ALU.mult).then_inc(S["map_set"], 1)
            dve.tensor_copy(tri[:], cst[:, C_TRI:C_TRI + P]).then_inc(S["tri_set"], 1)
            dve.memset(loc1[:, :, 1], 1.0).then_inc(S["loc_set"], 1)
            dve.tensor_copy(loc1[:, :, 0], cst[:, C_LOC:C_LOC + ST]).then_inc(S["loc_set"], 1)
            dve.wait_ge(S["map_set"], 1)
            for m in (map_f, map_b):
                dve.tensor_scalar(m[:], cst[:, C_E48:C_E48 + NEW], o2n_f[:, 0:1], None, ALU.is_equal)\
                    .then_inc(S["map_set"], 1)
            for m in range(KC):
                dve.wait_ge(S["kT_mm"], m + 1)
                dve.tensor_scalar(kT[0][:, m, :], banks[m][:, :], bk0[:, m:m + 1], None, ALU.add).then_inc(S["kT_set"], 1)
            dve.wait_ge(S["vblk_zero"], 2)
            for v in v_blk:
                for a in range(2):
                    dve.memset(v[CTX * a:CTX * a + CTX, :, :, a, DH:VW], 1.0).then_inc(S["vblk_ones"], 1)
            for c in range(4):
                dve.wait_ge(S["v_mm"], c + 1)
                for a in range(2):
                    h = slice(CTX * a, CTX * a + CTX)
                    src = banks[2 + c][h, :].rearrange("p (b r a d) -> p b r a d", b=2, a=2, d=DH)
                    bias = bv0[h, :].rearrange("p (r a d) -> p r a d", a=2, d=DH)
                    for e in range(2):
                        ins = dve.tensor_tensor(v_blk[0][h, 2 * c + e, :, a, 0:DH], src[:, e, :, a, :],
                                                bias[:, :, a, :], ALU.add)
                    ins.then_inc(S["v_set"], 1)
            for m in range(KC):
                dve.wait_ge(S["kT_mm"], KC + m + 1)
                dve.tensor_copy(kT[1][:, m, :], banks[m][:, :]).then_inc(S["kT_set"], 1)
            dve.wait_ge(S["v_mm"], 5)
            for a in range(2):
                h = slice(CTX * a, CTX * a + CTX)
                src = banks[6][h, :].rearrange("p (b g d) -> p b g d", b=BATCH, d=DH)
                dst = v_blk[1][h, :, :, a, 0:DH].rearrange("p b (g r) d -> p b g r d", r=2)
                for r in range(2):
                    dve.tensor_copy(dst[:, :, :, r, :], src).then_inc(S["v_set"], 1)
            dve.tensor_copy(ident_b[:], ident).then_inc(S["v_set"], 1)
            dve.wait_ge(S["bound_set"], 1)
            dve.wait_ge(S["place_set"], 6)

            def a_stat(b):
                hold(dve, S["x_in"], 16 * b + 16)
                for j in range(ST):
                    dve.bn_stats(stat6[:, j, :], x_all[:, ST * b + j, :]).then_inc(S["stat_a"], 1)
                hold(dve, S["stat_a"], 2 * b + 2)
                hold(dve, S["rstd_a_set"], b)
                for j in range(ST):
                    dve.bn_aggr(mv_a[:, j, :], stat6[:, j, :]).then_inc(S["mv_a_set"], 1)

            def a_norm(b):
                at_least(dve, S["rstd_a_set"], b + 1)
                at_least(dve, S["hs_T"], b)
                for j in range(ST):
                    ins = dve.tensor_scalar(hs[:, j, :], x_all[:, ST * b + j, :], mv_a[:, j, 0:1], rstd_a[:, j:j + 1],
                                            ALU.subtract, ALU.mult)
                ins.then_inc(S["hs_set"], 1)

            def b_clip(b, j):
                at_least(dve, S["exp_set"], 4 * b + j + 1)
                v = prob[:, j].rearrange("p m s -> p (m s)")
                dve.tensor_scalar(v, v, hi[:, b:b + 1] if isinstance(b, int) else hi[:, bass.ds(b, 1)], lo[:, 0:1],
                                  ALU.min, ALU.max).then_inc(S["clip_set"], 1)

            def b_att(b, j):
                at_least(dve, S["pv_mm"], 2 * b + j + 1)
                at_least(dve, S["att_T"], b)
                src = banks[PV_BANK[j]][:, 0:HEADS * VW].rearrange("p (h v) -> p h v", v=VW)
                r = rden[:, j].rearrange("p r a -> p (r a)")
                dve.reciprocal(r, src[:, :, DH]).then_inc(S["rden_set"], 1)
                at_least(dve, S["rden_set"], 2 * b + j + 1)
                dve.tensor_tensor(att[:, j, :].rearrange("p (h d) -> p h d", d=DH), src[:, :, 0:DH],
                                  r[:, :, None].broadcast_to([P, HEADS, DH]), ALU.mult).then_inc(S["att_set"], 1)

            def b_delta(b):
                at_least(dve, S["o_mm"], b + 1)
                at_least(dve, S["dgam_set"], 2 * b)
                dve.tensor_tensor(delta[:], banks[5][:, :].rearrange("p (j d) -> p j d", d=D),
                                  bo0[:, None, :].broadcast_to([P, ST, D]), ALU.add).then_inc(S["delta_set"], 1)
                at_least(dve, S["delta_set"], b + 1)
                for j in range(ST):
                    dve.bn_stats(stat6_d[:, j, :], delta[:, j, :]).then_inc(S["stat_d"], 1)
                hold(dve, S["stat_d"], 2 * b + 2)
                hold(dve, S["ve_d_set"], b)
                for j in range(ST):
                    dve.bn_aggr(mv_d[:, j, :], stat6_d[:, j, :]).then_inc(S["mv_d_set"], 1)

            def b_gamma(b):
                at_least(dve, S["mv_d_set"], 2 * b + 2)
                for j in range(ST):
                    dve.scalar_tensor_tensor(dgam[:, j, :], delta[:, j, :], mv_d[:, j, 0:1], gamma[:], ALU.subtract,
                                             ALU.mult).then_inc(S["dgam_set"], 1)

            def b_x1(b):
                at_least(dve, S["rstd_d_set"], b + 1)
                at_least(dve, S["xbeta_set"], 2 * b + 2)
                at_least(dve, S["dgam_set"], 2 * b + 2)
                for j in range(ST):
                    dve.scalar_tensor_tensor(x_all[:, ST * b + j, :], dgam[:, j, :], rstd_d[:, j:j + 1], xbeta[:, j, :],
                                             ALU.mult, ALU.add).then_inc(S["x1_set"], 1)
                hold(dve, S["x1_set"], 2 * b + 2)
                for j in range(ST):
                    dve.bn_stats(stat6_h[:, j, :], x_all[:, ST * b + j, :]).then_inc(S["stat_h"], 1)
                hold(dve, S["stat_h"], 2 * b + 2)
                hold(dve, S["rstd_h_set"], b)
                for j in range(ST):
                    dve.bn_aggr(mv_h[:, j, :], stat6_h[:, j, :]).then_inc(S["mv_h_set"], 1)

            def b_h(b):
                at_least(dve, S["rstd_h_set"], b + 1)
                at_least(dve, S["h_T"], b)
                at_least(dve, S["h_out"], 16 * b)
                for j in range(ST):
                    dve.tensor_scalar(h_rows[:, j, :], x_all[:, ST * b + j, :], mv_h[:, j, 0:1], rstd_h[:, j:j + 1],
                                      ALU.subtract, ALU.mult).then_inc(S["h_set"], 1)

            def c_top(b):
                at_least(dve, S["l_mm"], b + 1)
                at_least(dve, S["etop_set"], 2 * b)
                dve.tensor_tensor(logit[:], banks[6][:, 0:ST * OLD].rearrange("p (j o) -> p j o", o=OLD),
                                  unkept[:, None, :].broadcast_to([P, ST, OLD]), ALU.add).then_inc(S["logit_set"], 1)
                hold(dve, S["logit_set"], b + 1)
                for j in range(ST):
                    dve.max(top[:, j, :], logit[:, j, :]).then_inc(S["top_set"], 1)
                at_least(dve, S["top_set"], 2 * b + 2)
                at_least(dve, S["etop_set"], 2 * b)
                dve.tensor_scalar(ntop[:], top[:, :, 0], -1.0, None, ALU.mult).then_inc(S["ntop_set"], 1)

            def c_sel(b):
                hold(dve, S["top_set"], 2 * b + 2)
                hold(dve, S["sel_set"], b)
                for j in range(ST):
                    dve.match_replace(left[:, j, :], top[:, j, :], logit[:, j, :], TAKEN).then_inc(S["left_set"], 1)
                at_least(dve, S["count_mm"], b)
                if not isinstance(b, int) or b > 0:
                    dve.tensor_tensor(selboth[:], sel[:, 0, :], sel[:, 1, :], ALU.add).then_inc(S["selsum_set"], 1)
                    at_least(dve, S["selsum_set"], 2 * b - 1)
                    dve.tensor_tensor(selsum[:], selsum[:], selboth[:], ALU.add).then_inc(S["selsum_set"], 1)
                at_least(dve, S["left_set"], 2 * b + 2)
                dve.tensor_tensor(sel[:], left[:], logit[:], ALU.not_equal).then_inc(S["sel_set"], 1)

            def c_weight(b):
                at_least(dve, S["expl_set"], 2 * b + 2)
                at_least(dve, S["sel_set"], b + 1)
                at_least(dve, S["wsel_T"], b)
                for j in range(ST):
                    dve.tensor_tensor(wsel[:, j, :], expl[:, j, :], sel[:, j, :], ALU.mult).then_inc(S["wsel_set"], 1)
                at_least(dve, S["etop_set"], 2 * b + 2)
                at_least(dve, S["w_set"], 2 * b)
                dve.reciprocal(rdn[:], den[:]).then_inc(S["den_set"], 1)

            def c_count(b):
                at_least(dve, S["wsel_T"], b + 1)
                at_least(dve, S["pos_mm"], b)
                dve.tensor_scalar(countT[:].rearrange("p j s -> p (j s)"), banks[6][:, 0:ST * P], float(P), None,
                                  ALU.min).then_inc(S["countT_set"], 1)

            def c_pos(b):
                at_least(dve, S["pos_mm"], b + 1)
                dve.tensor_scalar(off[:].rearrange("p j e -> p (j e)"), banks[7][:, 96:192], 0.0, float(P), ALU.is_le,
                                  ALU.mult).then_inc(S["off_set"], 1)
                at_least(dve, S["off_set"], b + 1)
                dve.scalar_tensor_tensor(pos[:].rearrange("p j e -> p (j e)"), banks[7][:, 0:96], float(P),
                                         off[:].rearrange("p j e -> p (j e)"), ALU.min, ALU.add).then_inc(S["pos_set"], 1)

            def c_hit(b, j):
                at_least(dve, S["pos_set"], b + 1)
                at_least(dve, S["slot_mm"], 2 * (b - 1) + j + 1)
                choice = pos[:, j, :].rearrange("t (q e) -> t q e", e=EPG)
                dve.tensor_tensor(hit[:, j], place[:], choice[:, :, None, :].broadcast_to([P, QG, CAP, EPG]),
                                  ALU.is_equal).then_inc(S["hit_set"], 1)

            def d_slots(b):
                at_least(dve, S["slot_mm"], 2 * b + 2)
                src = banks[4][0:CAP, 0:2 * NEW].rearrange("p (n v) -> p n v", v=2)
                at_least(dve, S["slot_acc"], b)
                at_least(dve, S["slotb_acc"], b)
                dve.tensor_tensor(slots[:], src, slots[:], ALU.add).then_inc(S["slot_acc"], 1)
                col = cst[0:CAP, C_B256 + b:C_B256 + b + 1] if isinstance(b, int) else cst[0:CAP, bass.ds(C_B256 + b, 1)]
                dve.scalar_tensor_tensor(slot_b[:], src[:, :, 1], col, slot_b[:], ALU.mult, ALU.add)\
                    .then_inc(S["slotb_acc"], 1)

            def body(b, stages=range(5)):
                if 2 in stages:
                    b_x1(b - 2)
                if 3 in stages:
                    c_pos(b - 3)
                if 2 in stages:
                    b_h(b - 2)
                if 1 in stages:
                    b_clip(b - 1, 0)
                    b_clip(b - 1, 1)
                if 3 in stages:
                    c_hit(b - 3, 0)
                if 4 in stages:
                    d_slots(b - 4)
                if 1 in stages:
                    b_clip(b - 1, 2)
                    b_clip(b - 1, 3)
                if 2 in stages:
                    c_top(b - 2)
                if 0 in stages:
                    a_stat(b)
                if 1 in stages:
                    b_att(b - 1, 0)
                if 2 in stages:
                    c_sel(b - 2)
                if 1 in stages:
                    b_att(b - 1, 1)
                if 0 in stages:
                    a_norm(b)
                if 2 in stages:
                    c_weight(b - 2)
                if 3 in stages:
                    c_hit(b - 3, 1)
                if 2 in stages:
                    c_count(b - 2)
                if 1 in stages:
                    b_delta(b - 1)
                    b_gamma(b - 1)

            for b in range(0, 5):
                body(b, range(b + 1))
            with dve.Fori(5, BATCH) as b:
                body(b)
            for b in range(BATCH, BATCH + 4):
                body(b, range(b - BATCH + 1, 5))
            dve.wait_ge(S["slotb_acc"], BATCH)
            dve.wait_ge(S["slot_acc"], BATCH)
            dve.tensor_scalar(empty[:], slots[:, :, 1], -1.0, 1.0, ALU.mult, ALU.add).then_inc(S["slot_acc"], 1)
            dve.tensor_tensor(slot_f[:], slots[:, :, 0], slot_b[:], ALU.add).then_inc(S["slot_acc"], 1)
            dve.wait_ge(S["slot_acc"], BATCH + 2)
            dve.scalar_tensor_tensor(slot_f[:], empty[:], cst[0:CAP, C_PAD:C_PAD + 1], slot_f[:], ALU.mult, ALU.add)\
                .then_inc(S["slot_acc"], 1)
            dve.wait_ge(S["slot_acc"], BATCH + 3)
            dve.tensor_copy(slot_i[:], slot_f[:]).then_inc(S["route_done"], 1)

            def x0_T(i, h):
                q = 2 * i + h
                at_least(dve, S["xb_T"], q + 1)
                at_least(dve, S["gu0_mm"], 2 * q)
                dve.tensor_copy(xbT[:, 1, :], banks[1][:, 0:EPG * CAP]).then_inc(S["xbT_set"], 1)
                wgt = xb[h][:, :, D + EPG * q:D + EPG * q + EPG] if isinstance(q, int) else \
                    xb[h][:, :, bass.ds(D + EPG * q, EPG)]
                own = cst[0:CAP, C_SLOTE:C_SLOTE + EPG * EPG].rearrange("p (e f) -> p e f", f=EPG)
                at_least(dve, S["wslot_set"], q)
                dve.tensor_tensor(wpick[:], wgt, own, ALU.mult).then_inc(S["wpick_set"], 1)
                at_least(dve, S["wpick_set"], q + 1)
                at_least(dve, S["ya_set"], 2 * (q - 1))
                at_least(dve, S["yv_set"], 2 * (q - 1))
                dve.tensor_reduce(wslot[h][:], wpick[:], AX.X, ALU.add).then_inc(S["wslot_set"], 1)

            def act0_mul(i, h):
                q = 2 * i + h
                for u in range(2):
                    at_least(dve, S["silu0_set"], 2 * q + u + 1)
                    at_least(dve, S["y_mm"], 2 * (q - 1) + u + 1)
                    src = banks[2 + u][0:INTER0, 0:2 * 2 * CAP].rearrange("i (e s c) -> i e s c", e=2, s=2)
                    dve.tensor_tensor(act0[:, 2 * u:2 * u + 2, :], silu0[:, 2 * u:2 * u + 2, :], src[:, :, 1, :],
                                      ALU.mult).then_inc(S["act0_set"], 1)

            def y0(i, h):
                q = 2 * i + h
                at_least(dve, S["y_mm"], 2 * q + 1)
                at_least(dve, S["wslot_set"], q + 1)
                for c in range(2):
                    at_least(dve, S[f"scatter{c}"], 16 * (EPG // 2) * (q - 1))
                for e in range(2):
                    dve.tensor_scalar(y[h][:, e, :], banks[4 + 2 * h][0:CAP, D * e:D * e + D], wslot[h][:, e:e + 1],
                                      None, ALU.mult).then_inc(S["yv_set"], 1)

            def experts(i, h, i1, h1, first=False, last=False):
                if not last:
                    x0_T(i1, h1)
                if not first:
                    y0(i, h)
                if not last:
                    act0_mul(i1, h1)

            experts(-1, 1, 0, 0, first=True)
            experts(0, 0, 0, 1)
            experts(0, 1, 1, 0)
            with dve.Fori(1, QG // 2 - 1) as i:
                experts(i, 0, i, 1)
                experts(i, 1, i + 1, 0)
            experts(QG // 2 - 1, 0, QG // 2 - 1, 1)
            experts(QG // 2 - 1, 1, QG // 2, 0, last=True)

            def a1_stat(b):
                hold(dve, S["x2_set"], b + 1)
                for j in range(ST):
                    dve.bn_stats(stat6[:, j, :], x_all[:, ST * b + j, :]).then_inc(S["stat_a"], 1)
                hold(dve, S["stat_a"], 2 * (BATCH + b) + 2)
                hold(dve, S["rstd_a_set"], BATCH + b)
                for j in range(ST):
                    dve.bn_aggr(mv_a[:, j, :], stat6[:, j, :]).then_inc(S["mv_a_set"], 1)

            def b1_max(b, u):
                at_least(dve, S["s1_mm"], 4 * b + u + 1)
                src = banks[1 + u % 2][:, :].rearrange("p (h c) -> p h c", c=CTX)
                dve.tensor_reduce(great[:, u, :], src, AX.X, ALU.max).then_inc(S["great_set"], 1)
                at_least(dve, S["great_set"], 4 * b + u + 1)
                at_least(dve, S["soft_T"], 4 * (b - 1) + u + 1)
                dve.tensor_tensor(soft[:, u, :].rearrange("p (h c) -> p h c", c=CTX), src,
                                  great[:, u, :, None].broadcast_to([P, 8, CTX]), ALU.subtract).then_inc(S["sub_set"], 1)

            def b1_att(b, j):
                at_least(dve, S["pv_mm"], ST * (BATCH + b) + j + 1)
                at_least(dve, S["att_T"], BATCH + b)
                src = banks[4][:, 0:HEADS * VW].rearrange("p (h v) -> p h v", v=VW)
                r = rden[:, j].rearrange("p r a -> p (r a)")
                dve.reciprocal(r, src[:, :, DH]).then_inc(S["rden_set"], 1)
                at_least(dve, S["rden_set"], ST * (BATCH + b) + j + 1)
                dve.tensor_tensor(att[:, j, :].rearrange("p (h d) -> p h d", d=DH), src[:, :, 0:DH],
                                  r[:, :, None].broadcast_to([P, HEADS, DH]), ALU.mult).then_inc(S["att_set"], 1)

            def b1_x3(b):
                at_least(dve, S["o_mm"], BATCH + b + 1)
                x = x_all[:, bass.ds(ST * b, ST), :]
                dve.tensor_tensor(x, x, banks[0][:, :].rearrange("p (j d) -> p j d", d=D), ALU.add)\
                    .then_inc(S["x3_set"], 1)
                hold(dve, S["x3_set"], b + 1)
                for j in range(ST):
                    dve.bn_stats(stat6_h[:, j, :], x_all[:, ST * b + j, :]).then_inc(S["stat_h"], 1)
                hold(dve, S["stat_h"], 2 * (BATCH + b) + 2)
                for j in range(ST):
                    dve.bn_aggr(mv_h[:, j, :], stat6_h[:, j, :]).then_inc(S["mv_h_set"], 1)

            def b1_h(b):
                at_least(dve, S["rstd_h_set"], BATCH + b + 1)
                at_least(dve, S["h1_T"], b)
                for j in range(ST):
                    dve.tensor_scalar(h_rows[:, j, :], x_all[:, ST * b + j, :], mv_h[:, j, 0:1], rstd_h[:, j:j + 1],
                                      ALU.subtract, ALU.mult).then_inc(S["h_set"], 1)

            def c1_top(b):
                at_least(dve, S["l1_mm"], b + 1)
                dve.tensor_copy(logit1[:].rearrange("p j e -> p (j e)"), banks[3][:, 0:ST * E1])\
                    .then_inc(S["logit1_set"], 1)
                hold(dve, S["logit1_set"], b + 1)
                for j in range(ST):
                    dve.max(top1[:, j, :], logit1[:, j, :]).then_inc(S["top1_set"], 1)
                hold(dve, S["top1_set"], 2 * b + 2)
                for j in range(ST):
                    dve.max_index(index1[:, j, :], top1[:, j, :], logit1[:, j, :]).then_inc(S["index1_set"], 1)
                dve.tensor_tensor(gap[:], top1[:, :, 1], top1[:, :, 0], ALU.subtract).then_inc(S["gap_set"], 1)
                at_least(dve, S["index1_set"], 2 * b + 2)
                for n in range(2):
                    dve.tensor_tensor(chosen[:, n], index1[:, :, n:n + 1].broadcast_to([P, ST, E1]),
                                      cst[:, None, C_E8:C_E8 + E1].broadcast_to([P, ST, E1]), ALU.is_equal)\
                        .then_inc(S["chosen_set"], 1)

            def c1_share(b):
                at_least(dve, S["egap_set"], b + 1)
                dve.tensor_scalar(wsum[:], egap[:], 1.0, None, ALU.add).then_inc(S["wsum_set"], 1)
                at_least(dve, S["wsum_set"], b + 1)
                dve.reciprocal(wpair[:, 0, :], wsum[:]).then_inc(S["w0_set"], 1)
                at_least(dve, S["w0_set"], b + 1)
                dve.tensor_tensor(wpair[:, 1, :], wpair[:, 0, :], egap[:], ALU.mult).then_inc(S["w1_set"], 1)
                at_least(dve, S["w1_set"], b + 1)
                at_least(dve, S["chosen_set"], 2 * b + 2)
                for n in range(2):
                    dve.tensor_tensor(chosen_w[:, n], chosen[:, n], wpair[:, n, :, None].broadcast_to([P, ST, E1]),
                                      ALU.mult).then_inc(S["chosen_w_set"], 1)
                at_least(dve, S["chosen_w_set"], 2 * b + 2)
                at_least(dve, S["share_T"], b)
                dve.tensor_tensor(share_c[:], chosen_w[:, 0], chosen_w[:, 1], ALU.add).then_inc(S["share_set"], 1)

            def a1_norm(b):
                at_least(dve, S["rstd_a_set"], BATCH + b + 1)
                at_least(dve, S["hs_T"], BATCH + b)
                for j in range(ST):
                    ins = dve.tensor_scalar(hs[:, j, :], x_all[:, ST * b + j, :], mv_a[:, j, 0:1], rstd_a[:, j:j + 1],
                                            ALU.subtract, ALU.mult)
                ins.then_inc(S["hs_set"], 1)

            def d1_mul(b, e):
                at_least(dve, S["silu1_set"], E1 * b + e + 1)
                at_least(dve, S["act1w_set"], E1 * b + e - 1)
                dve.tensor_tensor(act1[e % 2][:], silu1[e % 2][:], banks[5 + e % 2][:, SEQ:2 * SEQ], ALU.mult)\
                    .then_inc(S["act1_set"], 1)

            def d1_out(b):
                at_least(dve, S["down1_mm"], E1 * b + E1)
                at_least(dve, S["o_out"], 16 * b)
                dve.tensor_tensor(o_rows[:], banks[7][:, :].rearrange("p (j d) -> p j d", d=D),
                                  x_all[:, bass.ds(ST * b, ST), :], ALU.add).then_inc(S["o_set"], 1)

            def layer1(b, stages=range(5)):
                if 1 in stages:
                    b1_max(b - 1, 0)
                    b1_max(b - 1, 1)
                    b1_max(b - 1, 2)
                    b1_max(b - 1, 3)
                if 2 in stages:
                    c1_share(b - 2)
                if 4 in stages:
                    d1_out(b - 4)
                if 1 in stages:
                    b1_att(b - 1, 0)
                if 3 in stages:
                    d1_mul(b - 3, 0)
                if 3 in stages:
                    d1_mul(b - 3, 1)
                    d1_mul(b - 3, 2)
                if 1 in stages:
                    b1_att(b - 1, 1)
                if 3 in stages:
                    d1_mul(b - 3, 3)
                if 0 in stages:
                    a1_stat(b)
                if 3 in stages:
                    d1_mul(b - 3, 4)
                if 0 in stages:
                    a1_norm(b)
                if 3 in stages:
                    d1_mul(b - 3, 5)
                if 1 in stages:
                    b1_x3(b - 1)
                if 3 in stages:
                    d1_mul(b - 3, 6)
                if 1 in stages:
                    b1_h(b - 1)
                if 3 in stages:
                    d1_mul(b - 3, 7)
                if 1 in stages:
                    c1_top(b - 1)

            for b in range(0, 5):
                layer1(b, range(b + 1))
            with dve.Fori(5, BATCH) as b:
                layer1(b)
            for b in range(BATCH, BATCH + 4):
                layer1(b, range(b - BATCH + 1, 5))


def laid_out(i):
    def chunks(w):
        return np.ascontiguousarray(w.reshape(-1, P, w.shape[-1]).transpose(1, 0, 2))

    def dup(m):
        return np.ascontiguousarray(np.concatenate([m.T, m.T], 0))
    left, rows = position_bias()
    return {
        "x": i["x"].reshape(TOKENS, D),
        "ctxT": chunks(i["ctx_2048"].reshape(BATCH * CTX, D).T),
        "cst": constants(), "bias_q": left, "bias_k": rows,
        "wk0": chunks(i["L0_xattn_Wk"].T), "wv0": chunks(i["L0_xattn_Wv"].T),
        "wq0": chunks(i["L0_xattn_Wq"].T), "wo0": chunks(i["L0_xattn_Wo"].T),
        "gate0": chunks(i["L0_ffn_gate_weight"].T),
        "wq1": chunks(i["L1_xattn_Wq"]), "wk1": chunks(i["L1_xattn_Wk"]),
        "wv1": chunks(i["L1_xattn_Wv"]), "wo1": chunks(i["L1_xattn_Wo"]),
        "bq0": i["L0_xattn_bq"].reshape(KC, P).T, "bk0": i["L0_xattn_bk"].reshape(KC, P).T,
        "bv0": i["L0_xattn_bv"], "bo0": i["L0_xattn_bo"],
        "gamma": i["L0_xattn_ln_gamma"], "beta": i["L0_xattn_ln_beta"],
        "rs": i["L0_xattn_residual_scale"].reshape(1),
        "o2n": i["L0_ffn_old_to_new"],
        "mask0": dup(i["mask_BxS2_ik0"]), "mask1": i["mask_BxS2_bf1"].view(np.uint8).reshape(1, BATCH * CTX),
        "gu0": np.ascontiguousarray(i["L0_ffn_gate_up_proj"].reshape(QG, EPG, 2 * INTER0, KC, P).transpose(0, 4, 3, 1, 2)),
        "down0": np.ascontiguousarray(i["L0_ffn_down_proj"].reshape(QG, EPG, D, INTER0).transpose(0, 3, 1, 2)),
        "gate1": chunks(i["L1_ffn_router_gate"].T),
        "gu1": np.ascontiguousarray(i["L1_ffn_expert_gate_up"].reshape(E1, KC, P, INTER1, 2).transpose(2, 0, 1, 4, 3)),
        "down1": np.ascontiguousarray(i["L1_ffn_expert_down"].transpose(1, 0, 2)),
    }


def kernel(**inputs):
    from concourse import bacc
    from concourse.bass_utils import run_bass_kernel_spmd

    nc = bacc.Bacc("TRN2", target_bir_lowering=False, num_devices=1)
    arrays = {f"in_{n}": np.ascontiguousarray(a) for n, a in laid_out(inputs).items()}
    t = {n[3:]: nc.dram_tensor(n, a.shape, mybir.dt.from_np(a.dtype), kind="ExternalInput").ap()
         for n, a in arrays.items()}
    out = nc.dram_tensor("out", (TOKENS, D), F32, kind="ExternalOutput").ap()
    build(nc, t, out)
    r = run_bass_kernel_spmd(nc, [arrays], core_ids=[0])
    return r.results[0]["out"].reshape(BATCH, SEQ, D)
```

```python
from contextlib import ExitStack

import concourse.bass as bass
import numpy as np
from concourse import mybir

F32, BF16, F32R = mybir.dt.float32, mybir.dt.bfloat16, mybir.dt.float32r
I32, U32, U8 = mybir.dt.int32, mybir.dt.uint32, mybir.dt.uint8
ALU = mybir.AluOpType
ACT = mybir.ActivationFunctionType
AX = mybir.AxisListType

P = 128
BATCH, SEQ, D = 8, 256, 256
CTX = 64
HEADS, DH = 16, 16
TOKENS = BATCH * SEQ
KC = D // P
ST = SEQ // P
PAIRS = HEADS // 2
VW = DH + 1
GROUPS = 4
OLD, NEW, TOPK, CAP, INTER0 = 128, 48, 8, 96, 96
EPG = 4
QG = NEW // EPG
TURN = 3
ROW = D + NEW
PADROWS = TOKENS + P
E1, INTER1 = 8, 128
EPS = 1e-5
MASKED = -1e30
TAKEN = -3e38
PV_BANK = (3, 7)
SOFT_BANK = (3, 1, 2, 3)

C_ID, C_TRI, C_E48 = 0, 128, 256
C_HEAD2, C_HEAD8, C_SLOTE, C_PAD, C_LOC, C_B256, C_E8 = 304, 306, 314, 330, 331, 333, 341
C_N = 349


def constants():
    c = np.zeros((P, C_N), np.float32)
    p = np.arange(P)
    c[:, C_ID:C_ID + P] = np.eye(P)
    c[:, C_TRI:C_TRI + P] = p[:, None] < p[None, :]
    c[:, C_E48:C_E48 + NEW] = np.arange(NEW)
    c[:, C_HEAD2:C_HEAD2 + 2] = (p[:, None] // DH) % 2 == np.arange(2)
    c[:, C_HEAD8:C_HEAD8 + 8] = p[:, None] // DH == np.arange(8)
    c[:, C_SLOTE:C_SLOTE + EPG * EPG] = np.eye(EPG).reshape(-1)
    c[:, C_PAD] = TOKENS + p
    c[:, C_LOC] = p
    c[:, C_B256:C_B256 + BATCH] = SEQ * np.arange(BATCH)
    c[:, C_E8:C_E8 + E1] = np.arange(E1)
    return c


def thirds(a):
    bf = mybir.dt.np(BF16)
    out = []
    for _ in range(3):
        out.append(a.astype(bf))
        a = a - out[-1].astype(np.float32)
    return out


def position_bias():
    slope = (np.float32(2.0 ** (-8.0 / HEADS)) ** np.arange(1, HEADS + 1, dtype=np.float32)).astype(np.float32)
    key = slope[:, None] * np.arange(CTX, dtype=np.float32)
    query = np.repeat(-slope[:, None], CTX, 1)
    rows = np.stack(thirds(key) + thirds(query)).reshape(6, HEADS * CTX)
    left = np.ones((7, SEQ), rows.dtype)
    left[4:] = np.arange(SEQ)
    return left, rows


def in_parts(pe, out, left, right, start, stop):
    pe.matmul(out, left[0].bitcast(F32R), right[0].bitcast(F32R), start=start, stop=False)
    pe.matmul(out, left[0].bitcast(F32R), right[1].bitcast(F32R), start=False, stop=False)
    return pe.matmul(out, left[1].bitcast(F32R), right[0].bitcast(F32R), start=False, stop=stop)


def at_least(eng, sem, value):
    if not isinstance(value, int) or value > 0:
        eng.wait_ge(sem, value)


def build(nc, t, out):
    with ExitStack() as ctx:
        def sb(name, shape, dt=F32):
            return ctx.enter_context(nc.sbuf_tensor(name, shape, dt))

        def sb_twice(name, shape, dt=F32):
            with nc.sbuf_tensor(name, shape, dt) as first:
                pass
            return first, sb(name + "_cut", shape, dt)

        def sem(name):
            return ctx.enter_context(nc.semaphore(name))

        def hold(eng, s, value):
            if isinstance(value, int):
                if value > 0:
                    eng.wait_ge(s, value)
            else:
                eng.wait_ge(s, value)
                eng.sem_inc(held, 1)

        held = sem("held")
        rows_d = nc.dram_tensor("rows_scratch", (PADROWS, ROW), F32, kind="Internal").ap()
        sums_d = [nc.dram_tensor(f"sum{k}_scratch", (PADROWS, D), F32, kind="Internal").ap() for k in range(2)]
        out_v = out.rearrange("(b j p) d -> b p j d", j=ST, p=P)
        x_v = t["x"].rearrange("(b j p) d -> b p j d", j=ST, p=P)
        rows_v = rows_d[0:TOKENS, :].rearrange("(b j p) d -> b p j d", j=ST, p=P)
        sums_v = [s[0:TOKENS, :].rearrange("(b j p) d -> b p j d", j=ST, p=P) for s in sums_d]

        x_all = sb("x_all", [P, BATCH * ST, D])
        cst = sb("cst", [P, C_N])
        ident = cst[:, C_ID:C_ID + P]
        half = sb("half", [P, ST])
        cT = sb("cT", [P, KC, BATCH * CTX])
        NV, NK, NW = BATCH * PAIRS * 2 * VW, KC * BATCH * CTX, KC * D
        early = sb("early", [P, NV + NK + 2 * NW])
        v_blk = [early[:, 0:NV].rearrange("p (b r a v) -> p b r a v", b=BATCH, r=PAIRS, a=2),
                 sb("v_blk1", [P, BATCH, PAIRS, 2, VW])[:]]
        kT = [early[:, NV:NV + NK].rearrange("p (k c) -> p k c", k=KC), sb("kT1", [P, KC, BATCH * CTX])[:]]
        wk0, wv0 = (early[:, NV + NK + n * NW:NV + NK + n * NW + NW].rearrange("p (k d) -> p k d", k=KC)
                    for n in range(2))
        wq0, wo0 = (sb(n, [P, KC, D]) for n in ("wq0", "wo0"))
        wq1, wo1, wk1 = (sb(n, [P, KC, D]) for n in ("wq1", "wo1", "wk1"))
        wk1n, wv1 = (sb(n, [P, KC, GROUPS * DH]) for n in ("wk1n", "wv1"))
        gate0 = sb("gate0", [P, KC, OLD])
        bq0, bk0 = sb("bq0", [P, KC]), sb("bk0", [P, KC])
        bv0, bo0, gamma, beta = (sb(n, [P, D]) for n in ("bv0", "bo0", "gamma", "beta"))
        cdup = sb("cdup", [P, KC, BATCH, 2, CTX])
        mask_i = sb("mask_i", [P, BATCH], I32)
        hi = sb("hi", [P, BATCH])
        lo = sb("lo", [P, 1])
        rs = sb("rs", [P, 1])
        rs2 = sb("rs2", [P, 1])
        o2n_c, o2n_r = sb("o2n_c", [P, 1], I32), sb("o2n_r", [P, OLD], I32)
        o2n_f = sb("o2n_f", [P, 1])
        unkept = sb("unkept", [P, OLD])
        map_f, map_b = sb("map_f", [P, NEW]), sb("map_b", [P, NEW], BF16)
        tri, ones_b = (sb(n, [P, P], BF16) for n in ("tri", "ones_b"))
        place, place_r = sb_twice("place", [P, QG, CAP, EPG], BF16)
        loc1 = sb("loc1", [P, 2], BF16)
        stat6, stat6_d, stat6_h = (sb(n, [P, ST, 6]) for n in ("stat6", "stat6_d", "stat6_h"))
        mv_a, mv_d, mv_h = (sb(n, [P, ST, 2]) for n in ("mv_a", "mv_d", "mv_h"))
        rstd_a, rstd_d, rstd_h = (sb(n, [P, ST]) for n in ("rstd_a", "rstd_d", "rstd_h"))
        ve_a, ve_d, ve_h = (sb(n, [P, ST]) for n in ("ve_a", "ve_d", "ve_h"))
        hs = sb("hs", [P, ST, D])
        hsT = sb("hsT", [P, KC, SEQ])
        qT = sb("qT", [P, KC, SEQ])
        k_blk = sb("k_blk", [P, KC, 2, CTX])
        xbeta = sb("xbeta", [P, ST, D])
        prob = sb("prob", [P, 4, KC, SEQ])
        rden = sb("rden", [P, ST, PAIRS, 2])
        att = sb("att", [P, ST, D])
        attT = sb("attT", [P, KC, SEQ])
        delta = sb("delta", [P, ST, D])
        dgam = sb("dgam", [P, ST, D])
        h_rows = sb("h_rows", [P, ST, D])
        hT = sb("hT", [P, KC, SEQ])
        logit = sb("logit", [P, ST, OLD])
        top = sb("top", [P, ST, TOPK])
        ntop = sb("ntop", [P, ST])
        etop = sb("etop", [P, ST, TOPK])
        den = sb("den", [P, ST])
        rdn = sb("rdn", [P, ST])
        left = sb("left", [P, ST, OLD])
        sel = sb("sel", [P, ST, OLD], BF16)
        selsum = sb("selsum", [P, OLD], BF16)
        selboth = sb("selboth", [P, OLD], BF16)
        expl = sb("expl", [P, ST, OLD])
        wsel = sb("wsel", [P, ST, OLD])
        countT = sb("countT", [P, ST, P], BF16)
        wselT = sb("wselT", [P, ST, P])
        w_rows = sb("w_rows", [P, ST, NEW])
        off = sb("off", [P, ST, NEW])
        pos = sb("pos", [P, ST, NEW], BF16)
        hit, hit_r = sb_twice("hit", [P, ST, QG, CAP, EPG], BF16)
        slots = sb("slots", [CAP, NEW, 2])
        slot_b = sb("slot_b", [CAP, NEW])
        empty, second = (sb(n, [CAP, NEW]) for n in ("empty", "second"))
        slot_f = sb("slot_f", [CAP, NEW])
        slot_i = sb("slot_i", [CAP, NEW + EPG], U32)
        zrow = sb("zrow", [P, ROW])
        take = [sb(f"take{h}", [CAP, EPG], U32) for h in range(TURN)]
        give = [sb(f"give{h}", [CAP, EPG], U32) for h in range(TURN)]
        NG, ND, NX = KC * EPG * 2 * INTER0, EPG * D, EPG * ROW
        late, late_r = sb_twice("late", [P, 2 * NG + 2 * ND])
        x_flat = x_all[:].rearrange("p n d -> p (n d)")
        (y_a, y_a_r), (xb_a, xb_a_r), (xb_b, xb_b_r) = (
            sb_twice(n, [P, m]) for n, m in (("y_a", ND), ("xb_a", NX), ("xb_b", NX)))
        y_b = sb("y_b", [P, ND])
        gu0 = [v.rearrange("p (k e o) -> p k e o", k=KC, e=EPG)
               for v in (late[:, 0:NG], late[:, NG:2 * NG], x_flat[:, 0:NG])]
        down0 = [v[0:INTER0].rearrange("p (e d) -> p e d", e=EPG)
                 for v in (late[:, 2 * NG:2 * NG + ND], late[:, 2 * NG + ND:2 * (NG + ND)], x_flat[:, NG:NG + ND])]
        y = [v[0:CAP].rearrange("p (e d) -> p e d", e=EPG)
             for v in (y_a[:], y_b[:], x_flat[:, NG + ND:NG + 2 * ND])]
        xb = [v[0:CAP].rearrange("p (e r) -> p e r", e=EPG)
              for v in (xb_a[:], xb_b[:],
                        prob[:].rearrange("p j k s -> p (j k s)")[:, 0:NX])]
        wpick = sb("wpick", [CAP, EPG, EPG])
        wslot = [sb(f"wslot{h}", [CAP, EPG]) for h in range(TURN)]
        xbT = sb("xbT", [P, KC, EPG * CAP])
        silu0 = sb("silu0", [INTER0, EPG, CAP])
        act0 = sb("act0", [INTER0, EPG, CAP])
        HALF = BATCH // 2
        NE = KC * 2 * INTER1
        x_add = late[:, 0:HALF * ST * D].rearrange("p (n d) -> p n d", d=D)
        gu1_low = [v.rearrange("p (k s i) -> p k s i", k=KC, s=2)
                   for v in [late_r[:, HALF * ST * D + NE * e:HALF * ST * D + NE * e + NE] for e in range(E1 - 2)]
                   + [y_a_r[:, NE * e:NE * e + NE] for e in range(2)]]
        down1_low = [xb[:, D * e:D * e + D] for xb in (xb_a_r, xb_b_r) for e in range(E1 // 2)]
        gu1, gu1_high = (h[:].rearrange("p j q c e -> p (j q c e)").bitcast(F32)[:, 0:E1 * NE]
                         .rearrange("p (e k s i) -> p e k s i", e=E1, k=KC, s=2) for h in (hit, hit_r))
        down1, down1_high = (h[:].rearrange("p q c e -> p (q c e)").bitcast(F32)[:, 0:E1 * D]
                             .rearrange("p (e d) -> p e d", e=E1) for h in (place, place_r))
        weight_parts = [(gu1[:, e], gu1_high[:, e], gu1_low[e]) for e in range(E1)] \
            + [(down1[:, e], down1_high[:, e], down1_low[e]) for e in range(E1)]
        late_parts = weight_parts[E1 - 2:E1]
        early_parts = weight_parts[:E1 - 2] + weight_parts[E1:]
        gate1 = sb("gate1", [P, KC, E1])
        bias_k = early[:, 0:BATCH * HEADS * CTX // 2].bitcast(BF16)[0:7].rearrange("p (b c) -> p b c", b=BATCH)
        bias_q = sb("bias_q", [7, SEQ], BF16)
        mask_u = sb("mask_u", [1, BATCH * CTX], U8)
        mask_b = sb("mask_b", [1, BATCH, 1, CTX], BF16)
        k1_blk = sb("k1_blk", [P, KC, 8, CTX])
        great = sb("great", [P, 4, 8])
        soft = prob[:].rearrange("p j m s -> p j (m s)")
        softT = cdup[:].rearrange("p k b a c -> p (k b a c)").rearrange("p (u c) -> p u c", u=4)
        hT1 = sb("hT1", [P, KC, SEQ])
        hT1_low = sb("hT1_low", [P, KC, SEQ])
        hTr = hT
        logit1 = sb("logit1", [P, ST, E1])
        top1, index1 = sb("top1", [P, ST, 8]), sb("index1", [P, ST, 8], U32)
        gap, egap, wsum = (sb(n, [P, ST]) for n in ("gap", "egap", "wsum"))
        wpair = sb("wpair", [P, 2, ST])
        chosen = sb("chosen", [P, 2, ST, E1])
        chosen_w = sb("chosen_w", [P, 2, ST, E1])
        share_c = sb("share_c", [P, ST, E1])
        silu1 = [sb(f"silu1_{h}", [P, SEQ]) for h in range(2)]
        act1 = [sb(f"act1_{h}", [P, SEQ]) for h in range(2)]
        act1_high, act1_low = ([sb(f"act1_{n}{h}", [P, SEQ]) for h in range(2)] for n in ("high", "low"))
        o_rows = delta

        banks = [ctx.enter_context(nc.psum_tensor(f"bank{k}", [P, 512], F32)) for k in range(8)]

        S = {}
        for n in ("ctx_in", "cst_in", "kv_w_in", "q_w_in", "bias_in", "route_in", "l1_w_in", "x_in", "zero_out",
                  "half_set", "wk1_set", "cdup_set", "vblk_zero", "vblk_ones", "hi_set", "bound_set", "rs_set",
                  "map_set", "tri_set", "place_set", "loc_set", "kT_mm", "kT_set", "v_mm", "v_set", "stat_a",
                  "mv_a_set", "ve_a_set", "rstd_a_set", "hs_set", "hs_T", "hsT_set", "q_mm", "q_set", "k_set",
                  "xbeta_set", "s_mm", "exp_set", "clip_set", "pv_mm", "rden_set", "att_set", "att_T", "attT_set",
                  "o_mm", "delta_set", "stat_d", "mv_d_set", "ve_d_set", "pow_d_set", "rstd_d_set", "dgam_set",
                  "x1_set", "stat_h", "mv_h_set", "ve_h_set", "rstd_h_set", "h_set", "x1_out", "h_out", "w_out",
                  "h_T", "hT_set", "l_mm", "logit_set", "top_set", "ntop_set", "left_set", "sel_set", "expl_set",
                  "etop_set", "den_set", "wsel_set", "count_mm", "wsel_T", "countT_set", "wselT_set", "pos_mm",
                  "w_set", "off_set", "pos_set", "hit_set", "signed_set", "slot_mm", "slot_acc", "slotb_acc",
                  "selsum_set", "route_done", "w0_ld0", "w0_ld1", "w0_ld2", "take_set", "give_set", "gather0",
                  "gather1", "gather2", "scatter0", "scatter1", "xb_T", "xbT_set", "wpick_set", "wslot_set",
                  "gu0_mm", "silu0_set", "act0_set", "y_mm", "yv_set", "ya_set", "gate1_in", "bias_q_in",
                  "bias1_in", "mask1_in", "mask_u_in", "mask_b_set", "e1_w_in", "sum_in0", "sum_in1", "x2_set",
                  "k1_set", "s1_mm", "great_set", "sub_set", "soft_set", "soft_T", "softT_set", "x3_set", "h1_T",
                  "hT1_set", "hTr_set", "hT1h_set", "whigh_set", "wlow_set", "wparts_set", "act1h_set", "act1l_set",
                  "l1_mm", "logit1_set", "top1_set", "index1_set", "gap_set", "egap_set", "wsum_set", "w0_set",
                  "w1_set", "chosen_set", "chosen_w_set", "share_set", "gu1_mm", "silu1_set", "act1_set",
                  "down1_mm", "acc_set", "o_out"):
            S[n] = sem(n)
        block = ctx.enter_context(nc.Block())

        @block.sync
        def _(sp):
            sp.dma_start(cT[:], t["ctxT"]).then_inc(S["ctx_in"], 16)
            sp.dma_start(wk0[:], t["wk0"]).then_inc(S["kv_w_in"], 16)
            sp.dma_start(wv0[:], t["wv0"]).then_inc(S["kv_w_in"], 16)
            sp.dma_start(cst[:], t["cst"]).then_inc(S["cst_in"], 16)
            sp.dma_start(x_all[:, 0:ST, :], x_v[0]).then_inc(S["x_in"], 16)
            for n, v in ((wq0, "wq0"), (wo0, "wo0"), (gate0, "gate0")):
                sp.dma_start(n[:], t[v]).then_inc(S["q_w_in"], 16)
            sp.wait_ge(S["x_in"], 16)
            with sp.Fori(1, BATCH) as b:
                sp.dma_start(x_all[:, bass.ds(ST * b, ST), :], x_v[b]).then_inc(S["x_in"], 16)
                sp.wait_ge(S["x_in"], 16 * b + 16)
                sp.sem_inc(held, 1)
            for n, v in ((wq1, "wq1"), (wk1n, "wk1"), (wv1, "wv1"), (wo1, "wo1")):
                sp.dma_start(n[:], t[v]).then_inc(S["l1_w_in"], 16)
            sp.wait_ge(S["place_set"], 1)
            sp.dma_start(rows_d[TOKENS:PADROWS, :], zrow[:]).then_inc(S["zero_out"], 16)
            for k in range(2):
                sp.dma_start(sums_d[k][TOKENS:PADROWS, :], zrow[:, 0:D]).then_inc(S["zero_out"], 16)
            for k in range(TOKENS // P):
                sp.dma_start(sums_d[1][P * k:P * k + P, :], zrow[:, 0:D]).then_inc(S["zero_out"], 16)

            def store_x1(b):
                at_least(sp, S["x1_set"], 2 * b + 2)
                sp.dma_start(sums_v[0][b], x_all[:, bass.ds(ST * b, ST), :]).then_inc(S["x1_out"], 16)
                at_least(sp, S["h_set"], 2 * b + 2)
                sp.dma_start(rows_v[b][:, :, 0:D], h_rows[:]).then_inc(S["h_out"], 16)

            def store_w(b):
                at_least(sp, S["w_set"], 2 * b + 2)
                sp.dma_start(rows_v[b][:, :, D:ROW], w_rows[:]).then_inc(S["w_out"], 16)


            def load_w0(i, h):
                q = TURN * i + h
                at_least(sp, S["gu0_mm"], 2 * (q - TURN + 1))
                sp.dma_start(gu0[h], t["gu0"][q]).then_inc(S[f"w0_ld{h}"], 16)
                at_least(sp, S["y_mm"], 2 * (q - TURN + 1))
                sp.dma_start(down0[h], t["down0"][q]).then_inc(S[f"w0_ld{h}"], 16)

            load_w0(0, 0)
            load_w0(0, 1)
            store_x1(0)
            with sp.Fori(0, BATCH - 1) as i:
                store_x1(i + 1)
                store_w(i)
            store_w(BATCH - 1)

            sp.wait_ge(S["x1_out"], 16 * BATCH)
            sp.wait_ge(S["h_set"], 2 * BATCH)
            load_w0(0, 2)
            def load_w1(e):
                sp.dma_start(gu1[:, e], t["gu1"][:, e]).then_inc(S["e1_w_in"], 16)
                sp.dma_start(down1[:, e], t["down1"][:, e]).then_inc(S["e1_w_in"], 16)

            sp.wait_ge(S["route_done"], 1)
            sp.wait_ge(S["slot_mm"], BATCH)
            sp.wait_ge(S["pv_mm"], 2 * BATCH)
            for h in range(TURN):
                load_w0(1, h)
                if h:
                    load_w1(h - 1)
            sp.dma_start(bias_k[1:7], t["bias_k"][:, None, :].broadcast_to([6, BATCH, HEADS * CTX]))\
                .then_inc(S["bias1_in"], 16)
            for i in range(2, QG // TURN):
                for h in range(TURN):
                    load_w0(i, h)
                    load_w1(TURN * (i - 2) + h + 2)

            sp.wait_ge(S["scatter0"], 16 * NEW // 2)
            sp.wait_ge(S["scatter1"], 16 * NEW // 2)
            sp.wait_ge(S["y_mm"], 2 * QG)

            def load_x(b, half):
                n = b + HALF * half
                sp.dma_start(x_all[:, bass.ds(ST * n, ST), :], sums_v[0][n]).then_inc(S["sum_in0"], 16)
                if half:
                    hold(sp, S["x2_set"], b + 1)
                sp.dma_start(x_add[:, bass.ds(ST * b, ST), :], sums_v[1][n]).then_inc(S["sum_in1"], 16)
                hold(sp, S["sum_in0"], 16 * n + 16)
                hold(sp, S["sum_in1"], 16 * n + 16)

            def store(b):
                if isinstance(b, int) and b == BATCH - 1:
                    for j in range(ST):
                        sp.wait_ge(S["acc_set"], E1 * b + E1 + j)
                        sp.dma_start(out_v[b][:, j, :], o_rows[:, j, :]).then_inc(S["o_out"], 16)
                    return
                at_least(sp, S["acc_set"], E1 * b + E1)
                sp.dma_start(out_v[b], o_rows[:]).then_inc(S["o_out"], 16)

            for half in range(2):
                with sp.Fori(0, HALF) as b:
                    load_x(b, half)
            with sp.Fori(0, BATCH - 1) as b:
                store(b)
            store(BATCH - 1)
            sp.wait_ge(S["o_out"], 16 * (BATCH - 1 + ST))

        @block.gpsimd
        def _(pool):
            pool.memset(half[:], -0.5).then_inc(S["half_set"], 1)
            pool.memset(zrow[:], 0.0).then_inc(S["place_set"], 1)
            pool.memset(lo[:], float(np.exp(-50.0))).then_inc(S["half_set"], 1)
            pool.wait_ge(S["ctx_in"], 16)
            cv = cT[:].rearrange("p k (b c) -> p (k b) c", c=CTX)
            dv = cdup[:].rearrange("p k b a c -> p (k b) a c")
            for a in range(2):
                pool.tensor_copy(dv[:, :, a, :], cv).then_inc(S["cdup_set"], 1)
            for v in v_blk:
                pool.memset(v[:], 0.0).then_inc(S["vblk_zero"], 1)
            pool.memset(slots[:], 0.0).then_inc(S["place_set"], 1)
            pool.memset(slot_b[:], 0.0).then_inc(S["place_set"], 1)
            pool.memset(selsum[:], 0.0).then_inc(S["place_set"], 1)
            pool.memset(ones_b[:], 1.0).then_inc(S["place_set"], 1)
            def rstd(b, mv_set, mv, ve, ve_set, out_, out_set):
                hold(pool, mv_set, 2 * b + 2)
                pool.tensor_scalar(ve[:], mv[:, :, 1], EPS, None, ALU.add).then_inc(ve_set, 1)
                at_least(pool, ve_set, b + 1)
                pool.tensor_tensor(out_[:], ve[:], half[:], ALU.pow).then_inc(out_set, 1)

            def a_rstd(b):
                rstd(b, S["mv_a_set"], mv_a, ve_a, S["ve_a_set"], rstd_a, S["rstd_a_set"])

            def a_keys(b):
                hold(pool, S["s_mm"], 8 * b)
                src = kT[0].rearrange("p m (b c) -> p m b c", c=CTX)
                for a in range(2):
                    head = cst[:, C_HEAD2 + a:C_HEAD2 + a + 1, None].broadcast_to([P, KC, CTX])
                    pool.tensor_tensor(k_blk[:, :, a, :], src[:, :, b, :], head, ALU.mult).then_inc(S["k_set"], 1)

            def b_beta(b):
                hold(pool, S["x1_set"], 2 * b)
                for j in range(ST):
                    pool.tensor_tensor(xbeta[:, j, :], x_all[:, ST * b + j, :], beta[:], ALU.add)\
                        .then_inc(S["xbeta_set"], 1)

            def b_rstd(b):
                hold(pool, S["mv_d_set"], 2 * b + 2)
                pool.tensor_scalar(ve_d[:], mv_d[:, :, 1], rs2[:, 0:1], EPS, ALU.mult, ALU.add)\
                    .then_inc(S["ve_d_set"], 1)
                at_least(pool, S["ve_d_set"], b + 1)
                pool.tensor_tensor(ve_d[:], ve_d[:], half[:], ALU.pow).then_inc(S["pow_d_set"], 1)
                hold(pool, S["pow_d_set"], b + 1)
                pool.tensor_scalar(rstd_d[:], ve_d[:], rs[:, 0:1], None, ALU.mult).then_inc(S["rstd_d_set"], 1)

            def b_rstd2(b):
                rstd(b, S["mv_h_set"], mv_h, ve_h, S["ve_h_set"], rstd_h, S["rstd_h_set"])

            def c_place(part):
                n = QG // 3
                pool.iota(place[:, n * part:n * part + n], [[0, n], [1, CAP], [0, EPG]], base=0, channel_multiplier=0,
                          allow_small_or_imprecise_dtypes=True).then_inc(S["place_set"], 1)

            def body(b, stages=range(5)):
                if 2 in stages:
                    b_rstd2(b - 2)
                if 0 in stages:
                    a_rstd(b)
                    a_keys(b)
                if isinstance(b, int) and b < 3:
                    c_place(b)
                if 1 in stages:
                    b_beta(b - 1)
                    b_rstd(b - 1)

            pool.wait_ge(S["kT_set"], 2)
            pool.wait_ge(S["rs_set"], 2)
            pool.wait_ge(S["half_set"], 2)
            for b in range(0, 5):
                body(b, range(b + 1))
            with pool.Fori(5, BATCH) as b:
                body(b)
            for b in range(BATCH, BATCH + 4):
                body(b, range(b - BATCH + 1, 5))

            pool.wait_ge(S["l1_w_in"], 64)
            wn = wk1n[:].rearrange("p k (g d) -> p (k g) d", d=DH)
            we = wk1[:].rearrange("p k (g h d) -> p (k g) h d", g=GROUPS, d=DH)
            for h in range(HEADS // GROUPS):
                pool.tensor_copy(we[:, :, h, :], wn).then_inc(S["wk1_set"], 1)

            def fetch(i, h, experts):
                q = TURN * i + h
                hold(pool, S["take_set"], q + 1)
                hold(pool, S["xb_T"], q - TURN + 1)
                hold(pool, S["wpick_set"], q - TURN + 1)
                for e in experts:
                    pool.indirect_dma_start(xb[h][:, e, :], None, rows_d,
                                            bass.IndirectOffsetOnAxis(ap=take[h][:, e:e + 1], axis=0))\
                        .then_inc(S[f"gather{h}"], 16)

            def add(i, h, experts):
                q = TURN * i + h
                hold(pool, S["give_set"], q + 1)
                for e in experts:
                    c, n = e // 2, e % 2
                    hold(pool, S["yv_set" if e < 2 else "ya_set"], 2 * q + n + 1)
                    hold(pool, S[f"scatter{c}"], 16 * ((EPG // 2) * q + n))
                    pool.indirect_dma_start(sums_d[c], bass.IndirectOffsetOnAxis(ap=give[h][:, e:e + 1], axis=0),
                                            y[h][:, e, :], None, compute_op=ALU.add).then_inc(S[f"scatter{c}"], 16)

            pool.wait_ge(S["route_done"], 1)
            pool.wait_ge(S["x1_out"], 16 * BATCH)
            pool.wait_ge(S["h_out"], 16 * BATCH)
            pool.wait_ge(S["w_out"], 16 * BATCH)
            pool.wait_ge(S["zero_out"], 16 * (3 + TOKENS // P))
            def experts(i, h, last=False):
                for part in ((0, 2), (1, 3)):
                    add(i, h, part)
                    if not last:
                        fetch(i + 1, h, part)

            for h in range(TURN):
                fetch(0, h, range(EPG))
            for h in range(TURN):
                experts(0, h)
            with pool.Fori(1, QG // TURN - 1) as i:
                for h in range(TURN):
                    experts(i, h)
            for h in range(TURN):
                experts(QG // TURN - 1, h, last=True)

            def a1_x(b):
                hold(pool, S["sum_in0"], 16 * b + 16)
                hold(pool, S["sum_in1"], 16 * b + 16)
                x = x_all[:, bass.ds(ST * b, ST), :]
                pool.tensor_tensor(x, x, x_add[:, bass.ds(ST * (b % HALF), ST), :], ALU.add).then_inc(S["x2_set"], 1)

            def a1_keys(b):
                hold(pool, S["s1_mm"], 4 * b)
                src = kT[1].rearrange("p m (b c) -> p m b c", c=CTX)
                for m in range(KC):
                    pool.tensor_tensor(k1_blk[:, m], src[:, m, b, None, :].broadcast_to([P, 8, CTX]),
                                       cst[:, C_HEAD8:C_HEAD8 + 8, None].broadcast_to([P, 8, CTX]), ALU.mult)\
                        .then_inc(S["k1_set"], 1)

            def a1_rstd(b):
                rstd(BATCH + b, S["mv_a_set"], mv_a, ve_a, S["ve_a_set"], rstd_a, S["rstd_a_set"])

            def b1_rstd(b):
                rstd(BATCH + b, S["mv_h_set"], mv_h, ve_h, S["ve_h_set"], rstd_h, S["rstd_h_set"])

            def d1_low(b, e):
                hold(pool, S["act1h_set"], E1 * b + e + 1)
                hold(pool, S["down1_mm"], E1 * b + e - 1)
                pool.tensor_tensor(act1_low[e % 2][:].bitcast(F32R), act1[e % 2][:], act1_high[e % 2][:], ALU.subtract)\
                    .then_inc(S["act1l_set"], 1)

            def layer1(b, stages=range(5)):
                if 4 in stages:
                    d1_low(b - 4, 7)
                if 1 in stages:
                    a1_keys(b - 1)
                if 0 in stages:
                    a1_rstd(b)
                if 3 in stages:
                    for e in range(6):
                        d1_low(b - 3, e)
                if 2 in stages:
                    b1_rstd(b - 2)
                if 3 in stages:
                    d1_low(b - 3, 6)

            pool.wait_ge(S["kT_set"], 4)
            for b in range(5):
                for n in ((0,), (1, 2), (3, 4), (5, 6), (7,))[b]:
                    a1_x(n)
                layer1(b, range(b + 1))
            with pool.Fori(5, BATCH) as b:
                layer1(b)
            for b in range(BATCH, BATCH + 4):
                layer1(b, range(b - BATCH + 1, 5))

        @block.scalar
        def _(act):
            for n, v in ((bq0, "bq0"), (bk0, "bk0"), (mask_i, "mask0")):
                act.dma_start(n[:], t[v]).then_inc(S["bias_in"], 16)
            for n, v in ((bv0, "bv0"), (bo0, "bo0"), (gamma, "gamma"), (beta, "beta"), (rs, "rs")):
                act.dma_start(n[:], t[v].partition_broadcast(P)).then_inc(S["bias_in"], 16)
            act.dma_start(o2n_c[:], t["o2n"].rearrange("(p o) -> p o", o=1)).then_inc(S["route_in"], 16)
            act.dma_start(o2n_r[:], t["o2n"].partition_broadcast(P)).then_inc(S["route_in"], 16)
            act.dma_start(mask_u[:], t["mask1"]).then_inc(S["mask_u_in"], 16)
            act.dma_start(bias_q[:], t["bias_q"]).then_inc(S["bias_q_in"], 16)
            act.dma_start(gate1[:], t["gate1"]).then_inc(S["gate1_in"], 16)
            act.wait_ge(S["hi_set"], 1)
            act.activation(hi[:], hi[:], ACT.Exp).then_inc(S["bound_set"], 1)

            def c_hT(b):
                at_least(act, S["h_T"], b + 1)
                at_least(act, S["l_mm"], b)
                act.activation(hT[:].rearrange("p k s -> p (k s)"), banks[6][:, :], ACT.Copy).then_inc(S["hT_set"], 1)

            def b_exp(b, j):
                at_least(act, S["s_mm"], 8 * b + 2 * j + 2)
                at_least(act, S["pv_mm"], 2 * b)
                act.activation(prob[:, j].rearrange("p m s -> p (m s)"), banks[1 + j % 2][:, :], ACT.Exp,
                               scale=DH ** -0.5).then_inc(S["exp_set"], 1)

            def a_hsT(b):
                at_least(act, S["hs_T"], b + 1)
                at_least(act, S["q_mm"], b)
                act.activation(hsT[:].rearrange("p k s -> p (k s)"), banks[0][:, :], ACT.Copy)\
                    .then_inc(S["hsT_set"], 1)

            def a_q(b):
                at_least(act, S["q_mm"], b + 1)
                at_least(act, S["s_mm"], 8 * b)
                for m in range(KC):
                    act.activation(qT[:, m, :], banks[0][:, SEQ * m:SEQ * m + SEQ], ACT.Identity,
                                   bias=bq0[:, m:m + 1]).then_inc(S["q_set"], 1)

            def c_exp(b):
                at_least(act, S["ntop_set"], b + 1)
                at_least(act, S["wsel_set"], 2 * b)
                for j in range(ST):
                    act.activation(expl[:, j, :], logit[:, j, :], ACT.Exp, bias=ntop[:, j:j + 1])\
                        .then_inc(S["expl_set"], 1)
                    act.activation(etop[:, j, :], top[:, j, :], ACT.Exp, bias=ntop[:, j:j + 1],
                                   accum_out=den[:, j:j + 1]).then_inc(S["etop_set"], 1)

            def b_attT(b):
                at_least(act, S["att_T"], b + 1)
                at_least(act, S["o_mm"], b)
                act.activation(attT[:].rearrange("p k s -> p (k s)"), banks[5][:, :], ACT.Copy)\
                    .then_inc(S["attT_set"], 1)

            def c_wT(b):
                at_least(act, S["countT_set"], b + 1)
                at_least(act, S["pos_mm"], b)
                act.activation(wselT[:].rearrange("p j s -> p (j s)"), banks[6][:, 256:512], ACT.Copy)\
                    .then_inc(S["wselT_set"], 1)

            def c_w(b):
                at_least(act, S["pos_set"], b + 1)
                at_least(act, S["den_set"], b + 1)
                at_least(act, S["w_out"], 16 * b)
                for j in range(ST):
                    act.activation(w_rows[:, j, :], banks[7][:, 96 + NEW * j:96 + NEW * j + NEW], ACT.Copy,
                                   scale=rdn[:, j:j + 1]).then_inc(S["w_set"], 1)

            def body(b, stages=range(5)):
                if 1 in stages:
                    b_exp(b - 1, 0)
                    b_exp(b - 1, 1)
                if 3 in stages:
                    c_w(b - 3)
                if 2 in stages:
                    c_hT(b - 2)
                if 1 in stages:
                    b_exp(b - 1, 2)
                    b_exp(b - 1, 3)
                if 2 in stages:
                    c_exp(b - 2)
                if 1 in stages:
                    b_attT(b - 1)
                if 0 in stages:
                    a_hsT(b)
                if 2 in stages:
                    c_wT(b - 2)
                if 0 in stages:
                    a_q(b)

            act.wait_ge(S["bias_in"], 16 * 8)
            for b in range(0, 5):
                body(b, range(b + 1))
            with act.Fori(5, BATCH) as b:
                body(b)
            for b in range(BATCH, BATCH + 4):
                body(b, range(b - BATCH + 1, 5))

            act.wait_ge(S["mask_b_set"], 1)
            act.wait_ge(S["pv_mm"], 2 * BATCH)
            act.wait_ge(S["k_set"], 2 * BATCH)
            for b in range(BATCH):
                act.dma_start(bias_k[0:1, b].rearrange("p (h c) -> p h c", c=CTX),
                              mask_b[:, b].broadcast_to([1, HEADS, CTX])).then_inc(S["mask1_in"], 16)

            def x0_T(i, h):
                q = TURN * i + h
                at_least(act, S["xb_T"], q + 1)
                at_least(act, S["gu0_mm"], 2 * q)
                act.activation(xbT[:, 0, :], banks[0][:, 0:EPG * CAP], ACT.Copy).then_inc(S["xbT_set"], 1)

            def silu(i, h):
                q = TURN * i + h
                for u in range(2):
                    at_least(act, S["gu0_mm"], 2 * q + u + 1)
                    at_least(act, S["act0_set"], 2 * q + u - 1)
                    src = banks[2 + u][0:INTER0, 0:2 * 2 * CAP].rearrange("i (e s c) -> i e s c", e=2, s=2)
                    act.activation(silu0[:, 2 * u:2 * u + 2, :], src[:, :, 0, :], ACT.Silu).then_inc(S["silu0_set"], 1)

            def y0(i, h):
                q = TURN * i + h
                at_least(act, S["wslot_set"], q + 1)
                at_least(act, S["y_mm"], 2 * q + 2)
                for c in range(2):
                    at_least(act, S[f"scatter{c}"], 16 * (EPG // 2) * (q - TURN + 1))
                for e in range(2, EPG):
                    act.activation(y[h][:, e, :], banks[5][0:CAP, D * (e - 2):D * (e - 2) + D], ACT.Copy,
                                   scale=wslot[h][:, e:e + 1]).then_inc(S["ya_set"], 1)

            def experts(i, h, i1, h1, first=False, last=False):
                if not first:
                    y0(i, h)
                if not last:
                    x0_T(i1, h1)
                    silu(i1, h1)

            experts(-1, TURN - 1, 0, 0, first=True)
            for h in range(TURN):
                experts(0, h, *((0, h + 1) if h + 1 < TURN else (1, 0)))
            with act.Fori(1, QG // TURN - 1) as i:
                for h in range(TURN):
                    experts(i, h, *((i, h + 1) if h + 1 < TURN else (i + 1, 0)))
            for h in range(TURN):
                experts(QG // TURN - 1, h, QG // TURN - 1, h + 1, last=h == TURN - 1)

            def a1_hsT(b):
                at_least(act, S["hs_T"], BATCH + b + 1)
                at_least(act, S["q_mm"], BATCH + b)
                act.activation(hsT[:].rearrange("p k s -> p (k s)"), banks[0][:, :], ACT.Copy)\
                    .then_inc(S["hsT_set"], 1)

            def a1_q(b):
                at_least(act, S["q_mm"], BATCH + b + 1)
                at_least(act, S["s1_mm"], 4 * b)
                act.activation(qT[:].rearrange("p k s -> p (k s)"), banks[0][:, :], ACT.Copy,
                               scale=DH ** -0.5).then_inc(S["q_set"], 1)

            def b1_exp(b, u):
                at_least(act, S["sub_set"], 4 * b + u + 1)
                act.activation(soft[:, u, :], soft[:, u, :], ACT.Exp).then_inc(S["soft_set"], 1)

            def b1_softT(b, u):
                at_least(act, S["soft_T"], 4 * b + u + 1)
                at_least(act, S["pv_mm"], ST * (BATCH + b))
                act.activation(softT[:, u, :], banks[SOFT_BANK[u]][:, :], ACT.Copy).then_inc(S["softT_set"], 1)

            def b1_attT(b):
                at_least(act, S["att_T"], BATCH + b + 1)
                at_least(act, S["o_mm"], BATCH + b)
                act.activation(attT[:].rearrange("p k s -> p (k s)"), banks[0][:, :], ACT.Copy)\
                    .then_inc(S["attT_set"], 1)

            def c1_hT(b):
                at_least(act, S["h1_T"], b + 1)
                at_least(act, S["l1_mm"], b)
                at_least(act, S["hT1_set"], b)
                act.activation(hTr[:].rearrange("p k s -> p (k s)"), banks[3][:, :], ACT.Copy).then_inc(S["hTr_set"], 1)

            def c1_exp(b):
                at_least(act, S["gap_set"], b + 1)
                act.activation(egap[:], gap[:], ACT.Exp).then_inc(S["egap_set"], 1)

            def d1_silu(b, e):
                at_least(act, S["gu1_mm"], E1 * b + e + 1)
                at_least(act, S["act1_set"], E1 * b + e - 1)
                act.activation(silu1[e % 2][:], banks[5 + e % 2][:, 0:SEQ], ACT.Silu).then_inc(S["silu1_set"], 1)

            def layer1(b, stages=range(5)):
                if 2 in stages:
                    b1_exp(b - 2, 0)
                    b1_exp(b - 2, 1)
                if 3 in stages:
                    c1_exp(b - 3)
                if 2 in stages:
                    b1_exp(b - 2, 2)
                if 1 in stages:
                    a1_hsT(b - 1)
                if 2 in stages:
                    b1_exp(b - 2, 3)
                    b1_softT(b - 2, 0)
                    b1_softT(b - 2, 1)
                if 3 in stages:
                    d1_silu(b - 3, 0)
                    d1_silu(b - 3, 1)
                if 1 in stages:
                    a1_q(b - 1)
                if 2 in stages:
                    b1_softT(b - 2, 2)
                    b1_softT(b - 2, 3)
                if 3 in stages:
                    for e in range(2, 5):
                        d1_silu(b - 3, e)
                if 2 in stages:
                    b1_attT(b - 2)
                if 3 in stages:
                    d1_silu(b - 3, 5)
                    d1_silu(b - 3, 6)
                    d1_silu(b - 3, 7)
                if 2 in stages:
                    c1_hT(b - 2)

            for b in range(0, 5):
                layer1(b, range(b + 1))
            with act.Fori(5, BATCH) as b:
                layer1(b)
            for b in range(BATCH, BATCH + 4):
                layer1(b, range(b - BATCH + 1, 5))

        @block.tensor
        def _(pe):
            pe.wait_ge(S["ctx_in"], 16)
            pe.wait_ge(S["kv_w_in"], 32)
            for m in range(KC):
                for k in range(KC):
                    mm = pe.matmul(banks[m][:, :], wk0[:, k, P * m:P * m + P], cT[:, k, :], start=k == 0, stop=k == KC - 1)
                mm.then_inc(S["kT_mm"], 1)
            pe.wait_ge(S["cdup_set"], 2)
            for b in range(BATCH):
                for k in range(KC):
                    mm = pe.matmul(banks[2 + b // 2][:, D * (b % 2):D * (b % 2) + D],
                                   cdup[:, k, b].rearrange("p a c -> p (a c)"), wv0[:, k, :],
                                   start=k == 0, stop=k == KC - 1)
                if b % 2:
                    mm.then_inc(S["v_mm"], 1)
            def a_T(b):
                at_least(pe, S["hs_set"], b + 1)
                at_least(pe, S["q_set"], 2 * b)
                for j in range(ST):
                    for k in range(KC):
                        mm = pe.transpose(banks[0][:, SEQ * k + P * j:SEQ * k + P * j + P], hs[:, j, P * k:P * k + P], ident)
                mm.then_inc(S["hs_T"], 1)

            def a_q(b, m):
                at_least(pe, S["hsT_set"], b + 1)
                for k in range(KC):
                    mm = pe.matmul(banks[0][:, SEQ * m:SEQ * m + SEQ], wq0[:, k, P * m:P * m + P], hsT[:, k, :],
                                   start=k == 0, stop=k == KC - 1)
                if m == KC - 1:
                    mm.then_inc(S["q_mm"], 1)

            def b_s(b, j):
                at_least(pe, S["exp_set"], 4 * b + j - 1)
                if j == 0:
                    at_least(pe, S["q_set"], 2 * b + 2)
                    at_least(pe, S["k_set"], 2 * b + 2)
                for m in range(KC):
                    rows = slice(32 * j, 32 * j + 32)
                    pe.matmul(banks[1 + j % 2][:, SEQ * m:SEQ * m + SEQ],
                              k_blk[rows, m].rearrange("p a c -> p (a c)"), qT[rows, m, :],
                              start=True, stop=True).then_inc(S["s_mm"], 1)

            def b_pv(b, j):
                at_least(pe, S["clip_set"], 4 * b + 4)
                if j == 0:
                    at_least(pe, S["att_set"], 2 * b - 1)
                else:
                    at_least(pe, S["w_set"], 2 * (b - 1))
                for r in range(PAIRS):
                    mm = pe.matmul(banks[PV_BANK[j]][:, 2 * VW * r:2 * VW * r + 2 * VW], prob[:, r % 4, r // 4, P * j:P * j + P],
                                   v_blk[0][:, b, r].rearrange("p a d -> p (a d)"), start=True, stop=True)
                mm.then_inc(S["pv_mm"], 1)

            def b_T(b):
                at_least(pe, S["att_set"], 2 * b + 2)
                at_least(pe, S["delta_set"], b)
                for j in range(ST):
                    for k in range(KC):
                        mm = pe.transpose(banks[5][:, SEQ * k + P * j:SEQ * k + P * j + P], att[:, j, P * k:P * k + P], ident)
                mm.then_inc(S["att_T"], 1)

            def b_o(b):
                at_least(pe, S["attT_set"], b + 1)
                for j in range(ST):
                    for k in range(KC):
                        mm = pe.matmul(banks[5][:, D * j:D * j + D], attT[:, k, P * j:P * j + P], wo0[:, k, :],
                                       start=k == 0, stop=k == KC - 1)
                mm.then_inc(S["o_mm"], 1)

            def c_T(b):
                at_least(pe, S["h_set"], 2 * b + 2)
                at_least(pe, S["wselT_set"], b)
                at_least(pe, S["countT_set"], b)
                for j in range(ST):
                    for k in range(KC):
                        mm = pe.transpose(banks[6][:, SEQ * k + P * j:SEQ * k + P * j + P], h_rows[:, j, P * k:P * k + P], ident)
                mm.then_inc(S["h_T"], 1)

            def c_l(b):
                at_least(pe, S["hT_set"], b + 1)
                for j in range(ST):
                    for k in range(KC):
                        mm = pe.matmul(banks[6][:, OLD * j:OLD * j + OLD], hT[:, k, P * j:P * j + P], gate0[:, k, :],
                                       start=k == 0, stop=k == KC - 1)
                mm.then_inc(S["l_mm"], 1)

            def c_count(b):
                at_least(pe, S["sel_set"], b + 1)
                at_least(pe, S["selsum_set"], 2 * b)
                at_least(pe, S["logit_set"], b + 1)
                for j in range(ST):
                    o = banks[6][:, P * j:P * j + P]
                    pe.matmul(o, selsum[:] , ones_b[:], start=True, stop=False)
                    if j == 1:
                        pe.matmul(o, sel[:, 0, :], ones_b[:], start=False, stop=False)
                    mm = pe.matmul(o, sel[:, j, :], tri[:], start=False, stop=True)
                mm.then_inc(S["count_mm"], 1)

            def c_wT(b):
                at_least(pe, S["wsel_set"], 2 * b + 2)
                for j in range(ST):
                    mm = pe.transpose(banks[6][:, 256 + P * j:256 + P * j + P], wsel[:, j, :], ident)
                mm.then_inc(S["wsel_T"], 1)

            def c_pos(b):
                at_least(pe, S["countT_set"], b + 1)
                at_least(pe, S["wselT_set"], b + 1)
                at_least(pe, S["w_set"], 2 * b)
                if not (isinstance(b, int) and b == BATCH - 1):
                    at_least(pe, S["att_set"], 2 * (b + 1) + 2)
                for j in range(ST):
                    pe.matmul(banks[7][:, NEW * j:NEW * j + NEW], countT[:, j, :], map_b[:], start=True, stop=True)
                    mm = pe.matmul(banks[7][:, 96 + NEW * j:96 + NEW * j + NEW], wselT[:, j, :], map_f[:],
                                   start=True, stop=True)
                mm.then_inc(S["pos_mm"], 1)

            def d_slots(b, part):
                if part == 0:
                    at_least(pe, S["signed_set"], b + 1)
                    at_least(pe, S["slotb_acc"], b)
                    at_least(pe, S["slot_acc"], b)
                for n in range(NEW // 4 * part, NEW // 4 * (part + 1)):
                    mm = pe.matmul(banks[4][0:CAP, 2 * n:2 * n + 2], hit[:, 1, n // EPG, :, n % EPG], loc1[:],
                                   start=n == 0, stop=True, skip_group_check=True)
                if part == 3:
                    mm.then_inc(S["slot_mm"], 1)

            def body(b, stages=range(5)):
                if 4 in stages:
                    d_slots(b - 4, 0)
                if 1 in stages:
                    b_s(b - 1, 0)
                    b_s(b - 1, 1)
                if 4 in stages:
                    d_slots(b - 4, 1)
                if 1 in stages:
                    b_s(b - 1, 2)
                if 4 in stages:
                    d_slots(b - 4, 2)
                if 1 in stages:
                    b_s(b - 1, 3)
                if 2 in stages:
                    c_T(b - 2)
                if 4 in stages:
                    d_slots(b - 4, 3)
                if 2 in stages:
                    c_l(b - 2)
                if 1 in stages:
                    b_pv(b - 1, 0)
                    b_pv(b - 1, 1)
                if 2 in stages:
                    c_count(b - 2)
                if 1 in stages:
                    b_T(b - 1)
                if 0 in stages:
                    a_T(b)
                if 2 in stages:
                    c_wT(b - 2)
                if 1 in stages:
                    b_o(b - 1)
                if 0 in stages:
                    a_q(b, 0)
                    a_q(b, 1)
                if 2 in stages:
                    c_pos(b - 2)

            pe.wait_ge(S["cst_in"], 16)
            pe.wait_ge(S["q_w_in"], 48)
            pe.wait_ge(S["kT_set"], 2)
            for b in range(0, 5):
                if b == 1:
                    pe.wait_ge(S["v_set"], 8)
                    pe.wait_ge(S["vblk_ones"], 4)
                if b == 2:
                    pe.wait_ge(S["tri_set"], 1)
                    pe.wait_ge(S["place_set"], 5)
                    pe.wait_ge(S["map_set"], 4)
                    pe.wait_ge(S["loc_set"], 2)
                body(b, range(b + 1))
            with pe.Fori(5, BATCH) as b:
                body(b)
            for b in range(BATCH, BATCH + 4):
                body(b, range(b - BATCH + 1, 5))

            pe.wait_ge(S["wk1_set"], 4)
            pe.wait_ge(S["q_set"], 2 * BATCH)
            pe.wait_ge(S["exp_set"], 4 * BATCH)
            pe.wait_ge(S["wselT_set"], BATCH)
            pe.wait_ge(S["l1_w_in"], 64)
            for m in range(KC):
                for k in range(KC):
                    mm = pe.matmul(banks[m][:, :], wk1[:, k, P * m:P * m + P], cT[:, k, :], start=k == 0, stop=k == KC - 1)
                mm.then_inc(S["kT_mm"], 1)
            for b in range(BATCH):
                for k in range(KC):
                    mm = pe.matmul(banks[6][:, CTX * b:CTX * b + CTX], cdup[:, k, b].rearrange("p a c -> p (a c)"),
                                   wv1[:, k, :], start=k == 0, stop=k == KC - 1)
            mm.then_inc(S["v_mm"], 1)

            def x0_T(i, h):
                q = TURN * i + h
                at_least(pe, S[f"gather{h}"], 16 * EPG * (i + 1))
                at_least(pe, S["xbT_set"], 2 * q)
                for k in range(KC):
                    for e in range(EPG):
                        mm = pe.transpose(banks[k][:, CAP * e:CAP * e + CAP], xb[h][:, e, P * k:P * k + P],
                                          ident[0:CAP, 0:CAP])
                mm.then_inc(S["xb_T"], 1)

            def gu(i, h):
                q = TURN * i + h
                at_least(pe, S["xbT_set"], 2 * q + 2)
                at_least(pe, S["act0_set"], 2 * q)
                at_least(pe, S[f"w0_ld{h}"], 32 * (i + 1))
                for e in range(EPG):
                    for s in range(2):
                        o = CAP * (2 * (e % 2) + s)
                        for k in range(KC):
                            mm = pe.matmul(banks[2 + e // 2][0:INTER0, o:o + CAP],
                                           gu0[h][:, k, e, INTER0 * s:INTER0 * s + INTER0], xbT[:, k, CAP * e:CAP * e + CAP],
                                           start=k == 0, stop=k == KC - 1)
                    if e % 2:
                        mm.then_inc(S["gu0_mm"], 1)

            def down(i, h):
                q = TURN * i + h
                for e in range(EPG):
                    if e % 2 == 0:
                        at_least(pe, S["act0_set"], 2 * q + e // 2 + 1)
                        at_least(pe, S["ya_set" if e else "yv_set"], 2 * q)
                    mm = pe.matmul(banks[4 + e // 2][0:CAP, D * (e % 2):D * (e % 2) + D], act0[:, e, :],
                                   down0[h][:, e, :], start=True, stop=True)
                    if e % 2:
                        mm.then_inc(S["y_mm"], 1)

            def experts(i, h, i1, h1, first=False, last=False):
                if not first:
                    down(i, h)
                if not last:
                    x0_T(i1, h1)
                    gu(i1, h1)

            pe.wait_ge(S["route_done"], 1)
            pe.wait_ge(S["w_set"], 2 * BATCH)
            pe.wait_ge(S["kT_set"], 4)
            experts(-1, TURN - 1, 0, 0, first=True)
            for h in range(TURN):
                experts(0, h, *((0, h + 1) if h + 1 < TURN else (1, 0)))
            with pe.Fori(1, QG // TURN - 1) as i:
                for h in range(TURN):
                    experts(i, h, *((i, h + 1) if h + 1 < TURN else (i + 1, 0)))
            for h in range(TURN):
                experts(QG // TURN - 1, h, QG // TURN - 1, h + 1, last=h == TURN - 1)

            def a1_T(b):
                at_least(pe, S["hs_set"], BATCH + b + 1)
                at_least(pe, S["x3_set"], b - 1)
                for j in range(ST):
                    for k in range(KC):
                        mm = pe.transpose(banks[0][:, SEQ * k + P * j:SEQ * k + P * j + P], hs[:, j, P * k:P * k + P], ident)
                mm.then_inc(S["hs_T"], 1)

            def a1_q(b):
                at_least(pe, S["hsT_set"], BATCH + b + 1)
                for m in range(KC):
                    for k in range(KC):
                        mm = pe.matmul(banks[0][:, SEQ * m:SEQ * m + SEQ], wq1[:, k, P * m:P * m + P], hsT[:, k, :],
                                       start=k == 0, stop=k == KC - 1)
                mm.then_inc(S["q_mm"], 1)

            def b1_s(b, u):
                j, m = u // KC, u % KC
                if u < 2:
                    at_least(pe, S["softT_set"], 4 * (b - 1) + u + 2)
                else:
                    at_least(pe, S["sub_set"], 4 * b + u - 1)
                if u == 0:
                    at_least(pe, S["q_set"], 2 * BATCH + b + 1)
                    at_least(pe, S["k1_set"], KC * b + KC)
                o = banks[1 + u % 2][:, :]
                pe.matmul(o, qT[:, m, P * j:P * j + P], k1_blk[:, m].rearrange("p h c -> p (h c)"), start=True,
                          stop=False)
                pe.matmul(o, bias_q[:, P * j:P * j + P], bias_k[:, b, 512 * m:512 * m + 512], start=False, stop=True)\
                    .then_inc(S["s1_mm"], 1)

            def b1_T(b, u):
                at_least(pe, S["soft_set"], 4 * b + u + 1)
                if u == 0:
                    at_least(pe, S["logit1_set"], b)
                else:
                    at_least(pe, S["sub_set"], 4 * b + min(u + 2, 4))
                if u == 3:
                    at_least(pe, S["softT_set"], 4 * b + 1)
                for r in range(4):
                    mm = pe.transpose(banks[SOFT_BANK[u]][:, P * r:P * r + P], soft[:, u, P * r:P * r + P], ident)
                mm.then_inc(S["soft_T"], 1)

            def b1_pv(b, j):
                at_least(pe, S["softT_set"], 4 * b + 2 * j + 2)
                at_least(pe, S["att_set"], ST * (BATCH + b) + j)
                for r in range(PAIRS):
                    mm = pe.matmul(banks[4][:, 2 * VW * r:2 * VW * r + 2 * VW],
                                   softT[:, 2 * j + r // 4, P * (r % 4):P * (r % 4) + P],
                                   v_blk[1][:, b, r].rearrange("p a d -> p (a d)"), start=True, stop=True)
                mm.then_inc(S["pv_mm"], 1)

            def b1_T2(b):
                at_least(pe, S["att_set"], ST * (BATCH + b) + ST)
                if not (isinstance(b, int) and b == BATCH - 1):
                    at_least(pe, S["q_set"], 2 * BATCH + b + 2)
                for j in range(ST):
                    for k in range(KC):
                        mm = pe.transpose(banks[0][:, SEQ * k + P * j:SEQ * k + P * j + P], att[:, j, P * k:P * k + P], ident)
                mm.then_inc(S["att_T"], 1)

            def b1_o(b):
                at_least(pe, S["attT_set"], BATCH + b + 1)
                for j in range(ST):
                    for k in range(KC):
                        mm = pe.matmul(banks[0][:, D * j:D * j + D], attT[:, k, P * j:P * j + P], wo1[:, k, :],
                                       start=k == 0, stop=k == KC - 1)
                mm.then_inc(S["o_mm"], 1)

            def c1_T(b):
                at_least(pe, S["h_set"], 2 * (BATCH + b) + 2)
                at_least(pe, S["softT_set"], 4 * b + 4)
                for j in range(ST):
                    for k in range(KC):
                        mm = pe.transpose(banks[3][:, SEQ * k + P * j:SEQ * k + P * j + P], h_rows[:, j, P * k:P * k + P], ident)
                mm.then_inc(S["h1_T"], 1)

            def c1_l(b):
                at_least(pe, S["hTr_set"], b + 1)
                for j in range(ST):
                    for k in range(KC):
                        mm = pe.matmul(banks[3][:, E1 * j:E1 * j + E1], hTr[:, k, P * j:P * j + P], gate1[:, k, :],
                                       start=k == 0, stop=k == KC - 1)
                mm.then_inc(S["l1_mm"], 1)

            def d1_gu(b, e):
                at_least(pe, S["act1_set"], E1 * b + e - 1)
                if e == 0:
                    at_least(pe, S["hT1_set"], b + 1)
                o = banks[5 + e % 2]
                for n in range(2):
                    for k in range(KC):
                        mm = in_parts(pe, o[:, SEQ * n:SEQ * n + SEQ], (gu1_high[:, e, k, n, :], gu1_low[e][:, k, n, :]),
                                      (hT1[:, k, :], hT1_low[:, k, :]), start=k == 0, stop=k == KC - 1)
                mm.then_inc(S["gu1_mm"], 1)

            def d1_down(b, e):
                at_least(pe, S["act1l_set"], E1 * b + e + 1)
                at_least(pe, S["acc_set"], E1 * b + e)
                for j in range(ST):
                    s = slice(P * j, P * j + P)
                    mm = in_parts(pe, banks[7][:, D * j:D * j + D], (act1_high[e % 2][:, s], act1_low[e % 2][:, s]),
                                  (down1_high[:, e, :], down1_low[e]), start=True, stop=True)
                mm.then_inc(S["down1_mm"], 1)

            def layer1(b, stages=range(5)):
                if 2 in stages:
                    b1_s(b - 2, 0)
                if 3 in stages:
                    c1_l(b - 3)
                if 4 in stages:
                    d1_down(b - 4, 7)
                if 2 in stages:
                    b1_s(b - 2, 1)
                if 3 in stages:
                    d1_gu(b - 3, 0)
                if 2 in stages:
                    b1_s(b - 2, 2)
                    b1_s(b - 2, 3)
                if 1 in stages:
                    a1_T(b - 1)
                if 3 in stages:
                    d1_gu(b - 3, 1)
                if 2 in stages:
                    b1_T(b - 2, 0)
                    b1_T(b - 2, 1)
                if 1 in stages:
                    a1_q(b - 1)
                if 2 in stages:
                    b1_T(b - 2, 2)
                    b1_T(b - 2, 3)
                    b1_pv(b - 2, 0)
                if 3 in stages:
                    d1_down(b - 3, 0)
                    d1_gu(b - 3, 2)
                    d1_down(b - 3, 1)
                    d1_gu(b - 3, 3)
                if 2 in stages:
                    b1_pv(b - 2, 1)
                if 3 in stages:
                    d1_down(b - 3, 2)
                    d1_gu(b - 3, 4)
                if 2 in stages:
                    b1_T2(b - 2)
                if 3 in stages:
                    d1_down(b - 3, 3)
                    d1_gu(b - 3, 5)
                    d1_down(b - 3, 4)
                if 2 in stages:
                    b1_o(b - 2)
                if 3 in stages:
                    d1_gu(b - 3, 6)
                    d1_down(b - 3, 5)
                    d1_gu(b - 3, 7)
                    d1_down(b - 3, 6)
                if 2 in stages:
                    c1_T(b - 2)

            pe.wait_ge(S["v_set"], 12)
            pe.wait_ge(S["gate1_in"], 16)
            pe.wait_ge(S["bias_q_in"], 16)
            pe.wait_ge(S["bias1_in"], 16)
            pe.wait_ge(S["mask1_in"], 16 * BATCH)
            pe.wait_ge(S["yv_set"], 2 * QG)
            pe.wait_ge(S["ya_set"], 2 * QG)
            for b in range(0, 5):
                if b == 3:
                    pe.wait_ge(S["wparts_set"], 2)
                layer1(b, range(b + 1))
            with pe.Fori(5, BATCH) as b:
                layer1(b)
            for b in range(BATCH, BATCH + 4):
                layer1(b, range(b - BATCH + 1, 5))

        @block.vector
        def _(dve):
            dve.wait_ge(S["bias_in"], 16 * 8)
            dve.tensor_scalar(hi[:], mask_i[:], 0.5, 100.0, ALU.is_gt, ALU.mult).then_inc(S["rs_set"], 1)
            dve.tensor_scalar(rs[:], rs[:], 0.0, 0.3, ALU.max, ALU.min).then_inc(S["rs_set"], 1)
            dve.wait_ge(S["rs_set"], 2)
            dve.tensor_scalar(hi[:], hi[:], -50.0, None, ALU.add).then_inc(S["hi_set"], 1)
            dve.tensor_tensor(rs2[:], rs[:], rs[:], ALU.mult).then_inc(S["rs_set"], 1)
            dve.wait_ge(S["mask_u_in"], 16)
            dve.tensor_scalar(mask_b[:].rearrange("p b o c -> p (b o c)"), mask_u[:], 1.0, -MASKED, ALU.subtract,
                              ALU.mult).then_inc(S["mask_b_set"], 1)
            dve.wait_ge(S["route_in"], 32)
            dve.wait_ge(S["cst_in"], 16)
            dve.tensor_copy(o2n_f[:], o2n_c[:]).then_inc(S["map_set"], 1)
            dve.tensor_scalar(unkept[:], o2n_r[:], -1.0, MASKED, ALU.is_equal, ALU.mult).then_inc(S["map_set"], 1)
            dve.tensor_copy(tri[:], cst[:, C_TRI:C_TRI + P]).then_inc(S["tri_set"], 1)
            dve.memset(loc1[:, 1:2], 1.0).then_inc(S["loc_set"], 1)
            dve.tensor_copy(loc1[:, 0:1], cst[:, C_LOC:C_LOC + 1]).then_inc(S["loc_set"], 1)
            dve.wait_ge(S["map_set"], 1)
            for m in (map_f, map_b):
                dve.tensor_scalar(m[:], cst[:, C_E48:C_E48 + NEW], o2n_f[:, 0:1], None, ALU.is_equal)\
                    .then_inc(S["map_set"], 1)
            for m in range(KC):
                dve.wait_ge(S["kT_mm"], m + 1)
                dve.tensor_scalar(kT[0][:, m, :], banks[m][:, :], bk0[:, m:m + 1], None, ALU.add).then_inc(S["kT_set"], 1)
            dve.wait_ge(S["vblk_zero"], 2)
            for v in v_blk:
                for a in range(2):
                    dve.memset(v[CTX * a:CTX * a + CTX, :, :, a, DH:VW], 1.0).then_inc(S["vblk_ones"], 1)
            for c in range(4):
                dve.wait_ge(S["v_mm"], c + 1)
                for a in range(2):
                    h = slice(CTX * a, CTX * a + CTX)
                    src = banks[2 + c][h, :].rearrange("p (b r a d) -> p b r a d", b=2, a=2, d=DH)
                    bias = bv0[h, :].rearrange("p (r a d) -> p r a d", a=2, d=DH)
                    for e in range(2):
                        ins = dve.tensor_tensor(v_blk[0][h, 2 * c + e, :, a, 0:DH], src[:, e, :, a, :],
                                                bias[:, :, a, :], ALU.add)
                    ins.then_inc(S["v_set"], 1)
            dve.wait_ge(S["bound_set"], 1)
            dve.wait_ge(S["place_set"], 5)

            def a_stat(b):
                hold(dve, S["x_in"], 16 * b + 16)
                for j in range(ST):
                    dve.bn_stats(stat6[:, j, :], x_all[:, ST * b + j, :]).then_inc(S["stat_a"], 1)
                hold(dve, S["stat_a"], 2 * b + 2)
                hold(dve, S["rstd_a_set"], b)
                for j in range(ST):
                    dve.bn_aggr(mv_a[:, j, :], stat6[:, j, :]).then_inc(S["mv_a_set"], 1)

            def a_norm(b):
                at_least(dve, S["rstd_a_set"], b + 1)
                at_least(dve, S["hs_T"], b)
                for j in range(ST):
                    ins = dve.tensor_scalar(hs[:, j, :], x_all[:, ST * b + j, :], mv_a[:, j, 0:1], rstd_a[:, j:j + 1],
                                            ALU.subtract, ALU.mult)
                ins.then_inc(S["hs_set"], 1)

            def b_clip(b, j):
                at_least(dve, S["exp_set"], 4 * b + j + 1)
                v = prob[:, j].rearrange("p m s -> p (m s)")
                dve.tensor_scalar(v, v, hi[:, b:b + 1] if isinstance(b, int) else hi[:, bass.ds(b, 1)], lo[:, 0:1],
                                  ALU.min, ALU.max).then_inc(S["clip_set"], 1)

            def b_att(b, j):
                at_least(dve, S["pv_mm"], 2 * b + j + 1)
                at_least(dve, S["att_T"], b)
                src = banks[PV_BANK[j]][:, 0:HEADS * VW].rearrange("p (h v) -> p h v", v=VW)
                r = rden[:, j].rearrange("p r a -> p (r a)")
                dve.reciprocal(r, src[:, :, DH]).then_inc(S["rden_set"], 1)
                at_least(dve, S["rden_set"], 2 * b + j + 1)
                dve.tensor_tensor(att[:, j, :].rearrange("p (h d) -> p h d", d=DH), src[:, :, 0:DH],
                                  r[:, :, None].broadcast_to([P, HEADS, DH]), ALU.mult).then_inc(S["att_set"], 1)

            def b_delta(b):
                at_least(dve, S["o_mm"], b + 1)
                at_least(dve, S["dgam_set"], 2 * b)
                dve.tensor_tensor(delta[:], banks[5][:, :].rearrange("p (j d) -> p j d", d=D),
                                  bo0[:, None, :].broadcast_to([P, ST, D]), ALU.add).then_inc(S["delta_set"], 1)
                at_least(dve, S["delta_set"], b + 1)
                for j in range(ST):
                    dve.bn_stats(stat6_d[:, j, :], delta[:, j, :]).then_inc(S["stat_d"], 1)
                hold(dve, S["stat_d"], 2 * b + 2)
                hold(dve, S["ve_d_set"], b)
                for j in range(ST):
                    dve.bn_aggr(mv_d[:, j, :], stat6_d[:, j, :]).then_inc(S["mv_d_set"], 1)

            def b_gamma(b):
                at_least(dve, S["mv_d_set"], 2 * b + 2)
                for j in range(ST):
                    dve.scalar_tensor_tensor(dgam[:, j, :], delta[:, j, :], mv_d[:, j, 0:1], gamma[:], ALU.subtract,
                                             ALU.mult).then_inc(S["dgam_set"], 1)

            def b_x1(b):
                at_least(dve, S["rstd_d_set"], b + 1)
                at_least(dve, S["xbeta_set"], 2 * b + 2)
                at_least(dve, S["dgam_set"], 2 * b + 2)
                for j in range(ST):
                    dve.scalar_tensor_tensor(x_all[:, ST * b + j, :], dgam[:, j, :], rstd_d[:, j:j + 1], xbeta[:, j, :],
                                             ALU.mult, ALU.add).then_inc(S["x1_set"], 1)
                hold(dve, S["x1_set"], 2 * b + 2)
                for j in range(ST):
                    dve.bn_stats(stat6_h[:, j, :], x_all[:, ST * b + j, :]).then_inc(S["stat_h"], 1)
                hold(dve, S["stat_h"], 2 * b + 2)
                hold(dve, S["rstd_h_set"], b)
                for j in range(ST):
                    dve.bn_aggr(mv_h[:, j, :], stat6_h[:, j, :]).then_inc(S["mv_h_set"], 1)

            def b_h(b):
                at_least(dve, S["rstd_h_set"], b + 1)
                at_least(dve, S["h_T"], b)
                at_least(dve, S["h_out"], 16 * b)
                for j in range(ST):
                    dve.tensor_scalar(h_rows[:, j, :], x_all[:, ST * b + j, :], mv_h[:, j, 0:1], rstd_h[:, j:j + 1],
                                      ALU.subtract, ALU.mult).then_inc(S["h_set"], 1)

            def c_top(b):
                at_least(dve, S["l_mm"], b + 1)
                at_least(dve, S["etop_set"], 2 * b)
                dve.tensor_tensor(logit[:], banks[6][:, 0:ST * OLD].rearrange("p (j o) -> p j o", o=OLD),
                                  unkept[:, None, :].broadcast_to([P, ST, OLD]), ALU.add).then_inc(S["logit_set"], 1)
                hold(dve, S["logit_set"], b + 1)
                for j in range(ST):
                    dve.max(top[:, j, :], logit[:, j, :]).then_inc(S["top_set"], 1)
                at_least(dve, S["top_set"], 2 * b + 2)
                at_least(dve, S["etop_set"], 2 * b)
                dve.tensor_scalar(ntop[:], top[:, :, 0], -1.0, None, ALU.mult).then_inc(S["ntop_set"], 1)

            def c_sel(b):
                hold(dve, S["top_set"], 2 * b + 2)
                hold(dve, S["sel_set"], b)
                for j in range(ST):
                    dve.match_replace(left[:, j, :], top[:, j, :], logit[:, j, :], TAKEN).then_inc(S["left_set"], 1)
                at_least(dve, S["count_mm"], b)
                if not isinstance(b, int) or b > 0:
                    dve.tensor_tensor(selboth[:], sel[:, 0, :], sel[:, 1, :], ALU.add).then_inc(S["selsum_set"], 1)
                    at_least(dve, S["selsum_set"], 2 * b - 1)
                    dve.tensor_tensor(selsum[:], selsum[:], selboth[:], ALU.add).then_inc(S["selsum_set"], 1)
                at_least(dve, S["left_set"], 2 * b + 2)
                dve.tensor_tensor(sel[:], left[:], logit[:], ALU.not_equal).then_inc(S["sel_set"], 1)

            def c_weight(b):
                at_least(dve, S["expl_set"], 2 * b + 2)
                at_least(dve, S["sel_set"], b + 1)
                at_least(dve, S["wsel_T"], b)
                for j in range(ST):
                    dve.tensor_tensor(wsel[:, j, :], expl[:, j, :], sel[:, j, :], ALU.mult).then_inc(S["wsel_set"], 1)
                at_least(dve, S["etop_set"], 2 * b + 2)
                at_least(dve, S["w_set"], 2 * b)
                dve.reciprocal(rdn[:], den[:]).then_inc(S["den_set"], 1)

            def c_count(b):
                at_least(dve, S["wsel_T"], b + 1)
                at_least(dve, S["pos_mm"], b)
                dve.tensor_scalar(countT[:].rearrange("p j s -> p (j s)"), banks[6][:, 0:ST * P], float(P), None,
                                  ALU.min).then_inc(S["countT_set"], 1)

            def c_pos(b):
                at_least(dve, S["pos_mm"], b + 1)
                dve.tensor_scalar(off[:].rearrange("p j e -> p (j e)"), banks[7][:, 96:192], 0.0, float(P), ALU.is_le,
                                  ALU.mult).then_inc(S["off_set"], 1)
                at_least(dve, S["off_set"], b + 1)
                dve.scalar_tensor_tensor(pos[:].rearrange("p j e -> p (j e)"), banks[7][:, 0:96], float(P),
                                         off[:].rearrange("p j e -> p (j e)"), ALU.min, ALU.add).then_inc(S["pos_set"], 1)

            def c_hit(b, j):
                at_least(dve, S["pos_set"], b + 1)
                at_least(dve, S["slot_mm" if j else "signed_set"], b)
                choice = pos[:, j, :].rearrange("t (q e) -> t q e", e=EPG)
                dve.tensor_tensor(hit[:, j], place[:], choice[:, :, None, :].broadcast_to([P, QG, CAP, EPG]),
                                  ALU.is_equal).then_inc(S["hit_set"], 1)

            def c_signed(b):
                at_least(dve, S["hit_set"], 2 * b + 2)
                dve.tensor_tensor(hit[:, 1], hit[:, 0], hit[:, 1], ALU.subtract).then_inc(S["signed_set"], 1)

            def d_slots(b):
                at_least(dve, S["slot_mm"], b + 1)
                src = banks[4][0:CAP, 0:2 * NEW].rearrange("p (n v) -> p n v", v=2)
                at_least(dve, S["slot_acc"], b)
                at_least(dve, S["slotb_acc"], b)
                dve.tensor_tensor(slots[:], src, slots[:], ALU.add).then_inc(S["slot_acc"], 1)
                col = cst[0:CAP, C_B256 + b:C_B256 + b + 1] if isinstance(b, int) else cst[0:CAP, bass.ds(C_B256 + b, 1)]
                dve.scalar_tensor_tensor(slot_b[:], src[:, :, 1], col, slot_b[:], ALU.mult, ALU.add)\
                    .then_inc(S["slotb_acc"], 1)

            def body(b, stages=range(5)):
                if 2 in stages:
                    b_x1(b - 2)
                if 3 in stages:
                    c_pos(b - 3)
                if 2 in stages:
                    b_h(b - 2)
                if 1 in stages:
                    b_clip(b - 1, 0)
                    b_clip(b - 1, 1)
                if 3 in stages:
                    c_hit(b - 3, 0)
                if 1 in stages:
                    b_clip(b - 1, 2)
                    b_clip(b - 1, 3)
                if 2 in stages:
                    c_top(b - 2)
                if 0 in stages:
                    a_stat(b)
                if 4 in stages:
                    d_slots(b - 4)
                if 3 in stages:
                    c_hit(b - 3, 1)
                if 1 in stages:
                    b_att(b - 1, 0)
                if 2 in stages:
                    c_sel(b - 2)
                if 1 in stages:
                    b_att(b - 1, 1)
                if 0 in stages:
                    a_norm(b)
                if 2 in stages:
                    c_weight(b - 2)
                if 3 in stages:
                    c_signed(b - 3)
                if 2 in stages:
                    c_count(b - 2)
                if 1 in stages:
                    b_delta(b - 1)
                    b_gamma(b - 1)

            for b in range(0, 5):
                if b == 3:
                    dve.wait_ge(S["place_set"], 8)
                body(b, range(b + 1))
            with dve.Fori(5, BATCH) as b:
                body(b)
            for b in range(BATCH, BATCH + 4):
                body(b, range(b - BATCH + 1, 5))
            sign = slots[:, :, 1]
            dve.memset(slot_i[:, NEW:NEW + EPG], 0)
            dve.wait_ge(S["slotb_acc"], BATCH)
            dve.wait_ge(S["slot_acc"], BATCH)
            dve.tensor_scalar(empty[:], sign, 0.0, None, ALU.is_equal).then_inc(S["slot_acc"], 1)
            dve.tensor_scalar(second[:], sign, 0.0, float(P), ALU.is_lt, ALU.mult).then_inc(S["slot_acc"], 1)
            dve.tensor_tensor(slot_f[:], slots[:, :, 0], slot_b[:], ALU.add).then_inc(S["slot_acc"], 1)
            dve.wait_ge(S["slot_acc"], BATCH + 3)
            dve.tensor_tensor(slot_f[:], slot_f[:], sign, ALU.mult).then_inc(S["slot_acc"], 1)
            dve.scalar_tensor_tensor(second[:], empty[:], cst[0:CAP, C_PAD:C_PAD + 1], second[:], ALU.mult, ALU.add)\
                .then_inc(S["slot_acc"], 1)
            dve.wait_ge(S["slot_acc"], BATCH + 5)
            dve.tensor_tensor(slot_i[:, 0:NEW], slot_f[:], second[:], ALU.add).then_inc(S["route_done"], 1)

            def group(q):
                return slot_i[:, EPG * q:EPG * q + EPG] if isinstance(q, int) else slot_i[:, bass.ds(EPG * q, EPG)]

            dve.wait_ge(S["route_done"], 1)
            for h in range(TURN):
                dve.tensor_copy(take[h][:], group(h)).then_inc(S["take_set"], 1)
            for m in range(KC):
                dve.wait_ge(S["kT_mm"], KC + m + 1)
                dve.tensor_copy(kT[1][:, m, :], banks[m][:, :]).then_inc(S["kT_set"], 1)
            dve.wait_ge(S["v_mm"], 5)
            for a in range(2):
                h = slice(CTX * a, CTX * a + CTX)
                src = banks[6][h, :].rearrange("p (b g d) -> p b g d", b=BATCH, d=DH)
                dst = v_blk[1][h, :, :, a, 0:DH].rearrange("p b (g r) d -> p b g r d", r=2)
                for r in range(2):
                    dve.tensor_copy(dst[:, :, :, r, :], src).then_inc(S["v_set"], 1)

            def x0_T(i, h):
                q = TURN * i + h
                at_least(dve, S["xb_T"], q + 1)
                at_least(dve, S["gu0_mm"], 2 * q)
                dve.tensor_copy(xbT[:, 1, :], banks[1][:, 0:EPG * CAP]).then_inc(S["xbT_set"], 1)
                wgt = xb[h][:, :, D + EPG * q:D + EPG * q + EPG] if isinstance(q, int) else \
                    xb[h][:, :, bass.ds(D + EPG * q, EPG)]
                own = cst[0:CAP, C_SLOTE:C_SLOTE + EPG * EPG].rearrange("p (e f) -> p e f", f=EPG)
                at_least(dve, S["wslot_set"], q)
                dve.tensor_tensor(wpick[:], wgt, own, ALU.mult).then_inc(S["wpick_set"], 1)
                at_least(dve, S["wpick_set"], q + 1)
                at_least(dve, S["ya_set"], 2 * (q - TURN + 1))
                at_least(dve, S["yv_set"], 2 * (q - TURN + 1))
                dve.tensor_reduce(wslot[h][:], wpick[:], AX.X, ALU.add).then_inc(S["wslot_set"], 1)
                if not isinstance(q, int) or q + TURN < QG:
                    dve.tensor_copy(take[h][:], group(q + TURN)).then_inc(S["take_set"], 1)

            def act0_mul(i, h):
                q = TURN * i + h
                for u in range(2):
                    at_least(dve, S["silu0_set"], 2 * q + u + 1)
                    at_least(dve, S["y_mm"], 2 * (q - 1) + u + 1)
                    src = banks[2 + u][0:INTER0, 0:2 * 2 * CAP].rearrange("i (e s c) -> i e s c", e=2, s=2)
                    dve.tensor_tensor(act0[:, 2 * u:2 * u + 2, :], silu0[:, 2 * u:2 * u + 2, :], src[:, :, 1, :],
                                      ALU.mult).then_inc(S["act0_set"], 1)

            def y0(i, h):
                q = TURN * i + h
                at_least(dve, S["y_mm"], 2 * q + 1)
                at_least(dve, S["wslot_set"], q + 1)
                for c in range(2):
                    at_least(dve, S[f"scatter{c}"], 16 * (EPG // 2) * (q - TURN + 1))
                dve.tensor_copy(give[h][:], group(q)).then_inc(S["give_set"], 1)
                for e in range(2):
                    dve.tensor_scalar(y[h][:, e, :], banks[4][0:CAP, D * e:D * e + D], wslot[h][:, e:e + 1],
                                      None, ALU.mult).then_inc(S["yv_set"], 1)

            def experts(i, h, i1, h1, first=False, last=False):
                if not first:
                    y0(i, h)
                if not last:
                    x0_T(i1, h1)
                    act0_mul(i1, h1)

            experts(-1, TURN - 1, 0, 0, first=True)
            for h in range(TURN):
                experts(0, h, *((0, h + 1) if h + 1 < TURN else (1, 0)))
            with dve.Fori(1, QG // TURN - 1) as i:
                for h in range(TURN):
                    experts(i, h, *((i, h + 1) if h + 1 < TURN else (i + 1, 0)))
            for h in range(TURN):
                experts(QG // TURN - 1, h, QG // TURN - 1, h + 1, last=h == TURN - 1)

            def a1_stat(b):
                hold(dve, S["x2_set"], b + 1)
                for j in range(ST):
                    dve.bn_stats(stat6[:, j, :], x_all[:, ST * b + j, :]).then_inc(S["stat_a"], 1)
                hold(dve, S["stat_a"], 2 * (BATCH + b) + 2)
                hold(dve, S["rstd_a_set"], BATCH + b)
                for j in range(ST):
                    dve.bn_aggr(mv_a[:, j, :], stat6[:, j, :]).then_inc(S["mv_a_set"], 1)

            def b1_max(b, u):
                at_least(dve, S["s1_mm"], 4 * b + u + 1)
                src = banks[1 + u % 2][:, :].rearrange("p (h c) -> p h c", c=CTX)
                dve.tensor_reduce(great[:, u, :], src, AX.X, ALU.max).then_inc(S["great_set"], 1)
                at_least(dve, S["great_set"], 4 * b + u + 1)
                at_least(dve, S["soft_T"], 4 * (b - 1) + u + 1)
                dve.tensor_tensor(soft[:, u, :].rearrange("p (h c) -> p h c", c=CTX), src,
                                  great[:, u, :, None].broadcast_to([P, 8, CTX]), ALU.subtract).then_inc(S["sub_set"], 1)

            def b1_att(b, j):
                at_least(dve, S["pv_mm"], ST * (BATCH + b) + j + 1)
                at_least(dve, S["att_T"], BATCH + b)
                src = banks[4][:, 0:HEADS * VW].rearrange("p (h v) -> p h v", v=VW)
                r = rden[:, j].rearrange("p r a -> p (r a)")
                dve.reciprocal(r, src[:, :, DH]).then_inc(S["rden_set"], 1)
                at_least(dve, S["rden_set"], ST * (BATCH + b) + j + 1)
                dve.tensor_tensor(att[:, j, :].rearrange("p (h d) -> p h d", d=DH), src[:, :, 0:DH],
                                  r[:, :, None].broadcast_to([P, HEADS, DH]), ALU.mult).then_inc(S["att_set"], 1)

            def b1_x3(b):
                at_least(dve, S["o_mm"], BATCH + b + 1)
                x = x_all[:, bass.ds(ST * b, ST), :]
                dve.tensor_tensor(x, x, banks[0][:, :].rearrange("p (j d) -> p j d", d=D), ALU.add)\
                    .then_inc(S["x3_set"], 1)
                hold(dve, S["x3_set"], b + 1)
                for j in range(ST):
                    dve.bn_stats(stat6_h[:, j, :], x_all[:, ST * b + j, :]).then_inc(S["stat_h"], 1)
                hold(dve, S["stat_h"], 2 * (BATCH + b) + 2)
                for j in range(ST):
                    dve.bn_aggr(mv_h[:, j, :], stat6_h[:, j, :]).then_inc(S["mv_h_set"], 1)

            def b1_h(b):
                at_least(dve, S["rstd_h_set"], BATCH + b + 1)
                at_least(dve, S["h1_T"], b)
                for j in range(ST):
                    dve.tensor_scalar(h_rows[:, j, :], x_all[:, ST * b + j, :], mv_h[:, j, 0:1], rstd_h[:, j:j + 1],
                                      ALU.subtract, ALU.mult).then_inc(S["h_set"], 1)

            def c1_top(b):
                at_least(dve, S["l1_mm"], b + 1)
                dve.tensor_copy(logit1[:].rearrange("p j e -> p (j e)"), banks[3][:, 0:ST * E1])\
                    .then_inc(S["logit1_set"], 1)
                hold(dve, S["logit1_set"], b + 1)
                for j in range(ST):
                    dve.max(top1[:, j, :], logit1[:, j, :]).then_inc(S["top1_set"], 1)
                hold(dve, S["top1_set"], 2 * b + 2)
                for j in range(ST):
                    dve.max_index(index1[:, j, :], top1[:, j, :], logit1[:, j, :]).then_inc(S["index1_set"], 1)
                dve.tensor_tensor(gap[:], top1[:, :, 1], top1[:, :, 0], ALU.subtract).then_inc(S["gap_set"], 1)
                at_least(dve, S["index1_set"], 2 * b + 2)
                for n in range(2):
                    dve.tensor_tensor(chosen[:, n], index1[:, :, n:n + 1].broadcast_to([P, ST, E1]),
                                      cst[:, None, C_E8:C_E8 + E1].broadcast_to([P, ST, E1]), ALU.is_equal)\
                        .then_inc(S["chosen_set"], 1)

            def c1_share(b):
                at_least(dve, S["egap_set"], b + 1)
                dve.tensor_scalar(wsum[:], egap[:], 1.0, None, ALU.add).then_inc(S["wsum_set"], 1)
                at_least(dve, S["wsum_set"], b + 1)
                dve.reciprocal(wpair[:, 0, :], wsum[:]).then_inc(S["w0_set"], 1)
                at_least(dve, S["w0_set"], b + 1)
                dve.tensor_tensor(wpair[:, 1, :], wpair[:, 0, :], egap[:], ALU.mult).then_inc(S["w1_set"], 1)
                at_least(dve, S["w1_set"], b + 1)
                at_least(dve, S["chosen_set"], 2 * b + 2)
                for n in range(2):
                    dve.tensor_tensor(chosen_w[:, n], chosen[:, n], wpair[:, n, :, None].broadcast_to([P, ST, E1]),
                                      ALU.mult).then_inc(S["chosen_w_set"], 1)
                at_least(dve, S["chosen_w_set"], 2 * b + 2)
                at_least(dve, S["acc_set"], E1 * b)
                dve.tensor_tensor(share_c[:], chosen_w[:, 0], chosen_w[:, 1], ALU.add).then_inc(S["share_set"], 1)

            def a1_norm(b):
                at_least(dve, S["rstd_a_set"], BATCH + b + 1)
                at_least(dve, S["hs_T"], BATCH + b)
                for j in range(ST):
                    ins = dve.tensor_scalar(hs[:, j, :], x_all[:, ST * b + j, :], mv_a[:, j, 0:1], rstd_a[:, j:j + 1],
                                            ALU.subtract, ALU.mult)
                ins.then_inc(S["hs_set"], 1)

            def d1_hT(b):
                at_least(dve, S["hTr_set"], b + 1)
                at_least(dve, S["gu1_mm"], E1 * b)
                dve.tensor_copy(hT1[:].bitcast(F32R), hTr[:])\
                    .then_inc(S["hT1h_set"], 1)
                at_least(dve, S["hT1h_set"], b + 1)
                dve.tensor_tensor(hT1_low[:].bitcast(F32R), hTr[:], hT1[:], ALU.subtract).then_inc(S["hT1_set"], 1)

            def d1_mul(b, e):
                at_least(dve, S["silu1_set"], E1 * b + e + 1)
                at_least(dve, S["act1l_set"], E1 * b + e - 1)
                dve.tensor_tensor(act1[e % 2][:], silu1[e % 2][:], banks[5 + e % 2][:, SEQ:2 * SEQ], ALU.mult)\
                    .then_inc(S["act1_set"], 1)
                at_least(dve, S["act1_set"], E1 * b + e + 1)
                at_least(dve, S["down1_mm"], E1 * b + e - 1)
                dve.tensor_copy(act1_high[e % 2][:].bitcast(F32R), act1[e % 2][:])\
                    .then_inc(S["act1h_set"], 1)

            def d1_acc(b, e):
                at_least(dve, S["down1_mm"], E1 * b + e + 1)
                at_least(dve, S["acc_set"], E1 * b + e)
                if e == 0:
                    at_least(dve, S["share_set"], b + 1)
                    at_least(dve, S["o_out"], 16 * b)
                for j in range(ST):
                    before = x_all[:, ST * b + j, :] if e == 0 else o_rows[:, j, :]
                    ins = dve.scalar_tensor_tensor(o_rows[:, j, :], banks[7][:, D * j:D * j + D], share_c[:, j, e:e + 1],
                                                   before, ALU.mult, ALU.add)
                    if j == 0 and isinstance(b, int) and (b, e) == (BATCH - 1, E1 - 1):
                        ins.then_inc(S["acc_set"], 1)
                ins.then_inc(S["acc_set"], 1)

            def weights_cut(parts):
                for w, _, low in parts:
                    high = dve.tensor_copy(low.bitcast(F32R), w)
                high.then_inc(S["whigh_set"], 1)
                at_least(dve, S["whigh_set"], 2 if parts is late_parts else 1)
                for w, _, low in parts:
                    rest = dve.tensor_tensor(low.bitcast(F32R), w, low, ALU.subtract)
                rest.then_inc(S["wlow_set"], 1)
                at_least(dve, S["wlow_set"], 2 if parts is late_parts else 1)
                for w, w_high, _ in parts:
                    cut = dve.tensor_copy(w_high.bitcast(F32R), w)
                cut.then_inc(S["wparts_set"], 1)

            def layer1(b, stages=range(5)):
                if 2 in stages:
                    b1_max(b - 2, 0)
                if 3 in stages:
                    c1_top(b - 3)
                if 2 in stages:
                    b1_max(b - 2, 1)
                if 4 in stages:
                    d1_acc(b - 4, 7)
                if 2 in stages:
                    b1_max(b - 2, 2)
                    b1_max(b - 2, 3)
                if 3 in stages:
                    c1_share(b - 3)
                if 0 in stages:
                    a1_stat(b)
                if 3 in stages:
                    d1_mul(b - 3, 0)
                    d1_mul(b - 3, 1)
                if 2 in stages:
                    b1_att(b - 2, 0)
                if 3 in stages:
                    d1_acc(b - 3, 0)
                if 0 in stages:
                    a1_norm(b)
                if 3 in stages:
                    d1_mul(b - 3, 2)
                    d1_acc(b - 3, 1)
                    d1_mul(b - 3, 3)
                if 2 in stages:
                    b1_att(b - 2, 1)
                if 3 in stages:
                    d1_acc(b - 3, 2)
                    d1_mul(b - 3, 4)
                    d1_acc(b - 3, 3)
                    d1_mul(b - 3, 5)
                    d1_acc(b - 3, 4)
                if 2 in stages:
                    b1_x3(b - 2)
                if 3 in stages:
                    d1_mul(b - 3, 6)
                    d1_acc(b - 3, 5)
                if 2 in stages:
                    b1_h(b - 2)
                if 3 in stages:
                    d1_mul(b - 3, 7)
                    d1_acc(b - 3, 6)
                if 2 in stages:
                    d1_hT(b - 2)

            dve.wait_ge(S["e1_w_in"], 2 * 16 * E1)
            dve.wait_ge(S["y_mm"], 2 * QG)
            weights_cut(early_parts)
            for b in range(0, 5):
                layer1(b, range(b + 1))
                if b == 0:
                    dve.wait_ge(S["scatter0"], 16 * NEW // 2)
                    dve.wait_ge(S["scatter1"], 16 * NEW // 2)
                    weights_cut(late_parts)
            with dve.Fori(5, BATCH) as b:
                layer1(b)
            for b in range(BATCH, BATCH + 4):
                layer1(b, range(b - BATCH + 1, 5))


def laid_out(i):
    def chunks(w):
        return np.ascontiguousarray(w.reshape(-1, P, w.shape[-1]).transpose(1, 0, 2))

    def dup(m):
        return np.ascontiguousarray(np.concatenate([m.T, m.T], 0))
    left, rows = position_bias()
    return {
        "x": i["x"].reshape(TOKENS, D),
        "ctxT": chunks(i["ctx_2048"].reshape(BATCH * CTX, D).T),
        "cst": constants(), "bias_q": left, "bias_k": rows,
        "wk0": chunks(i["L0_xattn_Wk"].T), "wv0": chunks(i["L0_xattn_Wv"].T),
        "wq0": chunks(i["L0_xattn_Wq"].T), "wo0": chunks(i["L0_xattn_Wo"].T),
        "gate0": chunks(i["L0_ffn_gate_weight"].T),
        "wq1": chunks(i["L1_xattn_Wq"]), "wk1": chunks(i["L1_xattn_Wk"]),
        "wv1": chunks(i["L1_xattn_Wv"]), "wo1": chunks(i["L1_xattn_Wo"]),
        "bq0": i["L0_xattn_bq"].reshape(KC, P).T, "bk0": i["L0_xattn_bk"].reshape(KC, P).T,
        "bv0": i["L0_xattn_bv"], "bo0": i["L0_xattn_bo"],
        "gamma": i["L0_xattn_ln_gamma"], "beta": i["L0_xattn_ln_beta"],
        "rs": i["L0_xattn_residual_scale"].reshape(1),
        "o2n": i["L0_ffn_old_to_new"],
        "mask0": dup(i["mask_BxS2_ik0"]), "mask1": i["mask_BxS2_bf1"].view(np.uint8).reshape(1, BATCH * CTX),
        "gu0": np.ascontiguousarray(i["L0_ffn_gate_up_proj"].reshape(QG, EPG, 2 * INTER0, KC, P).transpose(0, 4, 3, 1, 2)),
        "down0": np.ascontiguousarray(i["L0_ffn_down_proj"].reshape(QG, EPG, D, INTER0).transpose(0, 3, 1, 2)),
        "gate1": chunks(i["L1_ffn_router_gate"].T),
        "gu1": np.ascontiguousarray(i["L1_ffn_expert_gate_up"].reshape(E1, KC, P, INTER1, 2).transpose(2, 0, 1, 4, 3)),
        "down1": np.ascontiguousarray(i["L1_ffn_expert_down"].transpose(1, 0, 2)),
    }


def kernel(**inputs):
    from concourse import bacc
    from concourse.bass_utils import run_bass_kernel_spmd

    nc = bacc.Bacc("TRN2", target_bir_lowering=False, num_devices=1)
    arrays = {f"in_{n}": np.ascontiguousarray(a) for n, a in laid_out(inputs).items()}
    t = {n[3:]: nc.dram_tensor(n, a.shape, mybir.dt.from_np(a.dtype), kind="ExternalInput").ap()
         for n, a in arrays.items()}
    out = nc.dram_tensor("out", (TOKENS, D), F32, kind="ExternalOutput").ap()
    build(nc, t, out)
    r = run_bass_kernel_spmd(nc, [arrays], core_ids=[0])
    return r.results[0]["out"].reshape(BATCH, SEQ, D)
```
